# Optimizing a Trainium2 kernel written in Bass

```python
import numpy as np
import jax
import jax.numpy as jnp

def _softmax(x, axis=-1):
    return jax.nn.softmax(x, axis=axis)

def _gelu(x):
    return jax.nn.gelu(x, approximate=True)

def _silu(x):
    return jax.nn.silu(x)

def _sigmoid(x):
    return jax.nn.sigmoid(x)

def _layernorm(x, axis=-1, eps=1e-05):
    m = jnp.mean(x, axis=axis, keepdims=True)
    v = jnp.var(x, axis=axis, keepdims=True)
    return (x - m) / jnp.sqrt(v + eps)

def _scatter_add(tgt, idx, src, axis=0):
    return tgt.at[idx].add(src)

def _segment_sum(src, seg, n):
    return jax.ops.segment_sum(src, seg, n)
kernel_name = 'mk_macaron_d1_jaxref_r4_bfa9d4'

def setup_inputs(seed: int=0):
    np.random.seed(seed)
    _w = jnp.asarray

    def _L0_attn_setup():
        import math
        import jax, jax.numpy as jnp
        import numpy as np
        A = 256
        H = 16
        HS = A // H
        M = 64
        ITERS = 6

        def split_heads(t):
            B, L, _ = t.shape
            return t.reshape(B, L, H, HS).transpose(0, 2, 1, 3)

        def moore_penrose_pinv(x, num_iter):
            abs_x = jnp.abs(x)
            col = abs_x.sum(axis=-1).max(axis=-1)
            row = abs_x.sum(axis=-2).max(axis=-1)
            z = jnp.swapaxes(x, -1, -2) / (col * row)[..., None, None]
            I = jnp.eye(x.shape[-1], dtype=x.dtype)
            for _ in range(num_iter):
                xz = x @ z
                z = 0.25 * z @ (13.0 * I - xz @ (15.0 * I - xz @ (7.0 * I - xz)))
            return z
        key = jax.random.key(seed)
        ks = jax.random.split(key, 6)
        x = jax.random.normal(ks[0], (4, 1024, A), dtype=jnp.float32)
        s = 1.0 / math.sqrt(A)
        Wk = jax.random.normal(ks[1], (A, A), dtype=jnp.float32) * s
        Wq = jax.random.normal(ks[2], (A, A), dtype=jnp.float32) * s
        Wv = jax.random.normal(ks[3], (A, A), dtype=jnp.float32) * s
        Wo = jax.random.normal(ks[4], (A, A), dtype=jnp.float32) * s
        bo = jnp.zeros((A,), dtype=jnp.float32)
        return {'x': x, 'Wk': Wk, 'Wq': Wq, 'Wv': Wv, 'Wo': Wo, 'bo': bo}
    _L0_attn_in = _L0_attn_setup()

    def _L0_ffn_setup():
        import jax, jax.numpy as jnp
        import numpy as np
        B, S, H, F, E = (1, 512, 256, 512, 8)

        def _swiglu(x, wg, wu, wd):
            return jax.nn.silu(x @ wg.T) * (x @ wu.T) @ wd.T
        key = jax.random.key(seed)
        ks = jax.random.split(key, 8)
        sc = 1.0 / np.sqrt(H)
        scf = 1.0 / np.sqrt(F)
        return {'hidden_states': jax.random.normal(ks[0], (B, S, H), jnp.float32), 'gate_w': jax.random.normal(ks[1], (E, H), jnp.float32) * sc, 'shared_gate': jax.random.normal(ks[2], (F, H), jnp.float32) * sc, 'shared_up': jax.random.normal(ks[3], (F, H), jnp.float32) * sc, 'shared_down': jax.random.normal(ks[4], (H, F), jnp.float32) * scf, 'r_gate': jax.random.normal(ks[5], (E, F, H), jnp.float32) * sc, 'r_up': jax.random.normal(ks[6], (E, F, H), jnp.float32) * sc, 'r_down': jax.random.normal(ks[7], (E, H, F), jnp.float32) * scf}
    _L0_ffn_in = _L0_ffn_setup()
    _d = {'L0_attn_x': _L0_attn_in['x'], 'L0_attn_Wk': _L0_attn_in['Wk'], 'L0_attn_Wq': _L0_attn_in['Wq'], 'L0_attn_Wv': _L0_attn_in['Wv'], 'L0_attn_Wo': _L0_attn_in['Wo'], 'L0_attn_bo': _L0_attn_in['bo'], 'L0_ffn_gate_w': _L0_ffn_in['gate_w'], 'L0_ffn_shared_gate': _L0_ffn_in['shared_gate'], 'L0_ffn_shared_up': _L0_ffn_in['shared_up'], 'L0_ffn_shared_down': _L0_ffn_in['shared_down'], 'L0_ffn_r_gate': _L0_ffn_in['r_gate'], 'L0_ffn_r_up': _L0_ffn_in['r_up'], 'L0_ffn_r_down': _L0_ffn_in['r_down']}
    _x0 = _d['L0_attn_x']
    _d['L0_attn_x'] = jax.random.normal(jax.random.fold_in(jax.random.key(seed), 1), (8, 512, 256), dtype=_x0.dtype)
    del _x0
    return _d

def reference(L0_attn_x, L0_attn_Wk, L0_attn_Wq, L0_attn_Wv, L0_attn_Wo, L0_attn_bo, L0_ffn_gate_w, L0_ffn_shared_gate, L0_ffn_shared_up, L0_ffn_shared_down, L0_ffn_r_gate, L0_ffn_r_up, L0_ffn_r_down):

    def _L0_attn_ref(x, Wk, Wq, Wv, Wo, bo):
        import math
        import jax, jax.numpy as jnp
        import numpy as np
        A = 256
        H = 16
        HS = A // H
        M = 64
        ITERS = 6

        def split_heads(t):
            B, L, _ = t.shape
            return t.reshape(B, L, H, HS).transpose(0, 2, 1, 3)

        def moore_penrose_pinv(x, num_iter):
            abs_x = jnp.abs(x)
            col = abs_x.sum(axis=-1).max(axis=-1)
            row = abs_x.sum(axis=-2).max(axis=-1)
            z = jnp.swapaxes(x, -1, -2) / (col * row)[..., None, None]
            I = jnp.eye(x.shape[-1], dtype=x.dtype)
            for _ in range(num_iter):
                xz = x @ z
                z = 0.25 * z @ (13.0 * I - xz @ (15.0 * I - xz @ (7.0 * I - xz)))
            return z
        B, L, _ = x.shape
        k = split_heads(x @ Wk)
        q = split_heads(x @ Wq)
        v = split_heads(x @ Wv)
        q = q / math.sqrt(HS)
        denom = L // M
        q_l = q.reshape(B, H, M, denom, HS).sum(axis=-2) / denom
        k_l = k.reshape(B, H, M, denom, HS).sum(axis=-2) / denom
        s1 = jax.nn.softmax(jnp.einsum('bhld,bhmd->bhlm', q, k_l), axis=-1)
        s2 = jax.nn.softmax(jnp.einsum('bhmd,bhnd->bhmn', q_l, k_l), axis=-1)
        s3 = jax.nn.softmax(jnp.einsum('bhmd,bhld->bhml', q_l, k), axis=-1)
        z_star = moore_penrose_pinv(s2, ITERS)
        out = s1 @ (z_star @ (s3 @ v))
        out = out.transpose(0, 2, 1, 3).reshape(B, L, A)
        return out @ Wo + bo

    def _L0_ffn_ref(hidden_states, gate_w, shared_gate, shared_up, shared_down, r_gate, r_up, r_down):
        import jax, jax.numpy as jnp
        import numpy as np
        B, S, H, F, E = (1, 512, 256, 512, 8)

        def _swiglu(x, wg, wu, wd):
            return jax.nn.silu(x @ wg.T) * (x @ wu.T) @ wd.T
        b, s, h = hidden_states.shape
        x = hidden_states.reshape(-1, h)
        shared_out = _swiglu(x, shared_gate, shared_up, shared_down)
        logits = x @ gate_w.T
        top_id = jnp.argmax(logits, axis=-1)
        score = jax.nn.sigmoid(jnp.max(logits, axis=-1))
        xs = x * score[:, None]

        def body(acc, ws):
            wg, wu, wd, e = ws
            xe = jnp.where((top_id == e)[:, None], xs, 0.0)
            return (acc + _swiglu(xe, wg, wu, wd), None)
        acc0 = jnp.zeros_like(x)
        routed_out, _ = jax.lax.scan(body, acc0, (r_gate, r_up, r_down, jnp.arange(E)))
        return (shared_out + routed_out).reshape(b, s, h)
    x = L0_attn_x
    x = x + 0.5 * _L0_ffn_ref(_layernorm(x, axis=-1), L0_ffn_gate_w, L0_ffn_shared_gate, L0_ffn_shared_up, L0_ffn_shared_down, L0_ffn_r_gate, L0_ffn_r_up, L0_ffn_r_down)
    x = x + _L0_attn_ref(_layernorm(x, axis=-1), L0_attn_Wk, L0_attn_Wq, L0_attn_Wv, L0_attn_Wo, L0_attn_bo)
    x = x + 0.5 * _L0_ffn_ref(_layernorm(x, axis=-1), L0_ffn_gate_w, L0_ffn_shared_gate, L0_ffn_shared_up, L0_ffn_shared_down, L0_ffn_r_gate, L0_ffn_r_up, L0_ffn_r_down)
    return x

_drawn_inputs = setup_inputs


def setup_inputs(seed=0):
    import zlib

    import numpy as np

    out = dict(_drawn_inputs(seed))
    spreads = {'L0_attn_bo': (0.0, 0.1)}
    factors = {}
    for name, (base, spread) in spreads.items():
        noise = np.random.default_rng([zlib.crc32(name.encode()), seed]).standard_normal(out[name].shape)
        drawn = base * np.exp(spread * noise) if base else spread * noise
        out[name] = jnp.asarray(drawn.astype(out[name].dtype))
    for name, factor in factors.items():
        out[name] = (out[name] * factor).astype(out[name].dtype)
    return out
```

```python
from contextlib import ExitStack

import numpy as np

import concourse.bass as bass
from concourse import mybir

ALU = mybir.AluOpType
ACT = mybir.ActivationFunctionType
AX_X = mybir.AxisListType.X
F32 = mybir.dt.float32
F32R = mybir.dt.float32r
I32 = mybir.dt.int32

P = 128
D = 256
KD = D // P
T = 4096
NT = T // P
GT = 4
NG = NT // GT
GW = GT * P
F = 512
KF = F // P
E = 8
SLOT_TILES = (T + E * (P - 1)) // P
UNR = 3
assert SLOT_TILES % UNR == 0
NOBODY = 2 * T
H = 16
HS = D // H
M = 64
LM = GW // M
PAIRS = H // 2
HC = P // HS
PC = PAIRS // KD
PINV_ITERS = 6
EPS = 1e-5

CONSTS = [("ident", P), ("before", P), ("ones", P), ("halves", P), ("eye2", M), ("head_rows", HC), ("pair_cols", 2 * HS),
          ("expert_rank", E), ("tile_edges", NT), ("tile_no", SLOT_TILES), ("token_no", NT), ("eps", 1)]
CONST_AT = {}
_at = 0
for _n, _w in CONSTS:
    CONST_AT[_n] = (_at, _w)
    _at += _w
CONST_W = _at


def constants():
    c = {n: np.zeros((P, w), np.float32) for n, w in CONSTS}
    c["ident"][:] = np.eye(P)
    c["before"][:] = np.triu(np.ones((P, P)), 1)
    c["ones"][:] = 1
    c["halves"][:] = np.kron(np.eye(2), np.ones((M, M)))
    c["eye2"][:] = np.tile(np.eye(M), (2, 1))
    c["head_rows"][:] = np.kron(np.eye(HC), np.ones((HS, 1)))
    c["pair_cols"][:] = np.kron(np.eye(2), np.ones((M, HS)))
    c["expert_rank"][:] = E - np.arange(E)
    c["tile_edges"][:] = P * np.arange(NT)
    c["tile_no"][:] = np.arange(SLOT_TILES)
    c["token_no"][:] = np.arange(P)[:, None] + P * np.arange(NT)
    c["eps"][:] = EPS
    return np.concatenate([c[n] for n, _ in CONSTS], 1)


def macaron_kernel(nc, x, wq, wk, wv, wo, bo, gate_w, sh_gate, sh_up, sh_down, r_gate, r_up, r_down, consts, out):
    with ExitStack() as top:
        emit(nc, top, x, wq, wk, wv, wo, bo, gate_w, sh_gate, sh_up, sh_down, r_gate, r_up, r_down, consts, out)


def emit(nc, top, x, wq, wk, wv, wo, bo, gate_w, sh_gate, sh_up, sh_down, r_gate, r_up, r_down, consts, out):
    def sb(name, shape, dt=F32, ctx=top):
        return ctx.enter_context(nc.sbuf_tensor(name, shape, dt))

    def sem(name):
        return top.enter_context(nc.semaphore(name))

    banks = [top.enter_context(nc.psum_tensor(f"bank{i}", [P, 512], F32)) for i in range(8)]

    X = sb("X", [P, NT * D])
    CB = sb("CB", [P, CONST_W])
    WG = sb("WG", [P, E * KD * F])
    SG = sb("SG", [P, KD * F])
    SU = sb("SU", [P, KD * F])
    SDN = sb("SDN", [P, KF * D])
    GWT = sb("GWT", [P, KD * E])
    WQ = sb("WQ", [P, KD * D])
    WK = sb("WK", [P, KD * D])
    WV = sb("WV", [P, KD * D])
    WO = sb("WO", [P, KD * D])
    BO = sb("BO", [P, D])
    STATS = sb("STATS", [P, GT * 6])
    AGG = sb("AGG", [P, GT * 2])
    MV = sb("MV", [P, NT * 2])
    RSTD = sb("RSTD", [P, NT])

    def const(name, rows=P):
        a, w = CONST_AT[name]
        return CB[0:rows, a:a + w]

    xs_dram = nc.dram_tensor("xs_dram", [T, D], F32, kind="Internal").ap()
    y_dram = nc.dram_tensor("y_dram", [T, D], F32, kind="Internal").ap()
    who_dram = [nc.dram_tensor(f"who_dram{i}", [SLOT_TILES * P, 1], I32, kind="Internal").ap() for i in range(2)]

    x_rows = x.rearrange("b (j p) d -> p (b j) d", p=P)
    out_rows = out.rearrange("b (j p) d -> p (b j) d", p=P)
    xs_rows = xs_dram.rearrange("(t p) d -> p t d", p=P)
    y_rows = y_dram.rearrange("(t p) d -> p t d", p=P)
    mvv = MV[:].rearrange("p (t c) -> p t c", c=2)
    X3 = X[:].rearrange("p (t d) -> p t d", d=D)

    s_x = [sem(f"x_loaded{i}") for i in range(4)]
    s_const = sem("consts_loaded")
    s_gate = sem("gate_loaded")
    s_shared = sem("shared_loaded")
    s_attn_w = sem("attention_weights_loaded")
    s_wg = sem("routed_gate_loaded")
    s_stored = sem("stored")
    s_pool_past = sem("pool_past_a_wait")
    s_dve_past = sem("dve_past_a_wait")

    TILES3 = SLOT_TILES // UNR
    FFN_PER = dict(stat=NT, agg=NT, mv=NG, sd=1, rstd=1, xn=NT, xt_ready=NG, xt_sb=KD * NG, xt_copied=KD * NG, lg_ready=NG, mx=1, onehot_step=3, oh=1,
                   score=1, rs_step=1, rs=1, xs=NT, xs_out=16 * NG, cnt_ready=2, rt=23, slots=2, expert_of=1, nobody=1, who_init=16,
                   who=16 * NT, who_sb=16, gu=KF * NG, silu=KF * NG, h=KF * NG, y_ready=NG, x_new=2 * NG, gath0=16 * TILES3, gath1=16 * TILES3,
                   gath2=16 * TILES3, xg_t=SLOT_TILES, xgt=SLOT_TILES, rgu=SLOT_TILES, rsilu=SLOT_TILES, rh=SLOT_TILES, ht_ready=SLOT_TILES,
                   ht_sb=SLOT_TILES, ry_ready=SLOT_TILES, ry=SLOT_TILES, ry_out0=16 * TILES3, ry_out1=16 * TILES3, ry_out2=16 * TILES3, wu=16, wd=16,
                   xs_raw=3 * NG, ry_free=SLOT_TILES, sidx=2 * NG, gidx=SLOT_TILES, yidx=SLOT_TILES)
    s = {k: sem(f"ffn_{k}") for k in FFN_PER}
    GIVEN = {"xt_ready", "xt_sb", "xt_copied", "lg_ready", "xs_out", "h", "x_new", "xgt", "rh", "ry"}
    RES_SEMS = ["y_in0", "y_in1", "added0", "added1", "stat", "agg", "mv", "sd", "rstd"]
    res = [{k: sem(f"res{n}_{k}") for k in RES_SEMS[:9 if n == 0 else 4]} for n in range(2)]

    PER = dict(xn=4, xt_ready=1, xts=2, qk_ready=4, qk=4, v_ready=2, v_sb=2, lm=4, kls=1, bd=4, qkr=2, bdr=2, xbo=1,
               s2_ready=1, s2m=1, s2s=1, s2e=1, s2sum=1, s2rc=1, s2n=1, s2bd=2, s3max_ready=8, s3m=8, s2t_ready=1, s2t=1, s2tbd=2,
               col_ready=1, row_ready=1, cs=1, rs=1, prod=1, r8=1, zt=1, s1max_ready=8, s1m=8, y0_ready=1, y=1, b1=PINV_ITERS, ybd0=PINV_ITERS, ybd1=PINV_ITERS,
               nm3_ready=1, nm1_ready=1, nm3=1, nm1=1, m1=PINV_ITERS, b2=PINV_ITERS, m2=PINV_ITERS, qb=2 * PINV_ITERS,
               m3=PINV_ITERS, yz=2 * (PINV_ITERS - 1), zbd=4, s3t_ready=8, e3=8, pv_ready=2, trc=2, tt=2, pt_ready=2, tm=2,
               s1t_ready=8, e1=8, w_ready=1, ws=1, o_ready=2, orc=2, ot=2, pr_ready=2, xo=2)
    att = {k: sem(f"att_{k}") for k in PER}
    s_picks = sem("att_picks")
    s_zero = sem("att_zeroed")

    def ffn_buffers(ctx, n):
        def b(name, cols, dt=F32):
            return sb(f"{name}_{n}", [P, cols], dt, ctx)
        B = dict(WU=b("WU", E * KD * F), WD=b("WD", E * KF * D), XNT=b("XNT", KD * T), HB=b("HB", KF * GW), HSB=b("HSB", 2 * F),
                 XS=b("XS", GT * D), OH=b("OH", NT * E), RT1=b("RT1", NT * E), RT2=b("RT2", SLOT_TILES * E), RT3=b("RT3", NT * E),
                 MX=b("MX", NT), SCORE=b("SCORE", NT), RSC=b("RSC", NT), NMR=b("NMR", NT), VM=b("VM", NT), CNT=b("CNT", 3 * E),
                 SLOTF=b("SLOTF", NT), SLOT=b("SLOT", NT, I32), RS4=b("RS4", GT), NM4=b("NM4", GT), SIDX=b("SIDX", GT, I32), STOK=b("STOK", GT, I32), GIDX=b("GIDX", UNR, I32), YIDX=b("YIDX", UNR, I32),
                 STILE=b("STILE", NT, I32), SROW=b("SROW", NT, I32), TOK=b("TOK", NT, I32), EXF=b("EXF", SLOT_TILES),
                 EXPERT=b("EXPERT", SLOT_TILES, I32), WHO=b("WHO", SLOT_TILES, I32))
        B["XN"], B["XTS"] = B["HB"][:, 0:GT * D], B["HB"][:, GT * D:2 * GT * D]
        at = 0
        for name, cols in (("XGT", UNR * D), ("RS", 2 * F), ("RH", UNR * F), ("HT", 2 * F), ("RY", UNR * D)):
            B[name] = B["XNT"][:, at:at + cols]
            at += cols
        return B

    def attention_buffers(ctx):
        def b(name, cols, dt=F32):
            return sb(f"A_{name}", [P, cols], dt, ctx)
        B = {}
        for name, cols in (("XN", GT * D), ("XTS", KD * GW), ("QT", KD * GW), ("KT", KD * GW), ("V", GT * D), ("QL", KD * M), ("KL", KD * M),
                           ("KLS", KD * M), ("QBD", KD * 512), ("KBD", KD * 512), ("E1", PAIRS * GW), ("E3", GT * 512), ("NM1", GT * H),
                           ("NM3", PAIRS), ("S2", 512), ("S2T", 512), ("YZ", PAIRS * P), ("YBD", PAIRS * P), ("QB", PAIRS * P), ("B1", 512),
                           ("SM", 6 * PAIRS), ("TT", KD * P), ("TM", PAIRS * 2 * HS), ("WS", PAIRS * 2 * HS), ("S2BD", PAIRS * P), ("S2TBD", PAIRS * P)):
            B[name] = b(name, cols)
        for name, cols in (("QTR", KD * GW), ("KTR", KD * GW), ("QBDR", KD * 512), ("KBDR", KD * 512), ("NM1T", GW), ("NM3BD", PAIRS * P),
                           ("ONESR", P), ("PICK", PAIRS * P)):
            B[name] = b(name, cols, F32R)
        B["OT"], B["RC"] = B["XTS"], B["XN"]
        return B

    with ExitStack() as ctx:
        fb0 = ffn_buffers(ctx, 0)
    with ExitStack() as ctx:
        ab = attention_buffers(ctx)
    with ExitStack() as ctx:
        fb1 = ffn_buffers(ctx, 1)
    fbs = [fb0, fb1]
    with ExitStack() as ctx:
        YL = [fbs[0]["HB"][:, u * GT * D:(u + 1) * GT * D] for u in range(2)], [fbs[1]["HB"][:, u * GT * D:(u + 1) * GT * D] for u in range(2)]

    block = top.enter_context(nc.Block())

    @block.sync
    def _(sp):
        for i in range(4):
            n = NT // 4
            sp.dma_start(X3[:, i * n:(i + 1) * n, :], x_rows[:, i * n:(i + 1) * n, :]).then_inc(s_x[i], 16)
            if i == 0:
                sp.dma_start(CB[:], consts).then_inc(s_const, 16)
                sp.dma_start(GWT[:], gate_w).then_inc(s_gate, 16)
        for buf, src in ((SG, sh_gate), (SU, sh_up), (SDN, sh_down)):
            sp.dma_start(buf[:], src).then_inc(s_shared, 16)
        sp.dma_start(WG[:], r_gate).then_inc(s_wg, 16)
        for buf, src in ((WQ, wq), (WK, wk), (WV, wv), (WO, wo)):
            sp.dma_start(buf[:], src).then_inc(s_attn_w, 16)
        sp.dma_start(BO[:], bo).then_inc(s_attn_w, 16)

        def ffn_dma(n):
            B = fbs[n]

            def need(eng, k, v):
                eng.wait_ge(s[k], n * FFN_PER[k] + (k in GIVEN) + v)

            if n == 1:
                sp.wait_ge(att["xo"], PER["xo"] * NG)
            sp.dma_start(B["WU"][:], r_up).then_inc(s["wu"], 16)
            sp.dma_start(B["WD"][:], r_down).then_inc(s["wd"], 16)
            need(sp, "nobody", 1)
            sp.dma_start(who_dram[n].rearrange("(p t) o -> p (t o)", p=P), B["WHO"][:]).then_inc(s["who_init"], 16)
            with sp.Fori(0, NG) as g:
                need(sp, "xs", g * GT + GT)
                sp.dma_start(xs_rows[:, bass.ds(g * GT, GT), :], B["XS"][:].rearrange("p (t d) -> p t d", d=D)).then_inc(s["xs_out"], 16)
            need(sp, "who", 16 * NT)
            sp.dma_start(B["WHO"][:], who_dram[n].rearrange("(p t) o -> p (t o)", p=P)).then_inc(s["who_sb"], 16)

        def load_routed_sums(n):
            r = res[n]
            for u in range(UNR):
                sp.wait_ge(s[f"ry_out{u}"], (n + 1) * FFN_PER[f"ry_out{u}"])
            with sp.Fori(0, NG // 2) as i:
                for u in range(2):
                    sp.wait_ge(r[f"added{u}"], i + 1)
                    sp.dma_start(YL[n][u].rearrange("p (t d) -> p t d", d=D),
                                 y_rows[:, bass.ds(i * 2 * GT + u * GT, GT), :]).then_inc(r[f"y_in{u}"], 16)
                    if n == 1 and u == 1:
                        sp.wait_ge(r["added1"], i + 2)
                        sp.dma_start(out_rows[:, bass.ds(i * 2 * GT, 2 * GT), :],
                                     X3[:, bass.ds(i * 2 * GT, 2 * GT), :]).then_inc(s_stored, 16)
            if n == 1:
                sp.wait_ge(s_stored, 16 * (NG // 2))

        ffn_dma(0)
        load_routed_sums(0)
        ffn_dma(1)
        load_routed_sums(1)

    @block.vector
    def _(dve):
        def wait_alone(semaphore, v):
            dve.wait_ge(semaphore, v)
            dve.sem_inc(s_dve_past, 1)

        def stats(q, g, n=0):
            for j in range(GT):
                dve.bn_stats(STATS[:, j * 6:(j + 1) * 6], X[:, bass.ds(g * GT * D + j * D, D)]).then_inc(q["stat"], 1)
            wait_alone(q["stat"], g * GT + n * NT + GT)
            for j in range(GT):
                dve.bn_aggr(AGG[:, j * 2:(j + 1) * 2], STATS[:, j * 6:(j + 1) * 6]).then_inc(q["agg"], 1)
            dve.wait_ge(q["agg"], g * GT + n * NT + GT)
            dve.tensor_copy(MV[:, bass.ds(g * GT * 2, GT * 2)], AGG[:]).then_inc(q["mv"], 1)

        def rstd(q, n=0):
            dve.wait_ge(q["sd"], n + 1)
            dve.reciprocal(RSTD[:], RSTD[:]).then_inc(q["rstd"], 1)
            dve.wait_ge(q["rstd"], n + 1)

        def normalise(dst, g, sem_xn):
            for j in range(GT):
                dve.tensor_scalar(dst[:, j * D:(j + 1) * D], X[:, bass.ds(g * GT * D + j * D, D)], MV[:, bass.ds(g * GT * 2 + j * 2, 1)],
                                  RSTD[:, bass.ds(g * GT + j, 1)], ALU.subtract, ALU.mult).then_inc(sem_xn, 1)

        def ffn_vector(n):
            B = fbs[n]

            def need(eng, k, v):
                eng.wait_ge(s[k], n * FFN_PER[k] + (k in GIVEN) + v)

            dve.memset(B["WHO"][:], NOBODY).then_inc(s["nobody"], 1)
            if n == 0:
                for i in range(4):
                    dve.wait_ge(s_x[i], 16)
                    with dve.Fori(i * 2, i * 2 + 2) as g:
                        stats(s, g, n)
                dve.wait_ge(s_const, 16)
            else:
                with dve.Fori(0, NG) as g:
                    stats(s, g, n)
            rstd(s, n)
            with dve.Fori(0, NG) as g:
                need(dve, "xt_ready", g)
                normalise(B["XN"], g, s["xn"])

            oh3 = B["OH"][:].rearrange("p (t e) -> p t e", e=E)
            rt1, rt3 = (B[k][:].rearrange("p (t e) -> p t e", e=E) for k in ("RT1", "RT3"))
            logits = banks[2][:, 0:NT * E].rearrange("p (t e) -> p t e", e=E)

            def over_e(ap):
                return ap.unsqueeze(2).broadcast_to([P, NT, E])

            def over_t(ap):
                return ap.unsqueeze(1).broadcast_to([P, NT, E])

            need(dve, "lg_ready", NG)
            dve.tensor_reduce(B["MX"][:], logits, AX_X, ALU.max).then_inc(s["mx"], 1)
            need(dve, "mx", 1)
            dve.tensor_tensor(rt1, logits, over_e(B["MX"][:]), ALU.is_equal).then_inc(s["onehot_step"], 1)
            need(dve, "onehot_step", 1)
            dve.tensor_tensor(rt3, rt1, over_t(const("expert_rank")), ALU.mult).then_inc(s["onehot_step"], 1)
            need(dve, "onehot_step", 2)
            dve.tensor_reduce(B["VM"][:], rt3, AX_X, ALU.max).then_inc(s["onehot_step"], 1)
            need(dve, "onehot_step", 3)
            dve.tensor_tensor(oh3, rt3, over_e(B["VM"][:]), ALU.is_equal).then_inc(s["oh"], 1)
            need(dve, "score", 1)
            dve.tensor_tensor(B["RSC"][:], RSTD[:], B["SCORE"][:], ALU.mult).then_inc(s["rs_step"], 1)
            need(dve, "rs_step", 1)
            dve.scalar_tensor_tensor(B["NMR"][:], mvv[:, :, 0], -1.0, B["RSC"][:], ALU.mult, ALU.mult).then_inc(s["rs"], 1)

            step = [0]

            def then(ins):
                step[0] += 1
                ins.then_inc(s["rt"], 1)
                need(dve, "rt", step[0])

            need(dve, "cnt_ready", 2)
            then(dve.tensor_copy(B["RT1"][:], banks[4][:, 0:NT * E]))
            incl = B["RT2"][:, 0:NT * E].rearrange("p (t e) -> p t e", e=E)
            for e in range(E):
                ins = dve.tensor_tensor_scan(incl[:, :, e], const("ones")[:, 0:NT], rt1[:, :, e], 0.0, ALU.mult, ALU.add)
                if e < E - 1:
                    step[0] += 1
                    ins.then_inc(s["rt"], 1)
            then(ins)
            total = B["RT2"][:, (NT - 1) * E:NT * E]
            then(dve.tensor_tensor(rt1, incl, rt1, ALU.subtract))
            more = B["RT3"][:].rearrange("p (e k) -> p e k", k=NT)
            then(dve.tensor_tensor(more, total.unsqueeze(2).broadcast_to([P, E, NT]),
                                   const("tile_edges").unsqueeze(1).broadcast_to([P, E, NT]), ALU.is_gt))
            tiles, ends, starts = (B["CNT"][:, i * E:(i + 1) * E] for i in range(3))
            then(dve.tensor_reduce(tiles, more, AX_X, ALU.add))
            then(dve.tensor_tensor_scan(ends, const("ones")[:, 0:E], tiles, 0.0, ALU.mult, ALU.add))
            then(dve.tensor_tensor(starts, ends, tiles, ALU.subtract))
            then(dve.tensor_tensor(rt1, banks[3][:, 0:NT * E].rearrange("p (t e) -> p t e", e=E), rt1, ALU.add))
            then(dve.scalar_tensor_tensor(rt1, over_t(starts), float(P), rt1, ALU.mult, ALU.add))
            then(dve.tensor_tensor(rt1, rt1, oh3, ALU.mult))
            then(dve.tensor_reduce(B["SLOTF"][:], rt1, AX_X, ALU.add))
            dve.tensor_copy(B["TOK"][:], const("token_no")).then_inc(s["slots"], 1)
            then(dve.tensor_copy(B["SLOT"][:], B["SLOTF"][:]))
            then(dve.tensor_scalar(B["STILE"][:], B["SLOT"][:], P.bit_length() - 1, None, ALU.arith_shift_right))
            then(dve.tensor_scalar(B["SROW"][:], B["SLOT"][:], P - 1, None, ALU.bitwise_and))
            dve.scalar_tensor_tensor(B["SLOT"][:], B["SROW"][:], float(SLOT_TILES), B["STILE"][:], ALU.mult, ALU.add).then_inc(s["slots"], 1)
            past = B["RT2"][:].rearrange("p (t e) -> p t e", e=E)
            then(dve.tensor_tensor(past, ends.unsqueeze(1).broadcast_to([P, SLOT_TILES, E]),
                                   const("tile_no").unsqueeze(2).broadcast_to([P, SLOT_TILES, E]), ALU.is_le))
            then(dve.tensor_reduce(B["EXF"][:], past, AX_X, ALU.add))
            dve.tensor_scalar(B["EXPERT"][:], B["EXF"][:], float(E - 1), None, ALU.min).then_inc(s["expert_of"], 1)

            assert step[0] == FFN_PER["rt"]

            with dve.Fori(0, NG) as g:
                for f in range(KF):
                    need(dve, "silu", g * KF + f + 1)
                    dve.tensor_tensor(B["HB"][:, f * GW:(f + 1) * GW], B["HSB"][:, (f % 2) * F:(f % 2 + 1) * F], banks[5 + f % 2][:],
                                      ALU.mult).then_inc(s["h"], 1)
                need(dve, "y_ready", g + 1)
                need(dve, "xs", g * GT + GT)
                for jj in range(2):
                    xg = X[:, bass.ds(g * GT * D + jj * 2 * D, 2 * D)]
                    dve.scalar_tensor_tensor(xg, banks[7 if jj == 0 else 2][:], 0.5, xg, ALU.mult, ALU.add).then_inc(s["x_new"], 1)

            with dve.Fori(0, SLOT_TILES // UNR) as it:
                for u in range(UNR):
                    need(dve, "rsilu", it * UNR + u + 1)
                    dve.tensor_tensor(B["RH"][:, u * F:(u + 1) * F], B["RS"][:, (u % 2) * F:(u % 2 + 1) * F], banks[3 + u % 2][:],
                                      ALU.mult).then_inc(s["rh"], 1)
                for u in range(UNR):
                    need(dve, "ry_ready", it * UNR + u + 1)
                    dve.wait_ge(s["ry_free"], n * SLOT_TILES + it * UNR + u + 1)
                    dve.tensor_copy(B["RY"][:, u * D:(u + 1) * D], banks[7][:, 0:D]).then_inc(s["ry"], 1)

        def add_routed(n):
            r = res[n]
            with dve.Fori(0, NG // 2) as i:
                for u in range(2):
                    dve.wait_ge(r[f"y_in{u}"], i * 16 + 16)
                    xg = X[:, bass.ds(i * 2 * GT * D + u * GT * D, GT * D)]
                    dve.scalar_tensor_tensor(xg, YL[n][u], 0.5, xg, ALU.mult, ALU.add).then_inc(r[f"added{u}"], 1)
                    if n == 0:
                        wait_alone(r[f"added{u}"], i + 2)
                        stats(r, i * 2 + u)
            if n == 0:
                rstd(r)

        def attention_vector():
            B = ab
            for name in ("YBD", "QB", "S2BD", "S2TBD"):
                dve.memset(B[name][:], 0.0).then_inc(s_zero, 1)
            for name in ("NM1T", "NM3BD"):
                dve.memset(B[name][:].bitcast(F32), 0.0).then_inc(s_zero, 1)
            dve.memset(B["PICK"][:].bitcast(F32), 0.0).then_inc(s_zero, 1)
            dve.wait_ge(s_zero, 7)
            dve.tensor_copy(B["ONESR"][:], const("ones")).then_inc(s_picks, 1)
            dve.tensor_copy(B["PICK"][0:H, :].rearrange("p (h m) -> p h m", m=M),
                            const("ident", H)[:, 0:H].unsqueeze(2).broadcast_to([H, H, M])).then_inc(s_picks, 1)

            def pairs(ap, w=M):
                return ap.rearrange("p (a m) -> p a m", m=w)

            def col8(ap):
                return ap.unsqueeze(2).broadcast_to([P, PAIRS, M])

            eye = const("eye2").unsqueeze(1).broadcast_to([P, PAIRS, M])
            eye_half = [const("eye2")[64 * i:64 * i + 64].unsqueeze(1).broadcast_to([64, PAIRS, M]) for i in range(2)]
            smx, ssum, src8, cs, rs, r8 = (B["SM"][:, i * PAIRS:(i + 1) * PAIRS] for i in range(6))
            YZ3 = pairs(B["YZ"][:], P)

            def block_half(buf, i):
                return pairs(buf[64 * i:64 * i + 64, :], P)[:, :, 64 * i:64 * i + 64]

            with dve.Fori(0, NG) as b:
                def wait(k, n):
                    dve.wait_ge(att[k], b * PER[k] + n)

                normalise(B["XN"], b, att["xn"])
                for i, (src, dst) in enumerate((("QT", "QL"), ("KT", "KL"))):
                    for c in range(KD):
                        wait("qk", 2 * i + c + 1)
                        dve.tensor_reduce(B[dst][:, c * M:(c + 1) * M], B[src][:, c * GW:(c + 1) * GW].rearrange("p (m l) -> p m l", l=LM),
                                          AX_X, ALU.add).then_inc(att["lm"], 1)
                wait("lm", 4)
                dve.tensor_scalar(B["KLS"][:], B["KL"][:], 1.0 / LM, None, ALU.mult).then_inc(att["kls"], 1)
                for src, dst in (("QL", "QBD"), ("KL", "KBD")):
                    for c in range(KD):
                        dve.scalar_tensor_tensor(B[dst][:, c * 512:(c + 1) * 512].rearrange("p (h m) -> p h m", m=M),
                                                 B[src][:, c * M:(c + 1) * M].unsqueeze(1).broadcast_to([P, HC, M]), 1.0 / LM,
                                                 const("head_rows").unsqueeze(2).broadcast_to([P, HC, M]),
                                                 ALU.mult, ALU.mult).then_inc(att["bd"], 1)
                dve.tensor_copy(B["KTR"][:], B["KT"][:]).then_inc(att["qkr"], 1)
                dve.tensor_copy(B["QTR"][:], B["QT"][:]).then_inc(att["qkr"], 1)
                wait("s2_ready", 1)
                s2p = pairs(banks[0][:])
                s2 = pairs(B["S2"][:])
                dve.tensor_reduce(smx, s2p, AX_X, ALU.max).then_inc(att["s2m"], 1)
                wait("s2m", 1)
                dve.tensor_tensor(s2, s2p, col8(smx), ALU.subtract).then_inc(att["s2s"], 1)

                def s3_max(p):
                    wait("s3max_ready", p + 1)
                    dve.tensor_reduce(B["NM3"][:, p:p + 1], banks[4 + p % 4][:], AX_X, ALU.max, negate=True).then_inc(att["s3m"], 1)

                def s1_max(n):
                    c, j = divmod(n, GT)
                    wait("s1max_ready", n + 1)
                    dve.tensor_reduce(B["NM1"][:, j * H + c * HC:j * H + (c + 1) * HC],
                                      banks[4 + n % 4][:].rearrange("p (h m) -> p h m", m=M), AX_X, ALU.max,
                                      negate=True).then_inc(att["s1m"], 1)

                for p in range(4):
                    s3_max(p)
                wait("s2e", 1)
                dve.tensor_reduce(ssum, s2, AX_X, ALU.add).then_inc(att["s2sum"], 1)
                wait("s2sum", 1)
                dve.reciprocal(src8, ssum).then_inc(att["s2rc"], 1)
                wait("s2rc", 1)
                dve.tensor_tensor(s2, s2, col8(src8), ALU.mult).then_inc(att["s2n"], 1)
                wait("s2n", 1)
                for i in range(2):
                    dve.tensor_copy(block_half(B["S2BD"], i), s2[64 * i:64 * i + 64]).then_inc(att["s2bd"], 1)
                for p in range(4, 8):
                    s3_max(p)
                wait("s2t", 1)
                for i in range(2):
                    dve.tensor_copy(block_half(B["S2TBD"], i), pairs(B["S2T"][64 * i:64 * i + 64, :])).then_inc(att["s2tbd"], 1)
                for n in range(4):
                    s1_max(n)
                wait("col_ready", 1)
                dve.tensor_reduce(cs, pairs(banks[2][:]), AX_X, ALU.max).then_inc(att["cs"], 1)
                wait("row_ready", 1)
                dve.tensor_reduce(rs, pairs(banks[3][:]), AX_X, ALU.max).then_inc(att["rs"], 1)
                wait("cs", 1)
                wait("rs", 1)
                dve.tensor_tensor(cs, cs, rs, ALU.mult).then_inc(att["prod"], 1)
                wait("prod", 1)
                dve.reciprocal(r8, cs).then_inc(att["r8"], 1)
                wait("r8", 1)
                dve.tensor_tensor(YZ3[:, :, M:P], s2, col8(r8), ALU.mult).then_inc(att["zt"], 1)
                for n in range(4, 8):
                    s1_max(n)
                wait("y0_ready", 1)
                dve.tensor_tensor(YZ3[:, :, 0:M], pairs(banks[0][:]), col8(r8), ALU.mult).then_inc(att["y"], 1)
                wait("y", 1)
                dve.scalar_tensor_tensor(pairs(B["B1"][:]), eye, 7.0, YZ3[:, :, 0:M], ALU.mult, ALU.subtract).then_inc(att["b1"], 1)
                dve.tensor_copy(block_half(B["YBD"], 0), YZ3[0:64, :, 0:M]).then_inc(att["ybd0"], 1)
                wait("nm3_ready", 1)
                dve.tensor_tensor(pairs(B["NM3BD"][0:PAIRS, :], P), banks[2][0:PAIRS, 0:P].unsqueeze(1).broadcast_to([PAIRS, PAIRS, P]),
                                  const("ident", PAIRS)[:, 0:PAIRS].unsqueeze(2).broadcast_to([PAIRS, PAIRS, P]), ALU.mult).then_inc(att["nm3"], 1)

                def t_norm(c):
                    wait("pv_ready", c + 1)
                    num, den = ((banks[4], banks[5]), (banks[6], banks[7]))[c]
                    tt = B["TT"][:, c * P:(c + 1) * P]
                    dve.reciprocal(tt, den[:, 0:P]).then_inc(att["trc"], 1)
                    wait("trc", c + 1)
                    dve.tensor_tensor(tt, num[:, 0:P], tt, ALU.mult).then_inc(att["tt"], 1)

                def t_mask(c):
                    wait("pt_ready", c + 1)
                    dve.tensor_tensor(B["TM"][:, c * P:(c + 1) * P].rearrange("p (a d) -> p a d", d=2 * HS),
                                      banks[4 + c][:, 0:P].rearrange("p (a d) -> p a d", d=2 * HS),
                                      const("pair_cols").unsqueeze(1).broadcast_to([P, PC, 2 * HS]), ALU.mult).then_inc(att["tm"], 1)

                def unit(slot):
                    if slot == 4:
                        t_norm(0)
                    if slot == 9:
                        t_norm(1)
                        t_mask(0)

                for it in range(PINV_ITERS):
                    wait("m1", it + 1)
                    dve.scalar_tensor_tensor(pairs(B["B1"][:]), eye, 15.0, pairs(banks[0][:]), ALU.mult, ALU.subtract).then_inc(att["b2"], 1)
                    unit(3 * it)
                    wait("m2", it + 1)
                    for i in range(2):
                        dve.scalar_tensor_tensor(block_half(B["QB"], i), eye_half[i], 13.0, pairs(banks[1][64 * i:64 * i + 64, :]),
                                                 ALU.mult, ALU.subtract).then_inc(att["qb"], 1)
                    unit(3 * it + 1)
                    if it < PINV_ITERS - 1:
                        wait("yz", 2 * it + 2)
                        dve.scalar_tensor_tensor(pairs(B["B1"][:]), eye, 7.0, YZ3[:, :, 0:M], ALU.mult, ALU.subtract).then_inc(att["b1"], 1)
                        dve.tensor_copy(block_half(B["YBD"], 0), YZ3[0:64, :, 0:M]).then_inc(att["ybd0"], 1)
                    else:
                        wait("m3", it + 1)
                        for i in range(2):
                            for c in range(KD):
                                dve.tensor_scalar(block_half(B["YBD"], i)[:, c * PC:(c + 1) * PC, :],
                                                  pairs(banks[2 + c][64 * i:64 * i + 64, :], P)[:, :, M:P], 0.25, None,
                                                  ALU.mult).then_inc(att["zbd"], 1)
                    unit(3 * it + 2)
                t_mask(1)
                wait("w_ready", 1)
                dve.tensor_copy(B["WS"][:], banks[0][:, 0:PAIRS * 2 * HS]).then_inc(att["ws"], 1)
                for c in range(KD):
                    wait("o_ready", c + 1)
                    num, den = ((banks[6], banks[7]), (banks[4], banks[5]))[c]
                    rc = B["RC"][:, c * GW:(c + 1) * GW]
                    dve.reciprocal(rc, den[:]).then_inc(att["orc"], 1)
                    wait("orc", c + 1)
                    dve.tensor_tensor(B["OT"][:, c * GW:(c + 1) * GW], num[:], rc, ALU.mult).then_inc(att["ot"], 1)
                wait("xbo", 1)
                for jj in range(2):
                    wait("pr_ready", jj + 1)
                    xg = X[:, bass.ds(b * GT * D + jj * 2 * D, 2 * D)]
                    dve.tensor_tensor(xg, banks[jj][:], xg, ALU.add).then_inc(att["xo"], 1)
                wait("xo", 2)

        ffn_vector(0)
        add_routed(0)
        attention_vector()
        ffn_vector(1)
        add_routed(1)

    @block.scalar
    def _(act):
        def deviation(q, n=0):
            act.wait_ge(q["mv"], n * NG + NG)
            act.activation(RSTD[:], mvv[:, :, 1], ACT.Sqrt, bias=const("eps")).then_inc(q["sd"], 1)

        def ffn_scalar(n):
            B = fbs[n]

            def need(eng, k, v):
                eng.wait_ge(s[k], n * FFN_PER[k] + (k in GIVEN) + v)

            if n == 0:
                act.wait_ge(s_const, 16)
            deviation(s, n)
            with act.Fori(0, NG) as g:
                need(act, "xt_ready", g + 1)
                need(act, "lg_ready", g)
                need(act, "xt_copied", g * KD)
                for k in range(KD):
                    act.copy(B["XTS"][:, k * GW:(k + 1) * GW], banks[k][:]).then_inc(s["xt_sb"], 1)
            need(act, "mx", 1)
            act.activation(B["SCORE"][:], B["MX"][:], ACT.Sigmoid).then_inc(s["score"], 1)
            with act.Fori(0, NG) as g:
                for f in range(KF):
                    need(act, "gu", g * KF + f + 1)
                    act.activation(B["HSB"][:, (f % 2) * F:(f % 2 + 1) * F], banks[f % 2][:], ACT.Silu).then_inc(s["silu"], 1)
            with act.Fori(0, SLOT_TILES // UNR) as it:
                def xgt(u):
                    need(act, "xg_t", it * UNR + u + 1)
                    act.copy(B["XGT"][:, u * D:(u + 1) * D], banks[0][:, 0:D]).then_inc(s["xgt"], 1)

                def silu(u):
                    need(act, "rgu", it * UNR + u + 1)
                    act.activation(B["RS"][:, (u % 2) * F:(u % 2 + 1) * F], banks[1 + u % 2][:], ACT.Silu).then_inc(s["rsilu"], 1)

                def ht(u):
                    need(act, "ht_ready", it * UNR + u + 1)
                    act.copy(B["HT"][:, (u % 2) * F:(u % 2 + 1) * F], banks[5 + u % 2][:]).then_inc(s["ht_sb"], 1)

                xgt(0)
                xgt(1)
                silu(0)
                silu(1)
                ht(0)
                xgt(2)
                silu(2)
                ht(1)
                ht(2)

        def attention_scalar():
            B = ab
            deviation(res[0])
            with act.Fori(0, NG) as b:
                def wait(k, n):
                    act.wait_ge(att[k], b * PER[k] + n)

                wait("xt_ready", 1)
                for k in range(KD):
                    act.copy(B["XTS"][:, k * GW:(k + 1) * GW], banks[k][:]).then_inc(att["xts"], 1)
                for i, (dst, scale) in enumerate((("QT", HS ** -0.5), ("KT", 1.0))):
                    for c in range(KD):
                        wait("qk_ready", 2 * i + c + 1)
                        act.mul(B[dst][:, c * GW:(c + 1) * GW], banks[2 + 2 * i + c][:], scale).then_inc(att["qk"], 1)
                for jj in range(2):
                    wait("v_ready", jj + 1)
                    act.copy(B["V"][:, jj * 512:(jj + 1) * 512], banks[6 + jj][:]).then_inc(att["v_sb"], 1)
                for i, (src, dst) in enumerate((("QBD", "QBDR"), ("KBD", "KBDR"))):
                    wait("bd", 2 * i + 2)
                    act.copy(B[dst][:], B[src][:]).then_inc(att["bdr"], 1)
                wait("s2s", 1)
                act.activation(B["S2"][:], B["S2"][:], ACT.Exp).then_inc(att["s2e"], 1)
                wait("s2t_ready", 1)
                act.copy(B["S2T"][:], banks[1][:]).then_inc(att["s2t"], 1)
                yz3 = B["YZ"][64:P, :].rearrange("p (a m) -> p a m", m=P)

                def y_lower():
                    act.copy(B["YBD"][64:P, :].rearrange("p (a m) -> p a m", m=P)[:, :, 64:P], yz3[:, :, 0:M]).then_inc(att["ybd1"], 1)

                wait("y", 1)
                y_lower()
                wait("nm1_ready", 1)
                act.copy(B["NM1T"][0:H, :], banks[3][0:H, :]).then_inc(att["nm1"], 1)

                def exp3(n):
                    c, j = divmod(n, GT)
                    wait("s3t_ready", n + 1)
                    act.activation(B["E3"][:, j * 512:(j + 1) * 512], banks[4 + (j + 2 * c) % 4][:], ACT.Exp).then_inc(att["e3"], 1)

                def exp1(p):
                    wait("s1t_ready", p + 1)
                    act.activation(B["E1"][:, p * GW:(p + 1) * GW], banks[4 + (p + 1) % 4][:], ACT.Exp).then_inc(att["e1"], 1)

                def unit(slot):
                    if slot < 4:
                        exp3(slot)
                    elif 5 <= slot < 9:
                        exp3(slot - 1)
                    elif slot >= 10:
                        exp1(slot - 10)

                for it in range(PINV_ITERS):
                    unit(3 * it)
                    unit(3 * it + 1)
                    if it < PINV_ITERS - 1:
                        wait("m3", it + 1)
                        for c in range(KD):
                            act.mul(B["YZ"][:, c * 512:(c + 1) * 512], banks[2 + c][:], 0.25).then_inc(att["yz"], 1)
                        wait("yz", 2 * it + 2)
                        y_lower()
                    unit(3 * it + 2)

        ffn_scalar(0)
        attention_scalar()
        ffn_scalar(1)

    @block.gpsimd
    def _(pool):
        def wait_alone(semaphore, v):
            pool.wait_ge(semaphore, v)
            pool.sem_inc(s_pool_past, 1)

        def ffn_pool(n):
            B = fbs[n]

            def need(k, v):
                wait_alone(s[k], n * FFN_PER[k] + (k in GIVEN) + v)

            with pool.Fori(0, NG) as g:
                need("xt_sb", g * KD + KD)
                for k in range(KD):
                    pool.tensor_copy(B["XNT"][:, bass.ds(g * GW + k * T, GW)], B["XTS"][:, k * GW:(k + 1) * GW]).then_inc(s["xt_copied"], 1)
            need("rs", 1)
            with pool.Fori(0, NG) as g:
                need("xs_out", g * 16)
                pool.tensor_copy(B["XS"][:], X[:, bass.ds(g * GT * D, GT * D)]).then_inc(s["xs_raw"], 1)
                pool.tensor_copy(B["RS4"][:], B["RSC"][:, bass.ds(g * GT, GT)]).then_inc(s["xs_raw"], 1)
                pool.tensor_copy(B["NM4"][:], B["NMR"][:, bass.ds(g * GT, GT)]).then_inc(s["xs_raw"], 1)
                need("xs_raw", g * 3 + 3)
                for j in range(GT):
                    row = B["XS"][:, j * D:(j + 1) * D]
                    pool.tensor_scalar(row, row, B["RS4"][:, j:j + 1], B["NM4"][:, j:j + 1], ALU.mult, ALU.add).then_inc(s["xs"], 1)
            need("slots", 2)
            need("who_init", 16)
            with pool.Fori(0, NG) as g:
                pool.tensor_copy(B["SIDX"][:], B["SLOT"][:, bass.ds(g * GT, GT)]).then_inc(s["sidx"], 1)
                pool.tensor_copy(B["STOK"][:], B["TOK"][:, bass.ds(g * GT, GT)]).then_inc(s["sidx"], 1)
                need("sidx", g * 2 + 2)
                for j in range(GT):
                    pool.indirect_dma_start(out=who_dram[n], out_offset=bass.IndirectOffsetOnAxis(ap=B["SIDX"][:, j:j + 1], axis=0),
                                            in_=B["STOK"][:, j:j + 1], in_offset=None).then_inc(s["who"], 16)
                need("who", (g + 1) * (16 * GT))

            def gather(t, u):
                pool.tensor_copy(B["GIDX"][:, u:u + 1], B["WHO"][:, bass.ds(t, 1)]).then_inc(s["gidx"], 1)
                need("gidx", t + 1)
                pool.indirect_dma_start(out=B["XS"][:, u * D:(u + 1) * D], out_offset=None, in_=xs_dram,
                                        in_offset=bass.IndirectOffsetOnAxis(ap=B["GIDX"][:, u:u + 1], axis=0),
                                        bounds_check=T - 1, oob_is_err=False).then_inc(s[f"gath{u}"], 16)

            def scatter(t, u):
                pool.tensor_copy(B["YIDX"][:, u:u + 1], B["WHO"][:, bass.ds(t, 1)]).then_inc(s["yidx"], 1)
                need("yidx", t + 1)
                pool.indirect_dma_start(out=y_dram, out_offset=bass.IndirectOffsetOnAxis(ap=B["YIDX"][:, u:u + 1], axis=0),
                                        in_=B["RY"][:, u * D:(u + 1) * D], in_offset=None,
                                        bounds_check=T - 1, oob_is_err=False).then_inc(s[f"ry_out{u}"], 16)

            need("who_sb", 16)
            need("xs_out", 16 * NG)
            for u in range(UNR):
                gather(u, u)
            last = SLOT_TILES // UNR - 1
            with pool.Fori(0, last) as it:
                for u in range(UNR):
                    need("xg_t", it * UNR + u + 1)
                    gather(it * UNR + UNR + u, u)
                for u in range(UNR):
                    need("ry", it * UNR + u + 1)
                    scatter(it * UNR + u, u)
                for u in range(UNR):
                    need(f"ry_out{u}", it * 16 + 16)
                    pool.sem_inc(s["ry_free"], 1)
            for u in range(UNR):
                need("ry", last * UNR + u + 1)
                scatter(last * UNR + u, u)
            for u in range(UNR):
                pool.wait_ge(s[f"ry_out{u}"], (n + 1) * FFN_PER[f"ry_out{u}"])
                pool.sem_inc(s["ry_free"], 1)

        def attention_pool():
            B = ab
            with pool.Fori(0, NG) as b:
                def wait(k, n):
                    wait_alone(att[k], b * PER[k] + n)

                wait("xn", GT)
                xg = X[:, bass.ds(b * GT * D, GT * D)].rearrange("p (t d) -> p t d", d=D)
                pool.tensor_tensor(xg, xg, BO[:].unsqueeze(1).broadcast_to([P, GT, D]), ALU.add).then_inc(att["xbo"], 1)

        for k in sorted(GIVEN):
            pool.sem_inc(s[k], 1)
        pool.sem_inc(s["ry_free"], UNR)
        for r in res:
            for u in range(2):
                pool.sem_inc(r[f"added{u}"], 1)
        ffn_pool(0)
        pool.wait_ge(s_attn_w, 16 * 5)
        pool.wait_ge(s_zero, 7)
        attention_pool()
        ffn_pool(1)

    @block.tensor
    def _(pe):
        ident = const("ident")

        def transposes(src, bank0, inc):
            for k in range(KD):
                for j in range(GT):
                    ins = pe.transpose(banks[bank0 + k][:, j * P:(j + 1) * P], src[:, j * D + k * P:j * D + (k + 1) * P], ident)
            ins.then_inc(inc, 1)

        def ffn_tensor(n):
            B = fbs[n]

            def need(eng, k, v):
                eng.wait_ge(s[k], n * FFN_PER[k] + (k in GIVEN) + v)

            if n == 0:
                pe.wait_ge(s_const, 16)
                pe.wait_ge(s_gate, 16)
            with pe.Fori(0, NG) as g:
                need(pe, "xn", g * GT + GT)
                need(pe, "xt_sb", g * KD)
                transposes(B["XN"], 0, s["xt_ready"])
                need(pe, "xt_sb", g * KD + KD)
                for j in range(GT):
                    for k in range(KD):
                        ins = pe.matmul(banks[2][:, bass.ds(g * GT * E + j * E, E)], B["XTS"][:, k * GW + j * P:k * GW + (j + 1) * P],
                                        GWT[:, k * E:(k + 1) * E], start=(k == 0), stop=(k == KD - 1))
                ins.then_inc(s["lg_ready"], 1)
            need(pe, "oh", 1)
            pe.matmul(banks[3][:, 0:NT * E], const("before"), B["OH"][:], start=True, stop=True).then_inc(s["cnt_ready"], 1)
            pe.matmul(banks[4][:, 0:NT * E], const("ones"), B["OH"][:], start=True, stop=True).then_inc(s["cnt_ready"], 1)

            if n == 0:
                pe.wait_ge(s_shared, 16 * 3)
            need(pe, "xt_copied", NG * KD)
            with pe.Fori(0, NG) as g:
                def gate_up(f):
                    if f < 2:
                        need(pe, "h", g * KF)
                    else:
                        need(pe, "h", g * KF + f - 1)
                    for bank, w in ((f % 2, SG), (5 + f % 2, SU)):
                        for k in range(KD):
                            ins = pe.matmul(banks[bank][:], w[:, k * F + f * P:k * F + (f + 1) * P], B["XNT"][:, bass.ds(g * GW + k * T, GW)],
                                            start=(k == 0), stop=(k == KD - 1))
                    ins.then_inc(s["gu"], 1)

                def down(f):
                    need(pe, "h", g * KF + f + 1)
                    if f == 0:
                        need(pe, "x_new", g * 2)
                    for j in range(GT):
                        ins = pe.matmul(banks[7 if j < 2 else 2][:, (j % 2) * D:(j % 2 + 1) * D], B["HB"][:, f * GW + j * P:f * GW + (j + 1) * P],
                                        SDN[:, f * D:(f + 1) * D], start=(f == 0 and j % 2 == 0), stop=(f == KF - 1), skip_group_check=True)
                    if f == KF - 1:
                        ins.then_inc(s["y_ready"], 1)

                gate_up(0)
                gate_up(1)
                down(0)
                gate_up(2)
                down(1)
                gate_up(3)
                down(2)
                down(3)

            if n == 0:
                pe.wait_ge(s_wg, 16)
            need(pe, "wu", 16)
            need(pe, "wd", 16)
            need(pe, "expert_of", 1)
            need(pe, "x_new", 2 * NG)
            with pe.Fori(0, SLOT_TILES // UNR) as it:
                ex = [pe.value_load(B["EXPERT"][0:1, bass.ds(it * UNR + u, 1)], min_val=0, max_val=E - 1) for u in range(UNR)]

                def xt(u):
                    need(pe, f"gath{u}", it * 16 + 16)
                    need(pe, "xgt", it * UNR + u)
                    for k in range(KD):
                        ins = pe.transpose(banks[0][:, k * P:(k + 1) * P], B["XS"][:, u * D + k * P:u * D + (k + 1) * P], ident)
                    ins.then_inc(s["xg_t"], 1)

                def gate_up(u):
                    need(pe, "xgt", it * UNR + u + 1)
                    need(pe, "rh", it * UNR + max(0, u - 1))
                    for bank, w in ((1 + u % 2, WG), (3 + u % 2, B["WU"])):
                        for k in range(KD):
                            ins = pe.matmul(banks[bank][:], B["XGT"][:, u * D + k * P:u * D + (k + 1) * P],
                                            w[:, bass.ds(ex[u] * (KD * F) + k * F, F)], start=(k == 0), stop=(k == KD - 1))
                    ins.then_inc(s["rgu"], 1)

                def ht(u):
                    need(pe, "rh", it * UNR + u + 1)
                    for f in range(KF):
                        ins = pe.transpose(banks[5 + u % 2][:, f * P:(f + 1) * P], B["RH"][:, u * F + f * P:u * F + (f + 1) * P], ident)
                    ins.then_inc(s["ht_ready"], 1)

                def down(u):
                    need(pe, "ht_sb", it * UNR + u + 1)
                    need(pe, "ry", it * UNR + u)
                    for f in range(KF):
                        ins = pe.matmul(banks[7][:, 0:D], B["HT"][:, (u % 2) * F + f * P:(u % 2) * F + (f + 1) * P],
                                        B["WD"][:, bass.ds(ex[u] * (KF * D) + f * D, D)], start=(f == 0), stop=(f == KF - 1))
                    ins.then_inc(s["ry_ready"], 1)

                xt(0)
                xt(1)
                gate_up(0)
                gate_up(1)
                ht(0)
                xt(2)
                gate_up(2)
                down(0)
                ht(1)
                ht(2)
                down(1)
                down(2)

        def attention_tensor():
            B = ab
            pe.wait_ge(s_attn_w, 16 * 5)
            pe.wait_ge(s_picks, 2)
            pe.wait_ge(s_zero, 7)
            with pe.Fori(0, NG) as b:
                def wait(k, n):
                    pe.wait_ge(att[k], b * PER[k] + n)

                def bd(buf, p):
                    return buf[:, p * P:(p + 1) * P]

                wait("xn", GT)
                transposes(B["XN"], 0, att["xt_ready"])
                wait("xts", KD)
                for i, w in enumerate((WQ, WK)):
                    for c in range(KD):
                        for k in range(KD):
                            ins = pe.matmul(banks[2 + 2 * i + c][:], w[:, k * D + c * P:k * D + (c + 1) * P], B["XTS"][:, k * GW:(k + 1) * GW],
                                            start=(k == 0), stop=(k == KD - 1))
                        ins.then_inc(att["qk_ready"], 1)
                for j in range(GT):
                    for k in range(KD):
                        ins = pe.matmul(banks[6 + j // 2][:, (j % 2) * D:(j % 2 + 1) * D], B["XTS"][:, k * GW + j * P:k * GW + (j + 1) * P],
                                        WV[:, k * D:(k + 1) * D], start=(k == 0), stop=(k == KD - 1))
                    if j % 2:
                        ins.then_inc(att["v_ready"], 1)
                wait("bd", 2)
                wait("kls", 1)
                for p in range(PAIRS):
                    c = p // PC
                    ins = pe.matmul(banks[0][:, p * M:(p + 1) * M], bd(B["QBD"], p), B["KLS"][:, c * M:(c + 1) * M], start=True, stop=True)
                ins.then_inc(att["s2_ready"], 1)
                wait("v_sb", 2)
                wait("bdr", 1)
                wait("qkr", 1)
                for p in range(PAIRS):
                    c = p // PC
                    if p >= 4:
                        wait("s3m", p - 3)
                    pe.matmul(banks[4 + p % 4][:], bd(B["QBDR"], p), B["KTR"][:, c * GW:(c + 1) * GW],
                              start=True, stop=True).then_inc(att["s3max_ready"], 1)
                wait("s2bd", 2)
                for p in range(PAIRS):
                    ins = pe.matmul(banks[1][:, p * M:(p + 1) * M], bd(B["S2BD"], p), const("eye2"), start=True, stop=True)
                ins.then_inc(att["s2t_ready"], 1)
                pe.matmul(banks[2][:], const("halves"), B["S2"][:], start=True, stop=True).then_inc(att["col_ready"], 1)
                wait("s2t", 1)
                pe.matmul(banks[3][:], const("halves"), B["S2T"][:], start=True, stop=True).then_inc(att["row_ready"], 1)
                wait("bdr", 2)
                wait("qkr", 2)
                for n in range(KD * GT):
                    c, j = divmod(n, GT)
                    if n < 4:
                        wait("s3m", n + 5)
                    else:
                        wait("s1m", n - 3)
                    pe.matmul(banks[4 + n % 4][:], B["QTR"][:, c * GW + j * P:c * GW + (j + 1) * P], B["KBDR"][:, c * 512:(c + 1) * 512],
                              start=True, stop=True).then_inc(att["s1max_ready"], 1)
                wait("s2tbd", 2)
                for p in range(PAIRS):
                    ins = pe.matmul(banks[0][:, p * M:(p + 1) * M], bd(B["S2TBD"], p), B["S2T"][:, p * M:(p + 1) * M], start=True, stop=True)
                ins.then_inc(att["y0_ready"], 1)
                wait("s1m", 8)
                wait("rs", 1)
                pe.transpose(banks[2][0:PAIRS, 0:P], B["NM3"][:], ident).then_inc(att["nm3_ready"], 1)
                for j in range(GT):
                    ins = pe.transpose(banks[3][0:H, j * P:(j + 1) * P], B["NM1"][:, j * H:(j + 1) * H], ident)
                ins.then_inc(att["nm1_ready"], 1)

                def s3t(n):
                    c, j = divmod(n, GT)
                    if n == 0:
                        wait("nm3", 1)
                    if c == 1 and j >= 2:
                        wait("tt", 1)
                    bank = banks[4 + (j + 2 * c) % 4]
                    pe.matmul(bank[:], B["KT"][:, c * GW + j * P:c * GW + (j + 1) * P], B["QBD"][:, c * 512:(c + 1) * 512], start=True, stop=False)
                    pe.matmul(bank[:], B["ONESR"][:], B["NM3BD"][:, c * 512:(c + 1) * 512], start=False, stop=True).then_inc(att["s3t_ready"], 1)

                def pv(c):
                    num, den = ((banks[4], banks[5]), (banks[6], banks[7]))[c]
                    wait("e3", 4 * c + 4)
                    for j in range(GT):
                        for q in range(PC):
                            rows = slice(32 * q, 32 * q + 32)
                            e3 = B["E3"][:, j * 512 + q * P:j * 512 + (q + 1) * P]
                            pe.matmul(num[rows, 0:P], B["V"][:, j * D + c * P + q * 32:j * D + c * P + (q + 1) * 32], e3,
                                      start=(j == 0), stop=(j == GT - 1))
                        for q in range(PC):
                            rows = slice(32 * q, 32 * q + 32)
                            e3 = B["E3"][:, j * 512 + q * P:j * 512 + (q + 1) * P]
                            ins = pe.matmul(den[rows, 0:P], const("ones")[:, 0:32], e3, start=(j == 0), stop=(j == GT - 1))
                    ins.then_inc(att["pv_ready"], 1)

                def pt(c):
                    wait("tt", c + 1)
                    pe.transpose(banks[4 + c][:, 0:P], B["TT"][:, c * P:(c + 1) * P], ident).then_inc(att["pt_ready"], 1)

                def s1t(p):
                    c = p // PC
                    if p == 0:
                        wait("nm1", 1)
                    if p in (1, 2):
                        wait("tt", 2)
                    if p == 3:
                        wait("tm", 1)
                    if p >= 4:
                        wait("e1", p - 3)
                    bank = banks[4 + (p + 1) % 4]
                    pe.matmul(bank[:], bd(B["KBD"], p), B["QT"][:, c * GW:(c + 1) * GW], start=True, stop=False)
                    pe.matmul(bank[:], bd(B["PICK"], p), B["NM1T"][:], start=False, stop=True).then_inc(att["s1t_ready"], 1)

                def unit(slot):
                    if slot < 4:
                        s3t(slot)
                    elif slot == 4:
                        pv(0)
                    elif slot < 9:
                        s3t(slot - 1)
                    elif slot == 9:
                        pv(1)
                        pt(0)
                    else:
                        s1t(slot - 10)

                for it in range(PINV_ITERS):
                    wait("b1", it + 1)
                    wait("ybd0", it + 1)
                    wait("ybd1", it + 1)
                    for p in range(PAIRS):
                        ins = pe.matmul(banks[0][:, p * M:(p + 1) * M], bd(B["YBD"], p), B["B1"][:, p * M:(p + 1) * M], start=True, stop=True)
                    ins.then_inc(att["m1"], 1)
                    unit(3 * it)
                    wait("b2", it + 1)
                    for p in range(PAIRS):
                        ins = pe.matmul(banks[1][:, p * M:(p + 1) * M], bd(B["YBD"], p), B["B1"][:, p * M:(p + 1) * M], start=True, stop=True)
                    ins.then_inc(att["m2"], 1)
                    unit(3 * it + 1)
                    wait("qb", 2 * it + 2)
                    if it == 0:
                        wait("zt", 1)
                        wait("nm3", 1)
                        wait("nm1", 1)
                    for p in range(PAIRS):
                        ins = pe.matmul(banks[2 + p // PC][:, (p % PC) * P:(p % PC + 1) * P], bd(B["QB"], p), bd(B["YZ"], p), start=True, stop=True)
                    ins.then_inc(att["m3"], 1)
                    unit(3 * it + 2)
                wait("e1", 5)
                pt(1)
                wait("zbd", 4)
                wait("tm", 2)
                for p in range(PAIRS):
                    ins = pe.matmul(banks[0][:, p * 32:(p + 1) * 32], bd(B["YBD"], p), B["TM"][:, p * 32:(p + 1) * 32], start=True, stop=True)
                ins.then_inc(att["w_ready"], 1)
                wait("ws", 1)
                wait("e1", 8)
                for c in range(KD):
                    num, den = ((banks[6], banks[7]), (banks[4], banks[5]))[c]
                    for q in range(PC):
                        p = c * PC + q
                        pe.matmul(num[32 * q:32 * q + 32, :], B["WS"][:, p * 32:(p + 1) * 32], B["E1"][:, p * GW:(p + 1) * GW], start=True, stop=True)
                    for q in range(PC):
                        p = c * PC + q
                        ins = pe.matmul(den[32 * q:32 * q + 32, :], const("pair_cols"), B["E1"][:, p * GW:(p + 1) * GW], start=True, stop=True)
                    ins.then_inc(att["o_ready"], 1)
                wait("ot", 2)
                for j in range(GT):
                    for c in range(KD):
                        ins = pe.matmul(banks[j // 2][:, (j % 2) * D:(j % 2 + 1) * D], B["OT"][:, c * GW + j * P:c * GW + (j + 1) * P],
                                        WO[:, c * D:(c + 1) * D], start=(c == 0), stop=(c == KD - 1))
                    if j % 2:
                        ins.then_inc(att["pr_ready"], 1)

        ffn_tensor(0)
        attention_tensor()
        ffn_tensor(1)


def kernel(L0_attn_x, L0_attn_Wk, L0_attn_Wq, L0_attn_Wv, L0_attn_Wo, L0_attn_bo, L0_ffn_gate_w, L0_ffn_shared_gate, L0_ffn_shared_up,
           L0_ffn_shared_down, L0_ffn_r_gate, L0_ffn_r_up, L0_ffn_r_down):
    import numpy as _np
    import concourse.bacc as _bacc
    from concourse import mybir as _mybir
    from concourse.bass_utils import run_bass_kernel_spmd as _run

    def rows(w):
        w = _np.asarray(w)
        *lead, k, n = w.shape
        w = w.reshape(*lead, k // P, P, n)
        return _np.ascontiguousarray(_np.moveaxis(w, -2, 0).reshape(P, -1))

    def turned(w):
        return rows(_np.swapaxes(_np.asarray(w), -1, -2))

    arrays = {
        "x": _np.ascontiguousarray(L0_attn_x), "wq": rows(L0_attn_Wq), "wk": rows(L0_attn_Wk), "wv": rows(L0_attn_Wv), "wo": rows(L0_attn_Wo),
        "bo": _np.ascontiguousarray(_np.broadcast_to(_np.asarray(L0_attn_bo), (P, D))), "gate_w": turned(L0_ffn_gate_w),
        "sh_gate": turned(L0_ffn_shared_gate), "sh_up": turned(L0_ffn_shared_up), "sh_down": turned(L0_ffn_shared_down),
        "r_gate": turned(L0_ffn_r_gate), "r_up": turned(L0_ffn_r_up), "r_down": turned(L0_ffn_r_down), "consts": constants(),
    }
    nc = _bacc.Bacc("TRN2", target_bir_lowering=False, num_devices=1)
    args = [nc.dram_tensor(f"in_{n}", a.shape, _mybir.dt.from_np(a.dtype), kind="ExternalInput").ap() for n, a in arrays.items()]
    args.append(nc.dram_tensor("out_0", tuple(L0_attn_x.shape), _mybir.dt.float32, kind="ExternalOutput").ap())
    macaron_kernel(nc, *args)
    r = _run(nc, [{f"in_{n}": a for n, a in arrays.items()}], core_ids=[0])
    return r.results[0]["out_0"]
```

```python
from contextlib import ExitStack

import numpy as np

import concourse.bass as bass
from concourse import mybir

ALU = mybir.AluOpType
ACT = mybir.ActivationFunctionType
AX_X = mybir.AxisListType.X
F32 = mybir.dt.float32
F32R = mybir.dt.float32r
I32 = mybir.dt.int32

P = 128
D = 256
KD = D // P
T = 4096
NT = T // P
GT = 4
NG = NT // GT
GW = GT * P
F = 512
KF = F // P
E = 8
SLOT_TILES = (T + E * (P - 1)) // P
UNR = 3
assert SLOT_TILES % UNR == 0
NOBODY = 2 * T
H = 16
HS = D // H
M = 64
LM = GW // M
PAIRS = H // 2
HC = P // HS
PC = PAIRS // KD
PINV_ITERS = 6
EPS = 1e-5

CONSTS = [("ident", P), ("before", P), ("ones", P), ("halves", P), ("eye2", M), ("head_rows", HC), ("pair_cols", 2 * HS),
          ("expert_rank", E), ("tile_edges", NT), ("tile_no", SLOT_TILES), ("token_no", NT), ("eps", 1)]
CONST_AT = {}
_at = 0
for _n, _w in CONSTS:
    CONST_AT[_n] = (_at, _w)
    _at += _w
CONST_W = _at


def constants():
    c = {n: np.zeros((P, w), np.float32) for n, w in CONSTS}
    c["ident"][:] = np.eye(P)
    c["before"][:] = np.triu(np.ones((P, P)), 1)
    c["ones"][:] = 1
    c["halves"][:] = np.kron(np.eye(2), np.ones((M, M)))
    c["eye2"][:] = np.tile(np.eye(M), (2, 1))
    c["head_rows"][:] = np.kron(np.eye(HC), np.ones((HS, 1)))
    c["pair_cols"][:] = np.kron(np.eye(2), np.ones((M, HS)))
    c["expert_rank"][:] = E - np.arange(E)
    c["tile_edges"][:] = P * np.arange(NT)
    c["tile_no"][:] = np.arange(SLOT_TILES)
    c["token_no"][:] = np.arange(P)[:, None] + P * np.arange(NT)
    c["eps"][:] = EPS
    return np.concatenate([c[n] for n, _ in CONSTS], 1)


def macaron_kernel(nc, x, wq, wk, wv, wo, bo, gate_w, sh_gate, sh_up, sh_down, r_gate, r_up, r_down, consts, out):
    with ExitStack() as top:
        emit(nc, top, x, wq, wk, wv, wo, bo, gate_w, sh_gate, sh_up, sh_down, r_gate, r_up, r_down, consts, out)


def emit(nc, top, x, wq, wk, wv, wo, bo, gate_w, sh_gate, sh_up, sh_down, r_gate, r_up, r_down, consts, out):
    def sb(name, shape, dt=F32, ctx=top):
        return ctx.enter_context(nc.sbuf_tensor(name, shape, dt))

    def sem(name):
        return top.enter_context(nc.semaphore(name))

    banks = [top.enter_context(nc.psum_tensor(f"bank{i}", [P, 512], F32)) for i in range(8)]

    X = sb("X", [P, (NT + GT) * D])
    CB = sb("CB", [P, CONST_W])
    SG = sb("SG", [P, KD * F])
    SU = sb("SU", [P, KD * F])
    SDN = sb("SDN", [P, KF * D])
    GWT = sb("GWT", [P, KD * E])
    WQ = sb("WQ", [P, KD * D])
    WK = sb("WK", [P, KD * D])
    WV = sb("WV", [P, KD * D])
    WO = sb("WO", [P, KD * D])
    BO = sb("BO", [P, D])
    STATS = sb("STATS", [P, GT * 6])
    AGG = sb("AGG", [P, GT * 2])
    MV = sb("MV", [P, NT * 2])
    RSTD = sb("RSTD", [P, NT])

    def const(name, rows=P):
        a, w = CONST_AT[name]
        return CB[0:rows, a:a + w]

    xs_dram = nc.dram_tensor("xs_dram", [T, D], F32, kind="Internal").ap()
    shared_dram = nc.dram_tensor("shared_dram", [T, D], F32, kind="Internal").ap()
    mid_dram = nc.dram_tensor("mid_dram", [T, D], F32, kind="Internal").ap()
    who_dram = [nc.dram_tensor(f"who_dram{i}", [SLOT_TILES * P, 1], I32, kind="Internal").ap() for i in range(2)]

    x_rows = x.rearrange("b (j p) d -> p (b j) d", p=P)
    out_flat = out.rearrange("b l d -> (b l) d")
    xs_rows = xs_dram.rearrange("(t p) d -> p t d", p=P)
    shared_rows = shared_dram.rearrange("(t p) d -> p t d", p=P)
    mid_rows = mid_dram.rearrange("(t p) d -> p t d", p=P)
    mvv = MV[:].rearrange("p (t c) -> p t c", c=2)
    X3 = X[:].rearrange("p (t d) -> p t d", d=D)

    s_x = [sem(f"x_loaded{i}") for i in range(4)]
    s_const = sem("consts_loaded")
    s_gate = sem("gate_loaded")
    s_shared = sem("shared_loaded")
    s_attn_w = sem("attention_weights_loaded")
    s_pool_past = sem("pool_past_a_wait")
    s_dve_past = sem("dve_past_a_wait")

    TILES3 = SLOT_TILES // UNR
    FFN_PER = dict(stat=NT, agg=NT, mv=NG, sd=NG, rstd=NG, xn=NT, xt_ready=NG, xt_sb=KD * NG, xt_copied=NG, lg_ready=NG, mx=1, onehot_step=3, oh=1,
                   score=1, rs_step=1, rs=1, xs=NT, xs_out=16 * NG, cnt_ready=2, rt=23, slots=2, expert_of=1, nobody=1, who_init=16,
                   who=16 * NT, who_sb=16, gu=KF * NG, silu=KF * NG, h=KF * NG, y_ready=NG, x_new=2 * NG, gath0=16 * TILES3, gath1=16 * TILES3,
                   gath2=16 * TILES3, xg_t=SLOT_TILES, xgt=SLOT_TILES, rg=SLOT_TILES, ru=SLOT_TILES, rsilu=SLOT_TILES, rh=SLOT_TILES, ht_ready=SLOT_TILES,
                   ht_sb=SLOT_TILES, ry_ready=SLOT_TILES, ry=SLOT_TILES, ry_out0=16 * TILES3, ry_out1=16 * TILES3, ry_out2=16 * TILES3, wg=16, wu=16, wd=16,
                   xs_raw=3 * NG, x_out=16 * NG, ry_clear=1, res_in0=16 * TILES3, res_in1=16 * TILES3, res_in2=16 * TILES3, sidx=2 * NG, gidx=SLOT_TILES, yidx=SLOT_TILES)
    s = {k: sem(f"ffn_{k}") for k in FFN_PER}
    GIVEN = {"xs_out", "h", "x_new", "ry"}
    res = {k: sem(f"res_{k}") for k in ("x_in", "x_zero", "stat", "agg", "sd", "rstd")}

    PER = dict(xn=4, xt_ready=1, xts=2, qk_ready=4, qk=4, qkr=4, v_ready=2, v_sb=2, lm=4, kls=1, bd=4, bdr=2, xbo=1,
               s2_ready=1, s2m=1, s2s=1, s2e=1, s2sum=1, s2rc=1, s2n=1, s2bd=2, s3max_ready=8, s3m=8, s2t_ready=1, s2t=1, s2tbd=2,
               col_ready=1, row_ready=1, cs=1, rs=1, prod=1, r8=1, zt=1, s1max_ready=8, s1m=8, y0_ready=1, y=1, b1=PINV_ITERS, ybd0=PINV_ITERS, ybd1=PINV_ITERS,
               nm3_ready=1, nm1_ready=1, nm3=1, nm1=1, m1=PINV_ITERS, b2=PINV_ITERS, m2=PINV_ITERS, qb=2 * PINV_ITERS,
               m3=PINV_ITERS, yz=2 * (PINV_ITERS - 1), zbd=4, s3t_ready=8, e3=8, pv_ready=2, trc=2, tt=2, pt_ready=2, tm=2,
               s1t_ready=8, e1=8, w_ready=1, ws=1, o_ready=2, orc=4, ot=4, pr_ready=2, xo=2)
    att = {k: sem(f"att_{k}") for k in PER}
    s_picks = sem("att_picks")
    s_zero = sem("att_zeroed")

    def ffn_buffers(ctx, n):
        def b(name, cols, dt=F32):
            return sb(f"{name}_{n}", [P, cols], dt, ctx)
        B = dict(WG=b("WG", E * KD * F), WU=b("WU", E * KD * F), WD=b("WD", E * KF * D), XNT=b("XNT", KD * T), HB=b("HB", KF * GW), HSB=b("HSB", 2 * F),
                 XS=b("XS", GT * D), OH=b("OH", NT * E),
                 MX=b("MX", NT), SCORE=b("SCORE", NT), RSC=b("RSC", NT), NMR=b("NMR", NT), VM=b("VM", NT), CNT=b("CNT", 3 * E),
                 SLOTF=b("SLOTF", NT), SLOT=b("SLOT", NT, I32), RS4=b("RS4", GT), NM4=b("NM4", GT), SIDX=b("SIDX", GT, I32), STOK=b("STOK", GT, I32), GIDX=b("GIDX", UNR, I32), YIDX=b("YIDX", UNR, I32),
                 STILE=b("STILE", NT, I32), SROW=b("SROW", NT, I32), TOK=b("TOK", NT, I32), EXF=b("EXF", SLOT_TILES),
                 EXPERT=b("EXPERT", SLOT_TILES, I32), WHO=b("WHO", SLOT_TILES, I32))
        B["XN"], B["XTS"] = (B["HB"][:, 0:GT * D], B["XS"][:]), (B["HB"][:, GT * D:2 * GT * D], B["HSB"][:])
        at = 0
        for name, cols in (("RT1", NT * E), ("RT2", SLOT_TILES * E), ("RT3", NT * E)):
            B[name] = B["WD"][:, at:at + cols]
            at += cols
        at = 0
        for name, cols in (("XGT", UNR * D), ("RS", UNR * F), ("RH", UNR * F), ("HT", UNR * F), ("RY", UNR * D)):
            B[name] = B["XNT"][:, at:at + cols]
            at += cols
        return B

    def attention_buffers(ctx):
        def b(name, cols, dt=F32):
            return sb(f"A_{name}", [P, cols], dt, ctx)
        B = {}
        for name, cols in (("XN", GT * D), ("XTS", KD * GW), ("QL", KD * M), ("KL", KD * M), ("KLS", KD * M), ("E1", PAIRS * GW), ("E3", GT * 512),
                           ("NM1", GT * H), ("NM3", PAIRS), ("S2", 512), ("S2T", 512), ("YZ", PAIRS * P), ("YBD", PAIRS * P), ("QB", PAIRS * P),
                           ("B1", 512), ("SM", 6 * PAIRS), ("TT", KD * P), ("TM", PAIRS * 2 * HS), ("WS", PAIRS * 2 * HS), ("S2BD", PAIRS * P),
                           ("S2TBD", PAIRS * P), ("OT", KD * GW), ("LNR", GT)):
            B[name] = b(name, cols)
        for name, cols in (("KTR", KD * GW), ("QBDR", KD * 512), ("KBDR", KD * 512), ("NM1T", GW), ("NM3BD", PAIRS * P), ("ONESR", P),
                           ("PICK", PAIRS * P)):
            B[name] = b(name, cols, F32R)
        for name, cols, dt in (("QT", KD * GW, F32), ("KT", KD * GW, F32), ("V", GT * D, F32), ("QBD", KD * 512, F32), ("KBD", KD * 512, F32),
                               ("QTR", KD * GW, F32R)):
            B[name] = [b(f"{name}{q}", cols, dt) for q in range(2)]
        return B

    with ExitStack() as ctx:
        fb0 = ffn_buffers(ctx, 0)
    with ExitStack() as ctx:
        ab = attention_buffers(ctx)
    with ExitStack() as ctx:
        fb1 = ffn_buffers(ctx, 1)
    fbs = [fb0, fb1]
    def over_batches(eng, front_alone, batch):
        front_alone()
        batch(0, 0, True, False)
        with eng.Fori(0, (NG - 2) // 2) as i:
            for u in range(2):
                batch(i * 2 + 1 + u, 1 - u, False, False)
        batch(NG - 1, (NG - 1) % 2, False, True)

    block = top.enter_context(nc.Block())

    @block.sync
    def _(sp):
        for i in range(4):
            n = NT // 4
            sp.dma_start(X3[:, i * n:(i + 1) * n, :], x_rows[:, i * n:(i + 1) * n, :]).then_inc(s_x[i], 16)
            if i == 0:
                sp.dma_start(CB[:], consts).then_inc(s_const, 16)
                sp.dma_start(GWT[:], gate_w).then_inc(s_gate, 16)
        for buf, src in ((SG, sh_gate), (SU, sh_up), (SDN, sh_down)):
            sp.dma_start(buf[:], src).then_inc(s_shared, 16)
        for buf, src in ((WQ, wq), (WK, wk), (WV, wv), (WO, wo)):
            sp.dma_start(buf[:], src).then_inc(s_attn_w, 16)
        sp.dma_start(BO[:], bo).then_inc(s_attn_w, 16)

        def ffn_dma(n):
            B = fbs[n]

            def need(eng, k, v):
                eng.wait_ge(s[k], n * FFN_PER[k] + (k in GIVEN) + v)

            if n == 1:
                sp.wait_ge(att["xo"], PER["xo"] * NG)
            sp.dma_start(B["WG"][:], r_gate).then_inc(s["wg"], 16)
            sp.dma_start(B["WU"][:], r_up).then_inc(s["wu"], 16)
            need(sp, "nobody", 1)
            sp.dma_start(who_dram[n].rearrange("(p t) o -> p (t o)", p=P), B["WHO"][:]).then_inc(s["who_init"], 16)
            with sp.Fori(0, NG) as g:
                need(sp, "xs", g * GT + GT)
                sp.dma_start(xs_rows[:, bass.ds(g * GT, GT), :], B["XS"][:].rearrange("p (t d) -> p t d", d=D)).then_inc(s["xs_out"], 16)
            need(sp, "expert_of", 1)
            sp.dma_start(B["WD"][:], r_down).then_inc(s["wd"], 16)
            need(sp, "who", 16 * NT)
            sp.dma_start(B["WHO"][:], who_dram[n].rearrange("(p t) o -> p (t o)", p=P)).then_inc(s["who_sb"], 16)
            with sp.Fori(0, NG) as g:
                need(sp, "x_new", g * 2 + 2)
                sp.dma_start(shared_rows[:, bass.ds(g * GT, GT), :], X3[:, bass.ds(g * GT, GT), :]).then_inc(s["x_out"], 16)

        def load_residual():
            for u in range(UNR):
                sp.wait_ge(s[f"ry_out{u}"], FFN_PER[f"ry_out{u}"])

            def load(g):
                sp.dma_start(X3[:, bass.ds(g * GT, GT), :], mid_rows[:, bass.ds(g * GT, GT), :]).then_inc(res["x_in"], 16)

            load(0)
            with sp.Fori(1, NG) as g:
                sp.wait_ge(res["x_in"], g * 16)
                load(g)

        ffn_dma(0)
        load_residual()
        ffn_dma(1)

    @block.vector
    def _(dve):
        def wait_alone(semaphore, v):
            dve.wait_ge(semaphore, v)
            dve.sem_inc(s_dve_past, 1)

        def stats(q, g, n=0):
            for j in range(GT):
                dve.bn_stats(STATS[:, j * 6:(j + 1) * 6], X[:, bass.ds(g * GT * D + j * D, D)]).then_inc(q["stat"], 1)
            wait_alone(q["stat"], g * GT + n * NT + GT)
            for j in range(GT):
                dve.bn_aggr(AGG[:, j * 2:(j + 1) * 2], STATS[:, j * 6:(j + 1) * 6]).then_inc(q["agg"], 1)
            dve.wait_ge(q["agg"], g * GT + n * NT + GT)
            dve.tensor_copy(MV[:, bass.ds(g * GT * 2, GT * 2)], AGG[:]).then_inc(q["mv"], 1)

        def rstd(q, g, n=0):
            dve.wait_ge(q["sd"], n * NG + g + 1)
            dve.reciprocal(RSTD[:, bass.ds(g * GT, GT)], RSTD[:, bass.ds(g * GT, GT)]).then_inc(q["rstd"], 1)
            wait_alone(q["rstd"], n * NG + g + 1)

        def normalise(dst, g, sem_xn):
            for j in range(GT):
                dve.tensor_scalar(dst[:, j * D:(j + 1) * D], X[:, bass.ds(g * GT * D + j * D, D)], MV[:, bass.ds(g * GT * 2 + j * 2, 1)],
                                  RSTD[:, bass.ds(g * GT + j, 1)], ALU.subtract, ALU.mult).then_inc(sem_xn, 1)

        def ffn_vector(n):
            B = fbs[n]

            def need(eng, k, v):
                eng.wait_ge(s[k], n * FFN_PER[k] + (k in GIVEN) + v)

            dve.memset(B["WHO"][:], NOBODY).then_inc(s["nobody"], 1)

            def keep(g, u):
                need(dve, "xt_sb", g * KD + KD)
                dve.tensor_copy(B["XNT"][:].rearrange("p (k t) -> p k t", k=KD)[:, :, bass.ds(g * GW, GW)],
                                B["XTS"][u].rearrange("p (k t) -> p k t", k=KD)).then_inc(s["xt_copied"], 1)

            def normalise_pair(i, first):
                for u in range(2):
                    g = i * 2 + u
                    stats(s, g, n)
                    rstd(s, g, n)
                    if not first:
                        need(dve, "xt_ready", g - 1)
                    normalise(B["XN"][u], g, s["xn"])
                    if not (first and u == 0):
                        keep(g - 1, 1 - u)

            if n == 0:
                dve.wait_ge(s_x[0], 16)
            normalise_pair(0, True)
            if n == 0:
                for i in range(1, NG // 2):
                    dve.wait_ge(s_x[i], 16)
                    normalise_pair(i, False)
            else:
                with dve.Fori(1, NG // 2) as i:
                    normalise_pair(i, False)
            keep(NG - 1, 1)

            oh3 = B["OH"][:].rearrange("p (t e) -> p t e", e=E)
            rt1, rt3 = (B[k][:].rearrange("p (t e) -> p t e", e=E) for k in ("RT1", "RT3"))
            logits = banks[2][:, 0:NT * E].rearrange("p (t e) -> p t e", e=E)

            def over_e(ap):
                return ap.unsqueeze(2).broadcast_to([P, NT, E])

            def over_t(ap):
                return ap.unsqueeze(1).broadcast_to([P, NT, E])

            need(dve, "lg_ready", NG)
            dve.tensor_reduce(B["MX"][:], logits, AX_X, ALU.max).then_inc(s["mx"], 1)
            need(dve, "mx", 1)
            dve.tensor_tensor(rt1, logits, over_e(B["MX"][:]), ALU.is_equal).then_inc(s["onehot_step"], 1)
            need(dve, "onehot_step", 1)
            dve.tensor_tensor(rt3, rt1, over_t(const("expert_rank")), ALU.mult).then_inc(s["onehot_step"], 1)
            need(dve, "onehot_step", 2)
            dve.tensor_reduce(B["VM"][:], rt3, AX_X, ALU.max).then_inc(s["onehot_step"], 1)
            need(dve, "onehot_step", 3)
            dve.tensor_tensor(oh3, rt3, over_e(B["VM"][:]), ALU.is_equal).then_inc(s["oh"], 1)
            need(dve, "score", 1)
            dve.tensor_tensor(B["RSC"][:], RSTD[:], B["SCORE"][:], ALU.mult).then_inc(s["rs_step"], 1)
            need(dve, "rs_step", 1)
            dve.scalar_tensor_tensor(B["NMR"][:], mvv[:, :, 0], -1.0, B["RSC"][:], ALU.mult, ALU.mult).then_inc(s["rs"], 1)

            step = [0]

            def then(ins):
                step[0] += 1
                ins.then_inc(s["rt"], 1)
                need(dve, "rt", step[0])

            need(dve, "cnt_ready", 2)
            then(dve.tensor_copy(B["RT1"][:], banks[4][:, 0:NT * E]))
            incl = B["RT2"][:, 0:NT * E].rearrange("p (t e) -> p t e", e=E)
            for e in range(E):
                ins = dve.tensor_tensor_scan(incl[:, :, e], const("ones")[:, 0:NT], rt1[:, :, e], 0.0, ALU.mult, ALU.add)
                if e < E - 1:
                    step[0] += 1
                    ins.then_inc(s["rt"], 1)
            then(ins)
            total = B["RT2"][:, (NT - 1) * E:NT * E]
            then(dve.tensor_tensor(rt1, incl, rt1, ALU.subtract))
            more = B["RT3"][:].rearrange("p (e k) -> p e k", k=NT)
            then(dve.tensor_tensor(more, total.unsqueeze(2).broadcast_to([P, E, NT]),
                                   const("tile_edges").unsqueeze(1).broadcast_to([P, E, NT]), ALU.is_gt))
            tiles, ends, starts = (B["CNT"][:, i * E:(i + 1) * E] for i in range(3))
            then(dve.tensor_reduce(tiles, more, AX_X, ALU.add))
            then(dve.tensor_tensor_scan(ends, const("ones")[:, 0:E], tiles, 0.0, ALU.mult, ALU.add))
            then(dve.tensor_tensor(starts, ends, tiles, ALU.subtract))
            then(dve.tensor_tensor(rt1, banks[3][:, 0:NT * E].rearrange("p (t e) -> p t e", e=E), rt1, ALU.add))
            then(dve.scalar_tensor_tensor(rt1, over_t(starts), float(P), rt1, ALU.mult, ALU.add))
            then(dve.tensor_tensor(rt1, rt1, oh3, ALU.mult))
            then(dve.tensor_reduce(B["SLOTF"][:], rt1, AX_X, ALU.add))
            dve.tensor_copy(B["TOK"][:], const("token_no")).then_inc(s["slots"], 1)
            then(dve.tensor_copy(B["SLOT"][:], B["SLOTF"][:]))
            then(dve.tensor_scalar(B["STILE"][:], B["SLOT"][:], P.bit_length() - 1, None, ALU.arith_shift_right))
            then(dve.tensor_scalar(B["SROW"][:], B["SLOT"][:], P - 1, None, ALU.bitwise_and))
            dve.scalar_tensor_tensor(B["SLOT"][:], B["SROW"][:], float(SLOT_TILES), B["STILE"][:], ALU.mult, ALU.add).then_inc(s["slots"], 1)
            past = B["RT2"][:].rearrange("p (t e) -> p t e", e=E)
            then(dve.tensor_tensor(past, ends.unsqueeze(1).broadcast_to([P, SLOT_TILES, E]),
                                   const("tile_no").unsqueeze(2).broadcast_to([P, SLOT_TILES, E]), ALU.is_le))
            then(dve.tensor_reduce(B["EXF"][:], past, AX_X, ALU.add))
            dve.tensor_scalar(B["EXPERT"][:], B["EXF"][:], float(E - 1), None, ALU.min).then_inc(s["expert_of"], 1)

            assert step[0] == FFN_PER["rt"]

            with dve.Fori(0, NG) as g:
                for f in range(KF):
                    need(dve, "silu", g * KF + f + 1)
                    dve.tensor_tensor(B["HB"][:, f * GW:(f + 1) * GW], B["HSB"][:, (f % 2) * F:(f % 2 + 1) * F], banks[5 + f % 2][:],
                                      ALU.mult).then_inc(s["h"], 1)
                need(dve, "y_ready", g + 1)
                need(dve, "xs", g * GT + GT)
                for jj in range(2):
                    xg = X[:, bass.ds(g * GT * D + jj * 2 * D, 2 * D)]
                    dve.scalar_tensor_tensor(xg, banks[7 if jj == 0 else 2][:], 0.5, xg, ALU.mult, ALU.add).then_inc(s["x_new"], 1)

            dve.memset(B["RY"][:], 0.0).then_inc(s["ry_clear"], 1)

            def tile_vector(it, u, first=False):
                t = it * UNR + u
                need(dve, "rsilu", t + 1)
                need(dve, "ru", t + 1)
                dve.tensor_tensor(B["RH"][:, u * F:(u + 1) * F], B["RS"][:, u * F:(u + 1) * F], banks[3 + u][:],
                                  ALU.mult).then_inc(s["rh"], 1)
                if not first:
                    tile_out(it if u else it - 1, (u - 1) % UNR)

            def tile_out(it, u):
                need(dve, "ry_ready", it * UNR + u + 1)
                need(dve, f"res_in{u}", it * 16 + 16)
                row = B["RY"][:, u * D:(u + 1) * D]
                dve.scalar_tensor_tensor(row, banks[7][:, 0:D], 0.5, row, ALU.mult, ALU.add).then_inc(s["ry"], 1)

            tile_vector(0, 0, True)
            for u in range(1, UNR):
                tile_vector(0, u)
            with dve.Fori(1, TILES3) as it:
                for u in range(UNR):
                    tile_vector(it, u)
            tile_out(TILES3 - 1, UNR - 1)

        def attention_vector():
            B = ab
            for name in ("YBD", "QB", "S2BD", "S2TBD"):
                dve.memset(B[name][:], 0.0).then_inc(s_zero, 1)
            for name in ("NM1T", "NM3BD"):
                dve.memset(B[name][:].bitcast(F32), 0.0).then_inc(s_zero, 1)
            dve.memset(B["PICK"][:].bitcast(F32), 0.0).then_inc(s_zero, 1)
            dve.wait_ge(s_zero, 7)
            dve.tensor_copy(B["ONESR"][:], const("ones")).then_inc(s_picks, 1)
            dve.tensor_copy(B["PICK"][0:H, :].rearrange("p (h m) -> p h m", m=M),
                            const("ident", H)[:, 0:H].unsqueeze(2).broadcast_to([H, H, M])).then_inc(s_picks, 1)

            def pairs(ap, w=M):
                return ap.rearrange("p (a m) -> p a m", m=w)

            def col8(ap):
                return ap.unsqueeze(2).broadcast_to([P, PAIRS, M])

            eye = const("eye2").unsqueeze(1).broadcast_to([P, PAIRS, M])
            eye_half = [const("eye2")[64 * i:64 * i + 64].unsqueeze(1).broadcast_to([64, PAIRS, M]) for i in range(2)]
            smx, ssum, src8, cs, rs, r8 = (B["SM"][:, i * PAIRS:(i + 1) * PAIRS] for i in range(6))
            YZ3 = pairs(B["YZ"][:], P)

            def wait(k, b, n):
                dve.wait_ge(att[k], b * PER[k] + n)

            def block_half(buf, i):
                return pairs(buf[64 * i:64 * i + 64, :], P)[:, :, 64 * i:64 * i + 64]

            def batch_stats(g):
                for j in range(GT):
                    dve.bn_stats(STATS[:, j * 6:(j + 1) * 6], X[:, bass.ds(g * GT * D + j * D, D)]).then_inc(res["stat"], 1)
                wait_alone(res["stat"], g * GT + GT)
                for j in range(GT):
                    dve.bn_aggr(AGG[:, j * 2:(j + 1) * 2], STATS[:, j * 6:(j + 1) * 6]).then_inc(res["agg"], 1)

            def batch_normalise(g):
                dve.wait_ge(res["sd"], g + 1)
                dve.reciprocal(B["LNR"][:], B["LNR"][:]).then_inc(res["rstd"], 1)
                wait_alone(res["rstd"], g + 1)
                for j in range(GT):
                    dve.tensor_scalar(B["XN"][:, j * D:(j + 1) * D], X[:, bass.ds(g * GT * D + j * D, D)], AGG[:, j * 2:j * 2 + 1],
                                      B["LNR"][:, j:j + 1], ALU.subtract, ALU.mult).then_inc(att["xn"], 1)

            def landmarks(b, q, i, c):
                src, dst = (("QT", "QL"), ("KT", "KL"))[i]
                wait("qk", b, 2 * i + c + 1)
                dve.tensor_reduce(B[dst][:, c * M:(c + 1) * M], B[src][q][:, c * GW:(c + 1) * GW].rearrange("p (m l) -> p m l", l=LM),
                                  AX_X, ALU.add).then_inc(att["lm"], 1)

            def block_diagonal(b, q, i, c):
                src, dst = (("QL", "QBD"), ("KL", "KBD"))[i]
                wait("lm", b, 2 * i + c + 1)
                dve.scalar_tensor_tensor(B[dst][q][:, c * 512:(c + 1) * 512].rearrange("p (h m) -> p h m", m=M),
                                         B[src][:, c * M:(c + 1) * M].unsqueeze(1).broadcast_to([P, HC, M]), 1.0 / LM,
                                         const("head_rows").unsqueeze(2).broadcast_to([P, HC, M]), ALU.mult, ALU.mult).then_inc(att["bd"], 1)

            def s3_max(b, p):
                wait("s3max_ready", b, p + 1)
                dve.tensor_reduce(B["NM3"][:, p:p + 1], banks[7][:], AX_X, ALU.max, negate=True).then_inc(att["s3m"], 1)

            def s1_max(b, n):
                c, j = divmod(n, GT)
                wait("s1max_ready", b, n + 1)
                dve.tensor_reduce(B["NM1"][:, j * H + c * HC:j * H + (c + 1) * HC], banks[7][:].rearrange("p (h m) -> p h m", m=M),
                                  AX_X, ALU.max, negate=True).then_inc(att["s1m"], 1)

            s2 = pairs(B["S2"][:])

            def front(b, q, slot):
                if slot == 5:
                    landmarks(b, q, 0, 0)
                if slot == 6:
                    landmarks(b, q, 0, 1)
                    block_diagonal(b, q, 0, 0)
                if slot == 7:
                    block_diagonal(b, q, 0, 1)
                    landmarks(b, q, 1, 0)
                if slot == 8:
                    landmarks(b, q, 1, 1)
                    wait("lm", b, 4)
                    dve.tensor_scalar(B["KLS"][:], B["KL"][:], 1.0 / LM, None, ALU.mult).then_inc(att["kls"], 1)
                if slot == 9:
                    block_diagonal(b, q, 1, 0)
                    block_diagonal(b, q, 1, 1)
                if slot == 10:
                    wait("s2_ready", b, 1)
                    dve.tensor_reduce(smx, pairs(banks[6][:]), AX_X, ALU.max).then_inc(att["s2m"], 1)
                    wait("s2m", b, 1)
                    dve.tensor_tensor(s2, pairs(banks[6][:]), col8(smx), ALU.subtract).then_inc(att["s2s"], 1)
                if 11 <= slot < 15:
                    s3_max(b, 2 * (slot - 11))
                    s3_max(b, 2 * (slot - 11) + 1)
                if slot == 12:
                    wait("s2e", b, 1)
                    dve.tensor_reduce(ssum, s2, AX_X, ALU.add).then_inc(att["s2sum"], 1)
                    wait("s2sum", b, 1)
                    dve.reciprocal(src8, ssum).then_inc(att["s2rc"], 1)
                    wait("s2rc", b, 1)
                    dve.tensor_tensor(s2, s2, col8(src8), ALU.mult).then_inc(att["s2n"], 1)
                if slot == 13:
                    wait("s2n", b, 1)
                    for i in range(2):
                        dve.tensor_copy(block_half(B["S2BD"], i), s2[64 * i:64 * i + 64]).then_inc(att["s2bd"], 1)
                if slot == 15:
                    wait("s2t", b, 1)
                    for i in range(2):
                        dve.tensor_copy(block_half(B["S2TBD"], i), pairs(B["S2T"][64 * i:64 * i + 64, :])).then_inc(att["s2tbd"], 1)
                    wait("col_ready", b, 1)
                    dve.tensor_reduce(cs, pairs(banks[7][:]), AX_X, ALU.max).then_inc(att["cs"], 1)
                if slot == 16:
                    wait("row_ready", b, 1)
                    dve.tensor_reduce(rs, pairs(banks[6][:]), AX_X, ALU.max).then_inc(att["rs"], 1)
                    wait("cs", b, 1)
                    wait("rs", b, 1)
                    dve.tensor_tensor(cs, cs, rs, ALU.mult).then_inc(att["prod"], 1)
                    wait("prod", b, 1)
                    dve.reciprocal(r8, cs).then_inc(att["r8"], 1)

            def start_z(b):
                wait("r8", b, 1)
                dve.tensor_tensor(YZ3[:, :, M:P], s2, col8(r8), ALU.mult).then_inc(att["zt"], 1)

            def start_y(b):
                wait("y0_ready", b, 1)
                dve.tensor_tensor(YZ3[:, :, 0:M], pairs(banks[1][:]), col8(r8), ALU.mult).then_inc(att["y"], 1)
                wait("y", b, 1)
                dve.scalar_tensor_tensor(pairs(B["B1"][:]), eye, 7.0, YZ3[:, :, 0:M], ALU.mult, ALU.subtract).then_inc(att["b1"], 1)
                dve.tensor_copy(block_half(B["YBD"], 0), YZ3[0:64, :, 0:M]).then_inc(att["ybd0"], 1)
                wait("nm3_ready", b, 1)
                dve.tensor_tensor(pairs(B["NM3BD"][0:PAIRS, :], P), banks[2][0:PAIRS, 0:P].unsqueeze(1).broadcast_to([PAIRS, PAIRS, P]),
                                  const("ident", PAIRS)[:, 0:PAIRS].unsqueeze(2).broadcast_to([PAIRS, PAIRS, P]), ALU.mult).then_inc(att["nm3"], 1)

            def t_norm(b, c):
                wait("pv_ready", b, c + 1)
                tt = B["TT"][:, c * P:(c + 1) * P]
                dve.reciprocal(tt, banks[5][:, 0:P]).then_inc(att["trc"], 1)
                wait("trc", b, c + 1)
                dve.tensor_tensor(tt, banks[4][:, 0:P], tt, ALU.mult).then_inc(att["tt"], 1)

            def t_mask(b, c):
                wait("pt_ready", b, c + 1)
                dve.tensor_tensor(B["TM"][:, c * P:(c + 1) * P].rearrange("p (a d) -> p a d", d=2 * HS),
                                  banks[4 + c][:, 0:P].rearrange("p (a d) -> p a d", d=2 * HS),
                                  const("pair_cols").unsqueeze(1).broadcast_to([P, PC, 2 * HS]), ALU.mult).then_inc(att["tm"], 1)

            def heads_norm(b, c, i):
                wait("o_ready", b, c + 1)
                num, den = ((banks[4], banks[5]), (banks[6], banks[7]))[c]
                w = GW // 2
                ot = B["OT"][:, c * GW + i * w:c * GW + (i + 1) * w]
                dve.reciprocal(ot, den[:, i * w:(i + 1) * w]).then_inc(att["orc"], 1)
                wait("orc", b, 2 * c + i + 1)
                dve.tensor_tensor(ot, num[:, i * w:(i + 1) * w], ot, ALU.mult).then_inc(att["ot"], 1)

            def project(b, jj):
                if jj == 0:
                    wait("xbo", b, 1)
                wait("pr_ready", b, jj + 1)
                xg = X[:, bass.ds(b * GT * D + jj * 2 * D, 2 * D)]
                dve.tensor_tensor(xg, banks[6][:], xg, ALU.add).then_inc(att["xo"], 1)

            def back(b, slot):
                if 2 <= slot < 10:
                    s1_max(b, slot - 2)
                if slot == 4:
                    t_norm(b, 0)
                if slot == 9:
                    t_norm(b, 1)
                if slot == 10:
                    t_mask(b, 0)
                    t_mask(b, 1)

            def front_alone():
                dve.memset(X[:, NT * D:], 0.0).then_inc(res["x_zero"], 1)
                dve.wait_ge(res["x_in"], 16)
                batch_stats(0)
                batch_normalise(0)
                for slot in range(3 * PINV_ITERS):
                    front(0, 0, slot)
                dve.wait_ge(res["x_in"], 32)
                batch_stats(1)
                batch_normalise(1)
                start_z(0)
                start_y(0)

            def batch(b, q, first, last):
                def step(slot):
                    if slot in (2, 3) and not first:
                        project(b - 1, slot - 2)
                    back(b, slot)
                    if not last:
                        front(b + 1, 1 - q, slot)
                        if slot == 11:
                            batch_stats(b + 2)
                        if slot == 17:
                            batch_normalise(b + 2)

                if first:
                    dve.wait_ge(res["x_in"], 16 * NG)
                    dve.wait_ge(res["x_zero"], 1)
                else:
                    heads_norm(b - 1, 1, 0)
                for it in range(PINV_ITERS):
                    wait("m1", b, it + 1)
                    dve.scalar_tensor_tensor(pairs(B["B1"][:]), eye, 15.0, pairs(banks[0][:]), ALU.mult, ALU.subtract).then_inc(att["b2"], 1)
                    if it == 0 and not first:
                        heads_norm(b - 1, 1, 1)
                    step(3 * it)
                    wait("m2", b, it + 1)
                    for i in range(2):
                        dve.scalar_tensor_tensor(block_half(B["QB"], i), eye_half[i], 13.0, pairs(banks[1][64 * i:64 * i + 64, :]),
                                                 ALU.mult, ALU.subtract).then_inc(att["qb"], 1)
                    step(3 * it + 1)
                    if it < PINV_ITERS - 1:
                        wait("yz", b, 2 * it + 2)
                        dve.scalar_tensor_tensor(pairs(B["B1"][:]), eye, 7.0, YZ3[:, :, 0:M], ALU.mult, ALU.subtract).then_inc(att["b1"], 1)
                        dve.tensor_copy(block_half(B["YBD"], 0), YZ3[0:64, :, 0:M]).then_inc(att["ybd0"], 1)
                    else:
                        wait("m3", b, it + 1)
                        for i in range(2):
                            for c in range(KD):
                                dve.tensor_scalar(block_half(B["YBD"], i)[:, c * PC:(c + 1) * PC, :],
                                                  pairs(banks[2 + c][64 * i:64 * i + 64, :], P)[:, :, M:P], 0.25, None,
                                                  ALU.mult).then_inc(att["zbd"], 1)
                    step(3 * it + 2)
                if not last:
                    start_z(b + 1)
                wait("w_ready", b, 1)
                dve.tensor_copy(B["WS"][:], banks[0][:, 0:PAIRS * 2 * HS]).then_inc(att["ws"], 1)
                for i in range(2):
                    heads_norm(b, 0, i)
                if not last:
                    start_y(b + 1)
                else:
                    for i in range(2):
                        heads_norm(b, 1, i)
                    for jj in range(2):
                        project(b, jj)
                    wait("xo", b, 2)

            over_batches(dve, front_alone, batch)

        ffn_vector(0)
        attention_vector()
        ffn_vector(1)

    @block.scalar
    def _(act):
        def deviation(q, g, n=0):
            act.wait_ge(q["mv"], n * NG + g + 1)
            act.activation(RSTD[:, bass.ds(g * GT, GT)], mvv[:, bass.ds(g * GT, GT), 1], ACT.Sqrt, bias=const("eps")).then_inc(q["sd"], 1)

        def ffn_scalar(n):
            B = fbs[n]

            def need(eng, k, v):
                eng.wait_ge(s[k], n * FFN_PER[k] + (k in GIVEN) + v)

            if n == 0:
                act.wait_ge(s_const, 16)

            def turned(g, u, first=False):
                need(act, "xt_ready", g + 1)
                if not first:
                    need(act, "lg_ready", g - 1)
                    need(act, "xt_copied", g - 1)
                for k in range(KD):
                    act.copy(B["XTS"][u][:, k * GW:(k + 1) * GW], banks[(0, 5)[u] + k][:]).then_inc(s["xt_sb"], 1)

            deviation(s, 0, n)
            deviation(s, 1, n)
            turned(0, 0, True)
            deviation(s, 2, n)
            turned(1, 1, True)
            with act.Fori(1, NG // 2 - 1) as i:
                for u in range(2):
                    deviation(s, i * 2 + u + 1, n)
                    turned(i * 2 + u, u)
            deviation(s, NG - 1, n)
            turned(NG - 2, 0)
            turned(NG - 1, 1)
            need(act, "mx", 1)
            act.activation(B["SCORE"][:], B["MX"][:], ACT.Sigmoid).then_inc(s["score"], 1)
            with act.Fori(0, NG) as g:
                for f in range(KF):
                    need(act, "gu", g * KF + f + 1)
                    act.activation(B["HSB"][:, (f % 2) * F:(f % 2 + 1) * F], banks[f % 2][:], ACT.Silu).then_inc(s["silu"], 1)

            def xgt(t, u):
                need(act, "xg_t", t + 1)
                act.copy(B["XGT"][:, u * D:(u + 1) * D], banks[0][:, 0:D]).then_inc(s["xgt"], 1)

            def silu(t, u):
                need(act, "rg", t + 1)
                act.activation(B["RS"][:, u * F:(u + 1) * F], banks[1 + u % 2][:], ACT.Silu).then_inc(s["rsilu"], 1)

            def ht(t, u):
                need(act, "ht_ready", t + 1)
                act.copy(B["HT"][:, u * F:(u + 1) * F], banks[6][:]).then_inc(s["ht_sb"], 1)

            def tile_scalar(it, u, first=False, last=False):
                t = it * UNR + u
                silu(t, u)
                if not first:
                    ht(t - 1, (u - 1) % UNR)
                if not last:
                    xgt(t + 1, (u + 1) % UNR)

            xgt(0, 0)
            tile_scalar(0, 0, first=True)
            for u in range(1, UNR):
                tile_scalar(0, u)
            with act.Fori(1, TILES3 - 1) as it:
                for u in range(UNR):
                    tile_scalar(it, u)
            for u in range(UNR):
                tile_scalar(TILES3 - 1, u, last=(u == UNR - 1))
            ht(SLOT_TILES - 1, UNR - 1)

        def attention_scalar():
            B = ab
            yz3 = B["YZ"][64:P, :].rearrange("p (a m) -> p a m", m=P)

            def wait(k, b, n):
                act.wait_ge(att[k], b * PER[k] + n)

            def batch_deviation(g):
                act.wait_ge(res["agg"], g * GT + GT)
                act.activation(B["LNR"][:], AGG[:].rearrange("p (t c) -> p t c", c=2)[:, :, 1], ACT.Sqrt, bias=const("eps")).then_inc(res["sd"], 1)

            def turned(b):
                wait("xt_ready", b, 1)
                for k in range(KD):
                    act.copy(B["XTS"][:, k * GW:(k + 1) * GW], banks[6 + k][:]).then_inc(att["xts"], 1)

            def y_lower():
                act.copy(B["YBD"][64:P, :].rearrange("p (a m) -> p a m", m=P)[:, :, 64:P], yz3[:, :, 0:M]).then_inc(att["ybd1"], 1)

            def start_y(b):
                wait("y", b, 1)
                y_lower()

            def rounded(b, dst, src, k):
                act.copy(dst, src).then_inc(att[k], 1)

            def front(b, q, slot, alone=False):
                if 4 <= slot < 8:
                    i, c = divmod(slot - 4, KD)
                    (dst, scale), dst_r = (("QT", HS ** -0.5), ("KT", 1.0))[i], (B["QTR"][q], B["KTR"])[i]
                    part = slice(c * GW, (c + 1) * GW)
                    wait("qk_ready", b, slot - 3)
                    act.mul(B[dst][q][:, part], banks[6][:], scale).then_inc(att["qk"], 1)
                    wait("qk", b, slot - 3)
                    rounded(b, dst_r[:, part], B[dst][q][:, part], "qkr")
                if slot in (8, 9):
                    wait("v_ready", b, slot - 7)
                    act.copy(B["V"][q][:, (slot - 8) * 512:(slot - 7) * 512], banks[6][:]).then_inc(att["v_sb"], 1)
                if slot == 9:
                    wait("bd", b, 2)
                    rounded(b, B["QBDR"][:], B["QBD"][q][:], "bdr")
                if slot == 11:
                    wait("s2s", b, 1)
                    act.activation(B["S2"][:], B["S2"][:], ACT.Exp).then_inc(att["s2e"], 1)
                if slot == 12:
                    wait("bd", b, 4)
                    if not alone:
                        wait("s1max_ready", b - 1, 8)
                    rounded(b, B["KBDR"][:], B["KBD"][q][:], "bdr")
                if slot == 14:
                    wait("s2t_ready", b, 1)
                    act.copy(B["S2T"][:], banks[6][:]).then_inc(att["s2t"], 1)

            def exp3(b, n):
                wait("s3t_ready", b, n + 1)
                act.activation(B["E3"][:, n % GT * 512:(n % GT + 1) * 512], banks[4 + n % 2][:], ACT.Exp).then_inc(att["e3"], 1)

            def exp1(b, p):
                wait("s1t_ready", b, p + 1)
                act.activation(B["E1"][:, p * GW:(p + 1) * GW], banks[4 + p % 2][:], ACT.Exp).then_inc(att["e1"], 1)

            def back(b, slot):
                if slot < 4:
                    exp3(b, slot)
                elif 5 <= slot < 9:
                    exp3(b, slot - 1)
                elif slot == 10:
                    wait("nm1_ready", b, 1)
                    act.copy(B["NM1T"][0:H, :], banks[7][0:H, :]).then_inc(att["nm1"], 1)
                elif slot >= 11:
                    exp1(b, slot - 11)

            def front_alone():
                batch_deviation(0)
                turned(0)
                for slot in range(3 * PINV_ITERS):
                    front(0, 0, slot, alone=True)
                batch_deviation(1)
                turned(1)
                start_y(0)

            def batch(b, q, first, last):
                def step(slot):
                    if not last:
                        front(b + 1, 1 - q, slot)
                        if slot == 13:
                            batch_deviation(b + 2)
                    back(b, slot)

                for it in range(PINV_ITERS):
                    step(3 * it)
                    step(3 * it + 1)
                    if it < PINV_ITERS - 1:
                        wait("m3", b, it + 1)
                        for c in range(KD):
                            act.mul(B["YZ"][:, c * 512:(c + 1) * 512], banks[2 + c][:], 0.25).then_inc(att["yz"], 1)
                        wait("yz", b, 2 * it + 2)
                        y_lower()
                    step(3 * it + 2)
                exp1(b, PAIRS - 1)
                if not last:
                    turned(b + 2)
                    start_y(b + 1)

            over_batches(act, front_alone, batch)

        ffn_scalar(0)
        attention_scalar()
        ffn_scalar(1)

    @block.gpsimd
    def _(pool):
        def wait_alone(semaphore, v):
            pool.wait_ge(semaphore, v)
            pool.sem_inc(s_pool_past, 1)

        def ffn_pool(n):
            B = fbs[n]

            def need(k, v):
                wait_alone(s[k], n * FFN_PER[k] + (k in GIVEN) + v)

            need("rs", 1)
            with pool.Fori(0, NG) as g:
                need("xs_out", g * 16)
                pool.tensor_copy(B["XS"][:], X[:, bass.ds(g * GT * D, GT * D)]).then_inc(s["xs_raw"], 1)
                pool.tensor_copy(B["RS4"][:], B["RSC"][:, bass.ds(g * GT, GT)]).then_inc(s["xs_raw"], 1)
                pool.tensor_copy(B["NM4"][:], B["NMR"][:, bass.ds(g * GT, GT)]).then_inc(s["xs_raw"], 1)
                need("xs_raw", g * 3 + 3)
                for j in range(GT):
                    row = B["XS"][:, j * D:(j + 1) * D]
                    pool.tensor_scalar(row, row, B["RS4"][:, j:j + 1], B["NM4"][:, j:j + 1], ALU.mult, ALU.add).then_inc(s["xs"], 1)
            need("slots", 2)
            need("who_init", 16)
            with pool.Fori(0, NG) as g:
                pool.tensor_copy(B["SIDX"][:], B["SLOT"][:, bass.ds(g * GT, GT)]).then_inc(s["sidx"], 1)
                pool.tensor_copy(B["STOK"][:], B["TOK"][:, bass.ds(g * GT, GT)]).then_inc(s["sidx"], 1)
                need("sidx", g * 2 + 2)
                for j in range(GT):
                    pool.indirect_dma_start(out=who_dram[n], out_offset=bass.IndirectOffsetOnAxis(ap=B["SIDX"][:, j:j + 1], axis=0),
                                            in_=B["STOK"][:, j:j + 1], in_offset=None).then_inc(s["who"], 16)
                need("who", (g + 1) * (16 * GT))

            def gather(t, u):
                pool.tensor_copy(B["GIDX"][:, u:u + 1], B["WHO"][:, bass.ds(t, 1)]).then_inc(s["gidx"], 1)
                need("gidx", t + 1)
                pool.indirect_dma_start(out=B["XS"][:, u * D:(u + 1) * D], out_offset=None, in_=xs_dram,
                                        in_offset=bass.IndirectOffsetOnAxis(ap=B["GIDX"][:, u:u + 1], axis=0),
                                        bounds_check=T - 1, oob_is_err=False).then_inc(s[f"gath{u}"], 16)

            def gather_residual(t, u):
                pool.tensor_copy(B["YIDX"][:, u:u + 1], B["WHO"][:, bass.ds(t, 1)]).then_inc(s["yidx"], 1)
                need("yidx", t + 1)
                pool.indirect_dma_start(out=B["RY"][:, u * D:(u + 1) * D], out_offset=None, in_=shared_dram,
                                        in_offset=bass.IndirectOffsetOnAxis(ap=B["YIDX"][:, u:u + 1], axis=0),
                                        bounds_check=T - 1, oob_is_err=False).then_inc(s[f"res_in{u}"], 16)

            def scatter(t, u):
                need("ry", t + 1)
                pool.indirect_dma_start(out=mid_dram if n == 0 else out_flat, out_offset=bass.IndirectOffsetOnAxis(ap=B["YIDX"][:, u:u + 1], axis=0),
                                        in_=B["RY"][:, u * D:(u + 1) * D], in_offset=None,
                                        bounds_check=T - 1, oob_is_err=False).then_inc(s[f"ry_out{u}"], 16)

            def tile_dma(it, u, first=False, last=False):
                t = it * UNR + u
                if not last:
                    need("xg_t", t + 1)
                    gather(t + UNR, u)
                scatter(t, u)
                if not (last and u > 0):
                    if not first:
                        need(f"ry_out{(u - 1) % UNR}", (it if u else it - 1) * 16 + 16)
                    gather_residual(t + UNR - 1, (u - 1) % UNR)

            need("who_sb", 16)
            need("xs_out", 16 * NG)
            for u in range(UNR):
                gather(u, u)
            need("x_out", 16 * NG)
            need("ry_clear", 1)
            for u in range(UNR - 1):
                gather_residual(u, u)
            tile_dma(0, 0, first=True)
            for u in range(1, UNR):
                tile_dma(0, u)
            with pool.Fori(1, TILES3 - 1) as it:
                for u in range(UNR):
                    tile_dma(it, u)
            for u in range(UNR):
                tile_dma(TILES3 - 1, u, last=True)
            for u in range(UNR):
                pool.wait_ge(s[f"ry_out{u}"], (n + 1) * FFN_PER[f"ry_out{u}"])

        def attention_pool():
            B = ab
            with pool.Fori(0, NG) as b:
                def wait(k, n):
                    wait_alone(att[k], b * PER[k] + n)

                wait("xn", GT)
                xg = X[:, bass.ds(b * GT * D, GT * D)].rearrange("p (t d) -> p t d", d=D)
                pool.tensor_tensor(xg, xg, BO[:].unsqueeze(1).broadcast_to([P, GT, D]), ALU.add).then_inc(att["xbo"], 1)

        for k in sorted(GIVEN):
            pool.sem_inc(s[k], 1)
        ffn_pool(0)
        pool.wait_ge(s_attn_w, 16 * 5)
        pool.wait_ge(s_zero, 7)
        attention_pool()
        ffn_pool(1)

    @block.tensor
    def _(pe):
        ident = const("ident")

        def transposes(src, bank0, inc):
            for k in range(KD):
                for j in range(GT):
                    ins = pe.transpose(banks[bank0 + k][:, j * P:(j + 1) * P], src[:, j * D + k * P:j * D + (k + 1) * P], ident)
            ins.then_inc(inc, 1)

        def ffn_tensor(n):
            B = fbs[n]

            def need(eng, k, v):
                eng.wait_ge(s[k], n * FFN_PER[k] + (k in GIVEN) + v)

            if n == 0:
                pe.wait_ge(s_const, 16)
                pe.wait_ge(s_gate, 16)

            def turn(g, u, first=False):
                need(pe, "xn", g * GT + GT)
                if not first:
                    need(pe, "xt_sb", (g - 1) * KD)
                transposes(B["XN"][u], (0, 5)[u], s["xt_ready"])

            def logits(g, u):
                need(pe, "xt_sb", g * KD + KD)
                for j in range(GT):
                    for k in range(KD):
                        ins = pe.matmul(banks[2][:, bass.ds(g * GT * E + j * E, E)], B["XTS"][u][:, k * GW + j * P:k * GW + (j + 1) * P],
                                        GWT[:, k * E:(k + 1) * E], start=(k == 0), stop=(k == KD - 1))
                ins.then_inc(s["lg_ready"], 1)

            turn(0, 0, True)
            turn(1, 1, True)
            logits(0, 0)
            with pe.Fori(1, NG // 2) as i:
                turn(i * 2, 0)
                logits(i * 2 - 1, 1)
                turn(i * 2 + 1, 1)
                logits(i * 2, 0)
            logits(NG - 1, 1)
            need(pe, "oh", 1)
            pe.matmul(banks[3][:, 0:NT * E], const("before"), B["OH"][:], start=True, stop=True).then_inc(s["cnt_ready"], 1)
            pe.matmul(banks[4][:, 0:NT * E], const("ones"), B["OH"][:], start=True, stop=True).then_inc(s["cnt_ready"], 1)

            if n == 0:
                pe.wait_ge(s_shared, 16 * 3)
            need(pe, "xt_copied", NG)
            with pe.Fori(0, NG) as g:
                def gate_up(f):
                    if f < 2:
                        need(pe, "h", g * KF)
                    else:
                        need(pe, "h", g * KF + f - 1)
                    for bank, w in ((f % 2, SG), (5 + f % 2, SU)):
                        for k in range(KD):
                            ins = pe.matmul(banks[bank][:], w[:, k * F + f * P:k * F + (f + 1) * P], B["XNT"][:, bass.ds(g * GW + k * T, GW)],
                                            start=(k == 0), stop=(k == KD - 1))
                    ins.then_inc(s["gu"], 1)

                def down(f):
                    need(pe, "h", g * KF + f + 1)
                    if f == 0:
                        need(pe, "x_new", g * 2)
                    for j in range(GT):
                        ins = pe.matmul(banks[7 if j < 2 else 2][:, (j % 2) * D:(j % 2 + 1) * D], B["HB"][:, f * GW + j * P:f * GW + (j + 1) * P],
                                        SDN[:, f * D:(f + 1) * D], start=(f == 0 and j % 2 == 0), stop=(f == KF - 1), skip_group_check=True)
                    if f == KF - 1:
                        ins.then_inc(s["y_ready"], 1)

                gate_up(0)
                gate_up(1)
                down(0)
                gate_up(2)
                down(1)
                gate_up(3)
                down(2)
                down(3)

            need(pe, "wg", 16)
            need(pe, "wu", 16)
            need(pe, "wd", 16)
            need(pe, "expert_of", 1)
            need(pe, "x_new", 2 * NG)

            def expert(t):
                return pe.value_load(B["EXPERT"][0:1, bass.ds(t, 1)], min_val=0, max_val=E - 1)

            def xt(it, u):
                need(pe, f"gath{u}", it * 16 + 16)
                for k in range(KD):
                    ins = pe.transpose(banks[0][:, k * P:(k + 1) * P], B["XS"][:, u * D + k * P:u * D + (k + 1) * P], ident)
                ins.then_inc(s["xg_t"], 1)

            def through(bank, w, u, ex, inc):
                for k in range(KD):
                    ins = pe.matmul(banks[bank][:], B["XGT"][:, u * D + k * P:u * D + (k + 1) * P], w[:, bass.ds(ex * (KD * F) + k * F, F)],
                                    start=(k == 0), stop=(k == KD - 1))
                ins.then_inc(inc, 1)

            def ht(t, u):
                need(pe, "rh", t + 1)
                for f in range(KF):
                    ins = pe.transpose(banks[6][:, f * P:(f + 1) * P], B["RH"][:, u * F + f * P:u * F + (f + 1) * P], ident)
                ins.then_inc(s["ht_ready"], 1)

            def down(t, u, ex):
                need(pe, "ht_sb", t + 1)
                need(pe, "ry", t)
                for f in range(KF):
                    ins = pe.matmul(banks[7][:, 0:D], B["HT"][:, u * F + f * P:u * F + (f + 1) * P],
                                    B["WD"][:, bass.ds(ex * (KF * D) + f * D, D)], start=(f == 0), stop=(f == KF - 1))
                ins.then_inc(s["ry_ready"], 1)

            def tile_tensor(it, u, before, now, first=False, last=False):
                t = it * UNR + u
                need(pe, "xgt", t + 1)
                if not first:
                    need(pe, "rsilu", t)
                through(1 + u % 2, B["WG"], u, now, s["rg"])
                if not first:
                    ht(t - 1, (u - 1) % UNR)
                through(3 + u, B["WU"], u, now, s["ru"])
                if not last:
                    xt(it if u < UNR - 1 else it + 1, (u + 1) % UNR)
                if not first:
                    down(t - 1, (u - 1) % UNR, before)

            xt(0, 0)
            ex = [expert(u) for u in range(UNR)]
            tile_tensor(0, 0, None, ex[0], first=True)
            for u in range(1, UNR):
                tile_tensor(0, u, ex[u - 1], ex[u])
            with pe.Fori(1, TILES3 - 1) as it:
                ex = [expert(it * UNR + u - 1) for u in range(UNR + 1)]
                for u in range(UNR):
                    tile_tensor(it, u, ex[u], ex[u + 1])
            ex = [expert(SLOT_TILES - UNR + u - 1) for u in range(UNR + 1)]
            for u in range(UNR):
                tile_tensor(TILES3 - 1, u, ex[u], ex[u + 1], last=(u == UNR - 1))
            down_last = SLOT_TILES - 1
            ht(down_last, UNR - 1)
            down(down_last, UNR - 1, ex[UNR])

        def attention_tensor():
            B = ab
            pe.wait_ge(s_attn_w, 16 * 5)
            pe.wait_ge(s_picks, 2)
            pe.wait_ge(s_zero, 7)

            def wait(k, b, n):
                pe.wait_ge(att[k], b * PER[k] + n)

            def bd(buf, p):
                return buf[:, p * P:(p + 1) * P]

            def turn(b):
                wait("xn", b, GT)
                transposes(B["XN"], 6, att["xt_ready"])

            def front_wide(b, q, slot, alone=False):
                if 4 <= slot < 8:
                    i, c = divmod(slot - 4, KD)
                    if slot == 4:
                        wait("xts", b, KD)
                        if not alone:
                            wait("xo", b - 2, 2)
                    else:
                        wait("qk", b, slot - 4)
                    for k in range(KD):
                        ins = pe.matmul(banks[6][:], (WQ, WK)[i][:, k * D + c * P:k * D + (c + 1) * P], B["XTS"][:, k * GW:(k + 1) * GW],
                                        start=(k == 0), stop=(k == KD - 1))
                    ins.then_inc(att["qk_ready"], 1)
                if slot in (8, 9):
                    wait("qk", b, 4)
                    if slot == 9:
                        wait("v_sb", b, 1)
                    for jj in range(2):
                        j = (slot - 8) * 2 + jj
                        for k in range(KD):
                            ins = pe.matmul(banks[6][:, jj * D:(jj + 1) * D], B["XTS"][:, k * GW + j * P:k * GW + (j + 1) * P],
                                            WV[:, k * D:(k + 1) * D], start=(k == 0), stop=(k == KD - 1))
                    ins.then_inc(att["v_ready"], 1)
                if slot == 10:
                    wait("bd", b, 2)
                    wait("kls", b, 1)
                    wait("v_sb", b, 2)
                    for p in range(PAIRS):
                        c = p // PC
                        ins = pe.matmul(banks[6][:, p * M:(p + 1) * M], bd(B["QBD"][q], p), B["KLS"][:, c * M:(c + 1) * M], start=True, stop=True)
                    ins.then_inc(att["s2_ready"], 1)
                if slot == 14:
                    wait("s2bd", b, 2)
                    for p in range(PAIRS):
                        ins = pe.matmul(banks[6][:, p * M:(p + 1) * M], bd(B["S2BD"], p), const("eye2"), start=True, stop=True)
                    ins.then_inc(att["s2t_ready"], 1)
                if slot == 15:
                    wait("s3m", b, 8)
                    pe.matmul(banks[7][:], const("halves"), B["S2"][:], start=True, stop=True).then_inc(att["col_ready"], 1)
                if slot == 16:
                    wait("s2t", b, 1)
                    pe.matmul(banks[6][:], const("halves"), B["S2T"][:], start=True, stop=True).then_inc(att["row_ready"], 1)

            def s3_max(b, p, alone=False):
                c = p // PC
                if p == 0:
                    if not alone:
                        wait("nm1", b - 1, 1)
                    wait("bdr", b, 1)
                    wait("qkr", b, 4)
                else:
                    wait("s3m", b, p)
                pe.matmul(banks[7][:], bd(B["QBDR"], p), B["KTR"][:, c * GW:(c + 1) * GW], start=True, stop=True).then_inc(att["s3max_ready"], 1)

            def s1_max(b, q, n, first):
                c, j = divmod(n, GT)
                if n == 0:
                    wait("bdr", b, 2)
                    if first:
                        wait("xts", b + 1, KD)
                    else:
                        wait("ot", b - 1, 4)
                else:
                    wait("s1m", b, n)
                pe.matmul(banks[7][:], B["QTR"][q][:, c * GW + j * P:c * GW + (j + 1) * P], B["KBDR"][:, c * 512:(c + 1) * 512],
                          start=True, stop=True).then_inc(att["s1max_ready"], 1)

            def start_y(b):
                wait("s2tbd", b, 2)
                for p in range(PAIRS):
                    ins = pe.matmul(banks[1][:, p * M:(p + 1) * M], bd(B["S2TBD"], p), B["S2T"][:, p * M:(p + 1) * M], start=True, stop=True)
                ins.then_inc(att["y0_ready"], 1)
                wait("s3m", b, 8)
                pe.transpose(banks[2][0:PAIRS, 0:P], B["NM3"][:], ident).then_inc(att["nm3_ready"], 1)

            def s3t(b, q, n, first):
                c, j = divmod(n, GT)
                if n == 0:
                    wait("nm3", b, 1)
                    if not first:
                        wait("ot", b - 1, 2)
                elif n in (4, 5):
                    wait("tt", b, 1)
                elif n != 1:
                    wait("e3", b, n - 1)
                bank = banks[4 + n % 2]
                pe.matmul(bank[:], B["KT"][q][:, c * GW + j * P:c * GW + (j + 1) * P], B["QBD"][q][:, c * 512:(c + 1) * 512], start=True, stop=False)
                pe.matmul(bank[:], B["ONESR"][:], B["NM3BD"][:, c * 512:(c + 1) * 512], start=False, stop=True).then_inc(att["s3t_ready"], 1)

            def pv(b, q, c):
                wait("e3", b, 4 * c + 4)
                for j in range(GT):
                    for a in range(PC):
                        rows = slice(32 * a, 32 * a + 32)
                        e3 = B["E3"][:, j * 512 + a * P:j * 512 + (a + 1) * P]
                        pe.matmul(banks[4][rows, 0:P], B["V"][q][:, j * D + c * P + a * 32:j * D + c * P + (a + 1) * 32], e3,
                                  start=(j == 0), stop=(j == GT - 1))
                    for a in range(PC):
                        rows = slice(32 * a, 32 * a + 32)
                        e3 = B["E3"][:, j * 512 + a * P:j * 512 + (a + 1) * P]
                        ins = pe.matmul(banks[5][rows, 0:P], const("ones")[:, 0:32], e3, start=(j == 0), stop=(j == GT - 1))
                ins.then_inc(att["pv_ready"], 1)

            def pt(b):
                wait("tt", b, 2)
                for c in range(KD):
                    pe.transpose(banks[4 + c][:, 0:P], B["TT"][:, c * P:(c + 1) * P], ident).then_inc(att["pt_ready"], 1)

            def s1t(b, q, p):
                c = p // PC
                if p == 0:
                    wait("nm1", b, 1)
                if p < 2:
                    wait("tm", b, p + 1)
                else:
                    wait("e1", b, p - 1)
                bank = banks[4 + p % 2]
                pe.matmul(bank[:], bd(B["KBD"][q], p), B["QT"][q][:, c * GW:(c + 1) * GW], start=True, stop=False)
                pe.matmul(bank[:], bd(B["PICK"], p), B["NM1T"][:], start=False, stop=True).then_inc(att["s1t_ready"], 1)

            def heads(b, c):
                num, den = ((banks[4], banks[5]), (banks[6], banks[7]))[c]
                for a in range(PC):
                    p = c * PC + a
                    pe.matmul(num[32 * a:32 * a + 32, :], B["WS"][:, p * 32:(p + 1) * 32], B["E1"][:, p * GW:(p + 1) * GW], start=True, stop=True)
                for a in range(PC):
                    p = c * PC + a
                    ins = pe.matmul(den[32 * a:32 * a + 32, :], const("pair_cols"), B["E1"][:, p * GW:(p + 1) * GW], start=True, stop=True)
                ins.then_inc(att["o_ready"], 1)

            def project(b, jj):
                if jj == 0:
                    wait("ot", b, 4)
                else:
                    wait("xo", b, 1)
                for i in range(2):
                    j = jj * 2 + i
                    for c in range(KD):
                        ins = pe.matmul(banks[6][:, i * D:(i + 1) * D], B["OT"][:, c * GW + j * P:c * GW + (j + 1) * P],
                                        WO[:, c * D:(c + 1) * D], start=(c == 0), stop=(c == KD - 1))
                ins.then_inc(att["pr_ready"], 1)

            def back(b, q, slot, first):
                if slot < 4:
                    s3t(b, q, slot, first)
                elif slot == 4:
                    pv(b, q, 0)
                elif slot < 9:
                    s3t(b, q, slot - 1, first)
                elif slot == 9:
                    pv(b, q, 1)
                elif slot == 10:
                    pt(b)
                else:
                    s1t(b, q, slot - 11)

            def front_alone():
                turn(0)
                for slot in range(3 * PINV_ITERS):
                    front_wide(0, 0, slot, alone=True)
                    if 11 <= slot < 15:
                        for i in range(2):
                            s3_max(0, 2 * (slot - 11) + i, alone=True)
                wait("rs", 0, 1)
                turn(1)
                start_y(0)

            def batch(b, q, first, last):
                def step(slot):
                    if slot in (2, 3) and not first:
                        project(b - 1, slot - 2)
                    if not last:
                        front_wide(b + 1, 1 - q, slot, alone=first)
                        if 11 <= slot < 15:
                            s3_max(b + 1, 2 * (slot - 11))
                    if 2 <= slot < 10:
                        s1_max(b, q, slot - 2, first)
                    if slot == 10:
                        wait("s1m", b, 8)
                        for j in range(GT):
                            ins = pe.transpose(banks[7][0:H, j * P:(j + 1) * P], B["NM1"][:, j * H:(j + 1) * H], ident)
                        ins.then_inc(att["nm1_ready"], 1)
                    back(b, q, slot, first)
                    if not last and 11 <= slot < 15:
                        s3_max(b + 1, 2 * (slot - 11) + 1)

                for it in range(PINV_ITERS):
                    wait("b1", b, it + 1)
                    wait("ybd0", b, it + 1)
                    wait("ybd1", b, it + 1)
                    for p in range(PAIRS):
                        ins = pe.matmul(banks[0][:, p * M:(p + 1) * M], bd(B["YBD"], p), B["B1"][:, p * M:(p + 1) * M], start=True, stop=True)
                    ins.then_inc(att["m1"], 1)
                    step(3 * it)
                    wait("b2", b, it + 1)
                    for p in range(PAIRS):
                        ins = pe.matmul(banks[1][:, p * M:(p + 1) * M], bd(B["YBD"], p), B["B1"][:, p * M:(p + 1) * M], start=True, stop=True)
                    ins.then_inc(att["m2"], 1)
                    step(3 * it + 1)
                    wait("qb", b, 2 * it + 2)
                    if it == 0:
                        wait("zt", b, 1)
                        wait("nm3", b, 1)
                    for p in range(PAIRS):
                        ins = pe.matmul(banks[2 + p // PC][:, (p % PC) * P:(p % PC + 1) * P], bd(B["QB"], p), bd(B["YZ"], p), start=True, stop=True)
                    ins.then_inc(att["m3"], 1)
                    step(3 * it + 2)
                s1t(b, q, PAIRS - 1)
                wait("zbd", b, 4)
                wait("tm", b, 2)
                for p in range(PAIRS):
                    ins = pe.matmul(banks[0][:, p * 32:(p + 1) * 32], bd(B["YBD"], p), B["TM"][:, p * 32:(p + 1) * 32], start=True, stop=True)
                ins.then_inc(att["w_ready"], 1)
                if not last:
                    wait("rs", b + 1, 1)
                    turn(b + 2)
                wait("ws", b, 1)
                wait("e1", b, 8)
                heads(b, 0)
                if not last:
                    start_y(b + 1)
                    wait("xts", b + 2, KD)
                heads(b, 1)
                if last:
                    project(b, 0)
                    project(b, 1)

            over_batches(pe, front_alone, batch)

        ffn_tensor(0)
        attention_tensor()
        ffn_tensor(1)


def kernel(L0_attn_x, L0_attn_Wk, L0_attn_Wq, L0_attn_Wv, L0_attn_Wo, L0_attn_bo, L0_ffn_gate_w, L0_ffn_shared_gate, L0_ffn_shared_up,
           L0_ffn_shared_down, L0_ffn_r_gate, L0_ffn_r_up, L0_ffn_r_down):
    import numpy as _np
    import concourse.bacc as _bacc
    from concourse import mybir as _mybir
    from concourse.bass_utils import run_bass_kernel_spmd as _run

    def rows(w):
        w = _np.asarray(w)
        *lead, k, n = w.shape
        w = w.reshape(*lead, k // P, P, n)
        return _np.ascontiguousarray(_np.moveaxis(w, -2, 0).reshape(P, -1))

    def turned(w):
        return rows(_np.swapaxes(_np.asarray(w), -1, -2))

    arrays = {
        "x": _np.ascontiguousarray(L0_attn_x), "wq": rows(L0_attn_Wq), "wk": rows(L0_attn_Wk), "wv": rows(L0_attn_Wv), "wo": rows(L0_attn_Wo),
        "bo": _np.ascontiguousarray(_np.broadcast_to(_np.asarray(L0_attn_bo), (P, D))), "gate_w": turned(L0_ffn_gate_w),
        "sh_gate": turned(L0_ffn_shared_gate), "sh_up": turned(L0_ffn_shared_up), "sh_down": turned(L0_ffn_shared_down),
        "r_gate": turned(L0_ffn_r_gate), "r_up": turned(L0_ffn_r_up), "r_down": turned(L0_ffn_r_down), "consts": constants(),
    }
    nc = _bacc.Bacc("TRN2", target_bir_lowering=False, num_devices=1)
    args = [nc.dram_tensor(f"in_{n}", a.shape, _mybir.dt.from_np(a.dtype), kind="ExternalInput").ap() for n, a in arrays.items()]
    args.append(nc.dram_tensor("out_0", tuple(L0_attn_x.shape), _mybir.dt.float32, kind="ExternalOutput").ap())
    macaron_kernel(nc, *args)
    r = _run(nc, [{f"in_{n}": a for n, a in arrays.items()}], core_ids=[0])
    return r.results[0]["out_0"]
```

```python
from contextlib import ExitStack

import numpy as np

import concourse.bass as bass
from concourse import mybir

ALU = mybir.AluOpType
ACT = mybir.ActivationFunctionType
AX_X = mybir.AxisListType.X
F32 = mybir.dt.float32
F32R = mybir.dt.float32r
I32 = mybir.dt.int32

P = 128
D = 256
KD = D // P
T = 4096
NT = T // P
GT = 4
NG = NT // GT
GW = GT * P
F = 512
KF = F // P
E = 8
QUAD = 32
QG = P // QUAD
SLOT_TILES = (T + E * (P - 1)) // P
UNR = 3
assert SLOT_TILES % UNR == 0
NOBODY = 2 * T
H = 16
HS = D // H
M = 64
LM = GW // M
PAIRS = H // 2
HC = P // HS
PC = PAIRS // KD
PINV_ITERS = 6
EPS = 1e-5

CONSTS = [("ident", P), ("before", P), ("ones", P), ("halves", P), ("eye2", M), ("head_rows", HC), ("pair_cols", 2 * HS),
          ("expert_rank", E), ("tile_edges", NT), ("tile_no", SLOT_TILES), ("token_no", NT), ("eps", 1)]
CONST_AT = {}
_at = 0
for _n, _w in CONSTS:
    CONST_AT[_n] = (_at, _w)
    _at += _w
CONST_W = _at


def constants():
    c = {n: np.zeros((P, w), np.float32) for n, w in CONSTS}
    c["ident"][:] = np.eye(P)
    c["before"][:] = np.triu(np.ones((P, P)), 1)
    c["ones"][:] = 1
    c["halves"][:] = np.kron(np.eye(2), np.ones((M, M)))
    c["eye2"][:] = np.tile(np.eye(M), (2, 1))
    c["head_rows"][:] = np.kron(np.eye(HC), np.ones((HS, 1)))
    c["pair_cols"][:] = np.kron(np.eye(2), np.ones((M, HS)))
    c["expert_rank"][:] = E - np.arange(E)
    c["tile_edges"][:] = P * np.arange(NT)
    c["tile_no"][:] = np.arange(SLOT_TILES)
    c["token_no"][:] = np.arange(P)[:, None] + P * np.arange(NT)
    c["eps"][:] = EPS
    return np.concatenate([c[n] for n, _ in CONSTS], 1)


def macaron_kernel(nc, x, wq, wk, wv, wo, bo, gate_w, sh_gate, sh_up, sh_down, r_gate, r_up, r_down, consts, out):
    with ExitStack() as top:
        emit(nc, top, x, wq, wk, wv, wo, bo, gate_w, sh_gate, sh_up, sh_down, r_gate, r_up, r_down, consts, out)


def emit(nc, top, x, wq, wk, wv, wo, bo, gate_w, sh_gate, sh_up, sh_down, r_gate, r_up, r_down, consts, out):
    def sb(name, shape, dt=F32, ctx=top):
        return ctx.enter_context(nc.sbuf_tensor(name, shape, dt))

    def sem(name):
        return top.enter_context(nc.semaphore(name))

    banks = [top.enter_context(nc.psum_tensor(f"bank{i}", [P, 512], F32)) for i in range(8)]

    with ExitStack() as shared_with_x:
        PARTS_G = 6
        assert PARTS_G * GT * D == 6 * KD * F
        WHL = [sb(f"WHL{i}", [P, KD * F], F32R, shared_with_x) for i in range(6)]
    X = sb("X", [P, (NT + GT) * D])
    CB = sb("CB", [P, CONST_W])
    SGH, SGL, SUH, SUL = (sb(name, [P, KD * F], F32R) for name in ("SGH", "SGL", "SUH", "SUL"))
    SDN = sb("SDN", [P, KF * D])
    GWT = sb("GWT", [P, KD * QUAD])
    with ExitStack() as shared_with_xnt:
        XGH, XGL = (sb(name, [P, UNR * D], F32R, shared_with_xnt) for name in ("XGH", "XGL"))
    XNT = sb("XNT", [P, KD * T])
    ROUTED_W = 2 * UNR * D + 3 * UNR * F
    ATT_W = XNT[:, ROUTED_W:ROUTED_W + 4 * KD * D]
    WQ, WK, WV, WO = (ATT_W[:, i * KD * D:(i + 1) * KD * D] for i in range(4))
    BO = sb("BO", [P, D])
    STATS = sb("STATS", [P, GT * 6])
    AGG = sb("AGG", [P, GT * 2])
    MV = sb("MV", [P, NT * 2])
    RSTD = sb("RSTD", [P, NT])

    def const(name, rows=P):
        a, w = CONST_AT[name]
        return CB[0:rows, a:a + w]

    xs_dram = nc.dram_tensor("xs_dram", [T, D], F32, kind="Internal").ap()
    shared_dram = nc.dram_tensor("shared_dram", [T, D], F32, kind="Internal").ap()
    mid_dram = nc.dram_tensor("mid_dram", [T, D], F32, kind="Internal").ap()
    who_dram = [nc.dram_tensor(f"who_dram{i}", [SLOT_TILES * P, 1], I32, kind="Internal").ap() for i in range(2)]

    x_rows = x.rearrange("b (j p) d -> p (b j) d", p=P)
    out_flat = out.rearrange("b l d -> (b l) d")
    xs_rows = xs_dram.rearrange("(t p) d -> p t d", p=P)
    shared_rows = shared_dram.rearrange("(t p) d -> p t d", p=P)
    mid_rows = mid_dram.rearrange("(t p) d -> p t d", p=P)
    mvv = MV[:].rearrange("p (t c) -> p t c", c=2)
    X3 = X[:].rearrange("p (t d) -> p t d", d=D)

    s_x = [sem(f"x_loaded{i}") for i in range(4)]
    s_const = sem("consts_loaded")
    s_gate = sem("gate_loaded")
    s_gate_pad = sem("gate_padded")
    s_shared = sem("shared_loaded")
    s_split_hi = sem("shared_high_parts")
    s_split_lo = sem("shared_low_parts")
    s_attn_w = sem("attention_weights_loaded")
    s_pool_past = sem("pool_past_a_wait")
    s_dve_past = sem("dve_past_a_wait")
    s_pe_past = sem("pe_past_a_wait")

    TILES3 = SLOT_TILES // UNR
    FFN_PER = dict(stat=NT, agg=NT, mv=NG, sd=NG, rstd=NG, xn=NT, xt_ready=NG, xt_sb=KD * NG, lg_ready=NG, lgt_sb=NG // QG, logits=NG // QG, mx=1, onehot_step=3, oh=1,
                   score=1, rs_step=1, rs=1, xs=NT, xs_out=16 * NG, cnt_ready=2, rt=23, slots=2, expert_of=1, nobody=1, who_init=16,
                   who=16 * NT, who_sb=16, gu=KF * NG, silu=KF * NG, h=KF * NG, y_ready=NG, x_new=2 * NG, gath0=16 * TILES3, gath1=16 * TILES3,
                   gath2=16 * TILES3, xg_t=SLOT_TILES, xgt=SLOT_TILES, xgl=SLOT_TILES, whi=2 * SLOT_TILES, wlo=2 * SLOT_TILES, xh=NG, xl=NG, rg=SLOT_TILES, ru=SLOT_TILES, rsilu=SLOT_TILES, rh=SLOT_TILES, ht_ready=SLOT_TILES,
                   ht_sb=SLOT_TILES, ry_ready=SLOT_TILES, ry=SLOT_TILES, ry_out0=16 * TILES3, ry_out1=16 * TILES3, ry_out2=16 * TILES3, wg=16, wu=16, wd=32,
                   xs_raw=3 * NG, x_out=16 * PARTS_G, x_out_last=16 * (NG - PARTS_G), ry_clear=1, res_in0=16 * TILES3, res_in1=16 * TILES3, res_in2=16 * TILES3, sidx=2 * NG, gidx=SLOT_TILES, yidx=SLOT_TILES)
    s = {k: sem(f"ffn_{k}") for k in FFN_PER}
    GIVEN = {"xs_out", "h", "x_new", "ry"}
    res = {k: sem(f"res_{k}") for k in ("x_in", "stat", "agg", "sd", "rstd")}

    PER = dict(xn=4, xt_ready=1, xts=2, qk_ready=4, qk=4, qkr=4, v_ready=2, v_sb=2, lm=4, kls=1, bd=4, bdr=2, xbo=1,
               s2_ready=1, s2m=1, s2s=1, s2e=1, s2sum=1, s2rc=1, s2n=1, s3max_ready=8, s3m=8, s2t_ready=1, s2t=2,
               col_ready=1, row_ready=1, cs=1, rs=1, prod=1, r8=1, zt=1, s1max_ready=8, s1m=8, y0_ready=1, y=2, b1=PINV_ITERS,
               nm1_ready=1, nm3=PAIRS, nm1=1, m1=PINV_ITERS, b2=2 * PINV_ITERS, m2=PINV_ITERS, qb=2 * PINV_ITERS,
               m3=PINV_ITERS, yz=2 * (PINV_ITERS - 1), zw=2, s3t_ready=8, e3=8, pv_ready=2, trc=2, tt=2, pt_ready=2, tm=2,
               s1t_ready=8, e1=8, w_ready=1, ws=2, o_ready=2, orc=4, ot=4, pr_ready=2, xo=2)
    att = {k: sem(f"att_{k}") for k in PER}
    s_picks = sem("att_picks")
    s_zero = sem("att_zeroed")

    def ffn_buffers(ctx, n):
        def b(name, cols, dt=F32):
            return sb(f"{name}_{n}", [P, cols], dt, ctx)
        with ExitStack() as shared_with_wd:
            XHL = [sb(f"XHL{i}_{n}", [P, KD * GW], F32R, shared_with_wd) for i in range(4)]
        B = dict(WD=b("WD", E * KF * D), WG=b("WG", E * KD * F), WU=b("WU", E * KD * F), HB=b("HB", KF * GW), HSB=b("HSB", 2 * F),
                 OH=b("OH", NT * E),
                 MX=b("MX", NT), SCORE=b("SCORE", NT), RSC=b("RSC", NT), NMR=b("NMR", NT), VM=b("VM", NT), CNT=b("CNT", 3 * E),
                 SLOTF=b("SLOTF", NT), SLOT=b("SLOT", NT, I32), RS4=b("RS4", GT), NM4=b("NM4", GT), SIDX=b("SIDX", GT, I32), STOK=b("STOK", GT, I32), GIDX=b("GIDX", UNR, I32), YIDX=b("YIDX", UNR, I32),
                 STILE=b("STILE", NT, I32), SROW=b("SROW", NT, I32), TOK=b("TOK", NT, I32), EXF=b("EXF", SLOT_TILES),
                 EXPERT=b("EXPERT", SLOT_TILES, I32), WHO=b("WHO", SLOT_TILES, I32))
        B["XNT"], B["XS"] = XNT, X[:, NT * D:]
        B["XHL"] = XHL
        B["XN"] = (B["HB"][:, 0:GT * D], B["HB"][:, GT * D:2 * GT * D])
        at = E // 2 * KF * D
        for name, cols in (("RT1", NT * E), ("RT2", SLOT_TILES * E), ("RT3", NT * E), ("LGT0", GW), ("LGT1", GW)):
            B[name] = B["WD"][:, at:at + cols]
            at += cols
        at = 2 * UNR * D
        for name, cols in (("RS", UNR * F), ("RH", UNR * F), ("HT", UNR * F)):
            B[name] = B["XNT"][:, at:at + cols]
            at += cols
        assert at <= ROUTED_W
        B["RY"] = B["HSB"][:, 0:UNR * D]
        return B

    def attention_buffers(ctx):
        def b(name, cols, dt=F32):
            return sb(f"A_{name}", [P, cols], dt, ctx)
        B = {}
        for name, cols in (("XN", GT * D), ("XTS", KD * GW), ("QL", KD * M), ("KL", KD * M), ("KLS", KD * M),
                           ("NM1", GT * H), ("NM3", PAIRS), ("S2", 512), ("S2T", 512), ("YZ", PAIRS * P), ("ZW", PAIRS * M), ("QB", PAIRS * P),
                           ("B1", 512), ("SM", 6 * PAIRS), ("TT", KD * P), ("TM", PAIRS * 2 * HS), ("WS", PAIRS * 2 * HS), ("OT", KD * GW), ("LNR", GT)):
            B[name] = b(name, cols)
        for name, cols in (("KTR", KD * GW), ("QBDR", KD * 512), ("KBDR", KD * 512), ("NM1T", GW), ("NM3BD", PAIRS * P), ("ONESR", P),
                           ("PICK", PAIRS * P)):
            B[name] = b(name, cols, F32R)
        B["E1"], B["E3"] = XNT[:, 0:PAIRS * GW], XNT[:, PAIRS * GW:PAIRS * GW + GT * 512]
        assert PAIRS * GW + GT * 512 <= ROUTED_W
        for name, cols, dt in (("QT", KD * GW, F32), ("KT", KD * GW, F32), ("V", GT * D, F32), ("QBD", KD * 512, F32), ("KBD", KD * 512, F32),
                               ("QTR", KD * GW, F32R)):
            B[name] = [b(f"{name}{q}", cols, dt) for q in range(2)]
        return B

    with ExitStack() as ctx:
        fb0 = ffn_buffers(ctx, 0)
    with ExitStack() as ctx:
        ab = attention_buffers(ctx)
    with ExitStack() as ctx:
        fb1 = ffn_buffers(ctx, 1)
    fbs = [fb0, fb1]
    SG, SU = (fb0["WU"][:, i * KD * F:(i + 1) * KD * F] for i in range(2))

    def over_batches(eng, front_alone, batch):
        front_alone()
        batch(0, 0, True, False)
        with eng.Fori(0, (NG - 2) // 2) as i:
            for u in range(2):
                batch(i * 2 + 1 + u, 1 - u, False, False)
        batch(NG - 1, (NG - 1) % 2, False, True)

    def front_bank(slot, alone):
        return {4: 4, 5: 5, 6: 6, 7: 7, 8: 0, 12: 1, 10: 2, COLUMNS: 1, 16: 3}[slot] if alone else 7 if slot == COLUMNS else 6

    HALF = [slice(0, M), slice(M, P)]

    def turned_banks(alone):
        return (0, 1) if alone else (6, 7)

    FFN_STATS_SLOT = 4
    COLUMNS = 17

    def max_bank(p, alone):
        return 4 + p % 4 if alone else 6 if p in (1, 4, 6) else 7

    S3_MAX = {11: (0, 1), 12: (2,), 13: (3, 4), 15: (5, 6), 16: (7,)}

    block = top.enter_context(nc.Block())

    @block.sync
    def _(sp):
        for i in range(4):
            n = NT // 4
            sp.dma_start(X3[:, i * n:(i + 1) * n, :], x_rows[:, i * n:(i + 1) * n, :]).then_inc(s_x[i], 16)
            if i == 0:
                sp.dma_start(CB[:], consts).then_inc(s_const, 16)
                sp.dma_start(GWT[:].rearrange("p (k e) -> p k e", k=KD)[:, :, 0:E], gate_w.rearrange("p (k e) -> p k e", k=KD)).then_inc(s_gate, 16)
        for buf, src in ((SG, sh_gate), (SU, sh_up), (SDN[:], sh_down)):
            sp.dma_start(buf, src).then_inc(s_shared, 16)
        sp.dma_start(BO[:], bo).then_inc(s_attn_w, 16)

        def ffn_dma(n):
            B = fbs[n]

            def need(eng, k, v):
                eng.wait_ge(s[k], n * FFN_PER[k] + (k in GIVEN) + v)

            if n == 1:
                sp.wait_ge(att["xo"], PER["xo"] * NG)
            sp.dma_start(B["WG"][:], r_gate).then_inc(s["wg"], 16)
            if n == 0:
                sp.wait_ge(s_split_lo, 2)
            sp.dma_start(B["WU"][:], r_up).then_inc(s["wu"], 16)
            need(sp, "nobody", 1)
            sp.dma_start(who_dram[n].rearrange("(p t) o -> p (t o)", p=P), B["WHO"][:]).then_inc(s["who_init"], 16)
            with sp.Fori(0, NG) as g:
                need(sp, "xs", g * GT + GT)
                sp.dma_start(xs_rows[:, bass.ds(g * GT, GT), :], B["XS"].rearrange("p (t d) -> p t d", d=D)).then_inc(s["xs_out"], 16)
            need(sp, "expert_of", 1)
            half = E // 2 * KF * D
            sp.dma_start(B["WD"][:, half:], r_down[:, half:]).then_inc(s["wd"], 16)
            def store(g, k):
                need(sp, "x_new", g * 2 + 2)
                sp.dma_start(shared_rows[:, bass.ds(g * GT, GT), :], X3[:, bass.ds(g * GT, GT), :]).then_inc(s[k], 16)

            with sp.Fori(0, PARTS_G - 1) as g:
                store(g, "x_out")
            need(sp, "who", 16 * NT)
            sp.dma_start(B["WHO"][:], who_dram[n].rearrange("(p t) o -> p (t o)", p=P)).then_inc(s["who_sb"], 16)
            store(PARTS_G - 1, "x_out")
            for g in range(PARTS_G, NG - 1):
                store(g, "x_out_last")
            need(sp, "gu", KF * NG)
            sp.dma_start(B["WD"][:, 0:half], r_down[:, 0:half]).then_inc(s["wd"], 16)
            store(NG - 1, "x_out_last")
            if n == 0:
                for buf, src in ((WQ, wq), (WK, wk), (WV, wv), (WO, wo)):
                    sp.dma_start(buf, src).then_inc(s_attn_w, 16)

        def load_residual():
            for u in range(UNR):
                sp.wait_ge(s[f"ry_out{u}"], FFN_PER[f"ry_out{u}"])

            def load(g):
                sp.dma_start(X3[:, bass.ds(g * GT, GT), :], mid_rows[:, bass.ds(g * GT, GT), :]).then_inc(res["x_in"], 16)

            load(0)
            with sp.Fori(1, NG) as g:
                sp.wait_ge(res["x_in"], g * 16)
                load(g)

        ffn_dma(0)
        load_residual()
        ffn_dma(1)

    @block.vector
    def _(dve):
        def wait_alone(semaphore, v):
            dve.wait_ge(semaphore, v)
            dve.sem_inc(s_dve_past, 1)

        def stats(q, g, n=0):
            for j in range(GT):
                dve.bn_stats(STATS[:, j * 6:(j + 1) * 6], X[:, bass.ds(g * GT * D + j * D, D)]).then_inc(q["stat"], 1)
            wait_alone(q["stat"], g * GT + n * NT + GT)
            for j in range(GT):
                dve.bn_aggr(AGG[:, j * 2:(j + 1) * 2], STATS[:, j * 6:(j + 1) * 6]).then_inc(q["agg"], 1)
            dve.wait_ge(q["agg"], g * GT + n * NT + GT)
            dve.tensor_copy(MV[:, bass.ds(g * GT * 2, GT * 2)], AGG[:]).then_inc(q["mv"], 1)

        def rstd(q, g, n=0):
            dve.wait_ge(q["sd"], n * NG + g + 1)
            dve.reciprocal(RSTD[:, bass.ds(g * GT, GT)], RSTD[:, bass.ds(g * GT, GT)]).then_inc(q["rstd"], 1)
            wait_alone(q["rstd"], n * NG + g + 1)

        def normalise(dst, g, sem_xn):
            for j in range(GT):
                dve.tensor_scalar(dst[:, j * D:(j + 1) * D], X[:, bass.ds(g * GT * D + j * D, D)], MV[:, bass.ds(g * GT * 2 + j * 2, 1)],
                                  RSTD[:, bass.ds(g * GT + j, 1)], ALU.subtract, ALU.mult).then_inc(sem_xn, 1)

        def ffn_vector(n):
            B = fbs[n]

            def need(eng, k, v):
                eng.wait_ge(s[k], n * FFN_PER[k] + (k in GIVEN) + v)

            dve.memset(B["WHO"][:], NOBODY).then_inc(s["nobody"], 1)

            def spread(g):
                for j in range(GT):
                    dve.bn_stats(STATS[:, j * 6:(j + 1) * 6], X[:, bass.ds(g * GT * D + j * D, D)]).then_inc(s["stat"], 1)

            def mean_variance(g):
                wait_alone(s["stat"], g * GT + n * NT + GT)
                for j in range(GT):
                    dve.bn_aggr(AGG[:, j * 2:(j + 1) * 2], STATS[:, j * 6:(j + 1) * 6]).then_inc(s["agg"], 1)

            def keep_mean_variance(g):
                wait_alone(s["agg"], g * GT + n * NT + GT)
                dve.tensor_copy(MV[:, bass.ds(g * GT * 2, GT * 2)], AGG[:]).then_inc(s["mv"], 1)

            def normalise_group(g, u, first=False, last=False):
                if not last:
                    spread(g + 1)
                wait_alone(s["sd"], n * NG + g + 1)
                dve.reciprocal(RSTD[:, bass.ds(g * GT, GT)], RSTD[:, bass.ds(g * GT, GT)]).then_inc(s["rstd"], 1)
                if not last:
                    mean_variance(g + 1)
                wait_alone(s["rstd"], n * NG + g + 1)
                if not first:
                    need(dve, "xt_ready", g - 1)
                normalise(B["XN"][u], g, s["xn"])
                if not last:
                    keep_mean_variance(g + 1)

            def normalise_known(g, u, first=False):
                rstd(s, g, n)
                if not first:
                    need(dve, "xt_ready", g - 1)
                normalise(B["XN"][u], g, s["xn"])

            if n == 0:
                dve.memset(GWT[:].rearrange("p (k e) -> p k e", k=KD)[:, :, E:], 0.0).then_inc(s_gate_pad, 1)
                dve.wait_ge(s_x[0], 16)
                spread(0)
                mean_variance(0)
                keep_mean_variance(0)
                for g in range(NG):
                    if g % 2 and g < NG - 1:
                        dve.wait_ge(s_x[(g + 1) // 2], 16)
                    normalise_group(g, g % 2, first=g < 2, last=g == NG - 1)
            else:
                normalise_known(0, 0, first=True)
                normalise_known(1, 1, first=True)
                stats(s, NG - 1, n)
                with dve.Fori(1, NG // 2) as i:
                    for u in range(2):
                        normalise_known(i * 2 + u, u)

            def low_tokens(g, u):
                need(dve, "xh", g + 1)
                dve.tensor_tensor(B["XHL"][2 * u + 1][:].rearrange("p (k t) -> p k t", k=KD), tokens(g),
                                  B["XHL"][2 * u][:].bitcast(F32).rearrange("p (k t) -> p k t", k=KD), ALU.subtract).then_inc(s["xl"], 1)

            def tokens(g):
                return XNT[:].rearrange("p (k t) -> p k t", k=KD)[:, :, bass.ds(g * GW, GW)]

            low_tokens(0, 0)

            oh3 = B["OH"][:].rearrange("p (t e) -> p t e", e=E)
            rt1, rt3 = (B[k][:].rearrange("p (t e) -> p t e", e=E) for k in ("RT1", "RT3"))
            logits = banks[2][:, 0:NT * E].rearrange("p (t e) -> p t e", e=E)

            def over_e(ap):
                return ap.unsqueeze(2).broadcast_to([P, NT, E])

            def over_t(ap):
                return ap.unsqueeze(1).broadcast_to([P, NT, E])

            need(dve, "logits", NG // QG)
            dve.tensor_reduce(B["MX"][:], logits, AX_X, ALU.max).then_inc(s["mx"], 1)
            need(dve, "mx", 1)
            dve.tensor_tensor(rt1, logits, over_e(B["MX"][:]), ALU.is_equal).then_inc(s["onehot_step"], 1)
            need(dve, "onehot_step", 1)
            dve.tensor_tensor(rt3, rt1, over_t(const("expert_rank")), ALU.mult).then_inc(s["onehot_step"], 1)
            need(dve, "onehot_step", 2)
            dve.tensor_reduce(B["VM"][:], rt3, AX_X, ALU.max).then_inc(s["onehot_step"], 1)
            need(dve, "onehot_step", 3)
            dve.tensor_tensor(oh3, rt3, over_e(B["VM"][:]), ALU.is_equal).then_inc(s["oh"], 1)
            need(dve, "score", 1)
            dve.tensor_tensor(B["RSC"][:], RSTD[:], B["SCORE"][:], ALU.mult).then_inc(s["rs_step"], 1)
            need(dve, "rs_step", 1)
            dve.scalar_tensor_tensor(B["NMR"][:], mvv[:, :, 0], -1.0, B["RSC"][:], ALU.mult, ALU.mult).then_inc(s["rs"], 1)

            step = [0]

            def then(ins):
                step[0] += 1
                ins.then_inc(s["rt"], 1)
                need(dve, "rt", step[0])

            incl = B["RT2"][:, 0:NT * E].rearrange("p (t e) -> p t e", e=E)
            total = B["RT2"][:, (NT - 1) * E:NT * E]
            tiles, ends, starts = (B["CNT"][:, i * E:(i + 1) * E] for i in range(3))

            def count_tokens():
                need(dve, "cnt_ready", 2)
                then(dve.tensor_copy(B["RT1"][:], banks[4][:, 0:NT * E]))
                for e in range(E):
                    ins = dve.tensor_tensor_scan(incl[:, :, e], const("ones")[:, 0:NT], rt1[:, :, e], 0.0, ALU.mult, ALU.add)
                    if e < E - 1:
                        step[0] += 1
                        ins.then_inc(s["rt"], 1)
                then(ins)
                then(dve.tensor_tensor(rt1, incl, rt1, ALU.subtract))

            def count_tiles():
                more = B["RT3"][:].rearrange("p (e k) -> p e k", k=NT)
                then(dve.tensor_tensor(more, total.unsqueeze(2).broadcast_to([P, E, NT]),
                                       const("tile_edges").unsqueeze(1).broadcast_to([P, E, NT]), ALU.is_gt))
                then(dve.tensor_reduce(tiles, more, AX_X, ALU.add))
                then(dve.tensor_tensor_scan(ends, const("ones")[:, 0:E], tiles, 0.0, ALU.mult, ALU.add))
                then(dve.tensor_tensor(starts, ends, tiles, ALU.subtract))
                then(dve.tensor_tensor(rt1, banks[3][:, 0:NT * E].rearrange("p (t e) -> p t e", e=E), rt1, ALU.add))
                then(dve.scalar_tensor_tensor(rt1, over_t(starts), float(P), rt1, ALU.mult, ALU.add))

            def find_slots():
                then(dve.tensor_tensor(rt1, rt1, oh3, ALU.mult))
                then(dve.tensor_reduce(B["SLOTF"][:], rt1, AX_X, ALU.add))
                dve.tensor_copy(B["TOK"][:], const("token_no")).then_inc(s["slots"], 1)
                then(dve.tensor_copy(B["SLOT"][:], B["SLOTF"][:]))
                then(dve.tensor_scalar(B["STILE"][:], B["SLOT"][:], P.bit_length() - 1, None, ALU.arith_shift_right))
                then(dve.tensor_scalar(B["SROW"][:], B["SLOT"][:], P - 1, None, ALU.bitwise_and))
                dve.scalar_tensor_tensor(B["SLOT"][:], B["SROW"][:], float(SLOT_TILES), B["STILE"][:], ALU.mult, ALU.add).then_inc(s["slots"], 1)

            def find_experts():
                past = B["RT2"][:].rearrange("p (t e) -> p t e", e=E)
                then(dve.tensor_tensor(past, ends.unsqueeze(1).broadcast_to([P, SLOT_TILES, E]),
                                       const("tile_no").unsqueeze(2).broadcast_to([P, SLOT_TILES, E]), ALU.is_le))
                then(dve.tensor_reduce(B["EXF"][:], past, AX_X, ALU.add))
                dve.tensor_scalar(B["EXPERT"][:], B["EXF"][:], float(E - 1), None, ALU.min).then_inc(s["expert_of"], 1)

            def shared_group(g, u, first=False, last=False):
                for f in range(KF):
                    need(dve, "silu", g * KF + f + 1)
                    dve.tensor_tensor(B["HB"][:, f * GW:(f + 1) * GW], B["HSB"][:, (f % 2) * F:(f % 2 + 1) * F], banks[5 + f % 2][:],
                                      ALU.mult).then_inc(s["h"], 1)
                    if f == 1 and not last:
                        low_tokens(g + 1, 1 - u)
                    if first:
                        if f == 0:
                            count_tokens()
                        elif f == 1:
                            count_tiles()
                        elif f == 2:
                            find_slots()
                        else:
                            find_experts()
                need(dve, "y_ready", g + 1)
                need(dve, "xs", g * GT + GT)
                for jj in range(2):
                    xg = X[:, bass.ds(g * GT * D + jj * 2 * D, 2 * D)]
                    dve.scalar_tensor_tensor(xg, banks[7 if jj == 0 else 2][:], 0.5, xg, ALU.mult, ALU.add).then_inc(s["x_new"], 1)

            shared_group(0, 0, first=True)
            assert step[0] == FFN_PER["rt"]
            shared_group(1, 1)
            with dve.Fori(1, NG // 2 - 1) as i:
                for u in range(2):
                    shared_group(i * 2 + u, u)
            shared_group(NG - 2, 0)

            def low_weights(w, ex, i, slot):
                need(dve, "whi", i + 1)
                dve.tensor_tensor(WHL[2 * slot + 1][:], B[w][:, bass.ds(ex * (KD * F), KD * F)], WHL[2 * slot][:].bitcast(F32),
                                  ALU.subtract).then_inc(s["wlo"], 1)

            def expert(t):
                return dve.value_load(B["EXPERT"][0:1, bass.ds(t, 1)], min_val=0, max_val=E - 1)

            need(dve, "wg", 16)
            need(dve, "wu", 16)
            ex = [expert(u) for u in range(2)]
            low_weights("WG", ex[0], 0, 0)
            low_weights("WU", ex[0], 1, 1)
            low_weights("WG", ex[1], 2, 2)
            shared_group(NG - 1, 1, last=True)

            dve.memset(B["RY"][:], 0.0).then_inc(s["ry_clear"], 1)

            def low_tile(t, u):
                need(dve, "xgt", t + 1)
                part = slice(u * D, (u + 1) * D)
                dve.tensor_tensor(XGL[:, part], banks[0][:, 0:D], XGH[:, part].bitcast(F32), ALU.subtract).then_inc(s["xgl"], 1)

            def tile_vector(it, u, ex, first=False, ahead=2):
                t = it * UNR + u
                need(dve, "rsilu", t + 1)
                need(dve, "ru", t + 1)
                dve.tensor_tensor(B["RH"][:, u * F:(u + 1) * F], B["RS"][:, u * F:(u + 1) * F], banks[3 + u][:],
                                  ALU.mult).then_inc(s["rh"], 1)
                if ahead >= 1:
                    low_tile(t + 1, (u + 1) % UNR)
                    low_weights("WU", ex[u + 1], 2 * t + 3, (2 * u) % 3)
                if not first:
                    tile_out(it if u else it - 1, (u - 1) % UNR)
                if ahead >= 2:
                    low_weights("WG", ex[u + 2], 2 * t + 4, (2 * u + 1) % 3)

            def tile_out(it, u):
                need(dve, "ry_ready", it * UNR + u + 1)
                need(dve, f"res_in{u}", it * 16 + 16)
                row = B["RY"][:, u * D:(u + 1) * D]
                dve.scalar_tensor_tensor(row, banks[7][:, 0:D], 0.5, row, ALU.mult, ALU.add).then_inc(s["ry"], 1)

            low_tile(0, 0)
            ex = ex + [expert(u) for u in range(2, UNR + 2)]
            tile_vector(0, 0, ex, first=True)
            for u in range(1, UNR):
                tile_vector(0, u, ex)
            with dve.Fori(1, TILES3 - 1) as it:
                ex = [None] + [expert(it * UNR + u) for u in range(1, UNR + 2)]
                for u in range(UNR):
                    tile_vector(it, u, ex)
            ex = [None] + [expert(SLOT_TILES - UNR + u) for u in range(1, UNR)]
            for u in range(UNR):
                tile_vector(TILES3 - 1, u, ex, ahead=UNR - 1 - u)
            tile_out(TILES3 - 1, UNR - 1)

        def attention_vector():
            B = ab
            def pairs(ap, w=M):
                return ap.rearrange("p (a m) -> p a m", m=w)

            def col8(ap):
                return ap.unsqueeze(2).broadcast_to([P, PAIRS, M])

            eye = const("eye2").unsqueeze(1).broadcast_to([P, PAIRS, M])
            eye_half = [const("eye2")[64 * i:64 * i + 64].unsqueeze(1).broadcast_to([64, PAIRS, M]) for i in range(2)]
            smx, ssum, src8, cs, rs, r8 = (B["SM"][:, i * PAIRS:(i + 1) * PAIRS] for i in range(6))
            YZ3 = pairs(B["YZ"][:], P)

            def wait(k, b, n):
                dve.wait_ge(att[k], b * PER[k] + n)

            def block_half(buf, i):
                return pairs(buf[64 * i:64 * i + 64, :], P)[:, :, 64 * i:64 * i + 64]

            def batch_stats(g):
                for j in range(GT):
                    dve.bn_stats(STATS[:, j * 6:(j + 1) * 6], X[:, bass.ds(g * GT * D + j * D, D)]).then_inc(res["stat"], 1)
                wait_alone(res["stat"], g * GT + GT)
                for j in range(GT):
                    dve.bn_aggr(AGG[:, j * 2:(j + 1) * 2], STATS[:, j * 6:(j + 1) * 6]).then_inc(res["agg"], 1)

            def batch_normalise(g):
                dve.wait_ge(res["sd"], g + 1)
                dve.reciprocal(B["LNR"][:], B["LNR"][:]).then_inc(res["rstd"], 1)
                wait_alone(res["rstd"], g + 1)
                for j in range(GT):
                    dve.tensor_scalar(B["XN"][:, j * D:(j + 1) * D], X[:, bass.ds(g * GT * D + j * D, D)], AGG[:, j * 2:j * 2 + 1],
                                      B["LNR"][:, j:j + 1], ALU.subtract, ALU.mult).then_inc(att["xn"], 1)

            def landmarks(b, q, i, c):
                src, dst = (("QT", "QL"), ("KT", "KL"))[i]
                wait("qk", b, 2 * i + c + 1)
                dve.tensor_reduce(B[dst][:, c * M:(c + 1) * M], B[src][q][:, c * GW:(c + 1) * GW].rearrange("p (m l) -> p m l", l=LM),
                                  AX_X, ALU.add).then_inc(att["lm"], 1)

            def block_diagonal(b, q, i, c):
                src, dst = (("QL", "QBD"), ("KL", "KBD"))[i]
                wait("lm", b, 2 * i + c + 1)
                dve.scalar_tensor_tensor(B[dst][q][:, c * 512:(c + 1) * 512].rearrange("p (h m) -> p h m", m=M),
                                         B[src][:, c * M:(c + 1) * M].unsqueeze(1).broadcast_to([P, HC, M]), 1.0 / LM,
                                         const("head_rows").unsqueeze(2).broadcast_to([P, HC, M]), ALU.mult, ALU.mult).then_inc(att["bd"], 1)

            def s3_max(b, p, alone):
                wait("s3max_ready", b, p + 1)
                dve.tensor_reduce(B["NM3"][:, p:p + 1], banks[max_bank(p, alone)][:], AX_X, ALU.max, negate=True).then_inc(att["s3m"], 1)

            def s1_max(b, n):
                c, j = divmod(n, GT)
                wait("s1max_ready", b, n + 1)
                dve.tensor_reduce(B["NM1"][:, j * H + c * HC:j * H + (c + 1) * HC], banks[7][:].rearrange("p (h m) -> p h m", m=M),
                                  AX_X, ALU.max, negate=True).then_inc(att["s1m"], 1)

            s2 = pairs(B["S2"][:])

            def front(b, q, slot, alone=False):
                if slot == 5:
                    landmarks(b, q, 0, 0)
                if slot == 6:
                    landmarks(b, q, 0, 1)
                    block_diagonal(b, q, 0, 0)
                if slot == 7:
                    block_diagonal(b, q, 0, 1)
                    landmarks(b, q, 1, 0)
                if slot == 8:
                    landmarks(b, q, 1, 1)
                    wait("lm", b, 4)
                    dve.tensor_scalar(B["KLS"][:], B["KL"][:], 1.0 / LM, None, ALU.mult).then_inc(att["kls"], 1)
                if slot == 9:
                    block_diagonal(b, q, 1, 0)
                    block_diagonal(b, q, 1, 1)
                if slot == 10:
                    wait("s2_ready", b, 1)
                    dve.tensor_reduce(smx, pairs(banks[front_bank(slot, alone)][:]), AX_X, ALU.max).then_inc(att["s2m"], 1)
                    wait("s2m", b, 1)
                    dve.tensor_tensor(s2, pairs(banks[front_bank(slot, alone)][:]), col8(smx), ALU.subtract).then_inc(att["s2s"], 1)
                for p in S3_MAX.get(slot, ()):
                    s3_max(b, p, alone)
                if slot == 12:
                    wait("s2e", b, 1)
                    dve.tensor_reduce(ssum, s2, AX_X, ALU.add).then_inc(att["s2sum"], 1)
                    wait("s2sum", b, 1)
                    dve.reciprocal(src8, ssum).then_inc(att["s2rc"], 1)
                    wait("s2rc", b, 1)
                    dve.tensor_tensor(s2, s2, col8(src8), ALU.mult).then_inc(att["s2n"], 1)
                if slot == 16:
                    wait("row_ready", b, 1)
                    dve.tensor_reduce(rs, pairs(banks[front_bank(slot, alone)][:]), AX_X, ALU.max).then_inc(att["rs"], 1)
                if slot == 17:
                    wait("col_ready", b, 1)
                    dve.tensor_reduce(cs, pairs(banks[front_bank(COLUMNS, alone)][:]), AX_X, ALU.max).then_inc(att["cs"], 1)
                    wait("cs", b, 1)
                    wait("rs", b, 1)
                    dve.tensor_tensor(cs, cs, rs, ALU.mult).then_inc(att["prod"], 1)
                    wait("prod", b, 1)
                    dve.reciprocal(r8, cs).then_inc(att["r8"], 1)

            def start_z(b):
                wait("r8", b, 1)
                wait("s2n", b, 1)
                dve.tensor_tensor(YZ3[:, :, M:P], s2, col8(r8), ALU.mult).then_inc(att["zt"], 1)

            def start_y(b):
                wait("y0_ready", b, 1)
                for i, h in enumerate(HALF):
                    dve.tensor_tensor(YZ3[h, :, 0:M], pairs(banks[1 - i][h, :]), r8[h].unsqueeze(2).broadcast_to([M, PAIRS, M]),
                                      ALU.mult).then_inc(att["y"], 1)
                wait("y", b, 2)
                dve.scalar_tensor_tensor(pairs(B["B1"][:]), eye, 7.0, YZ3[:, :, 0:M], ALU.mult, ALU.subtract).then_inc(att["b1"], 1)

            def t_norm(b, c):
                wait("pv_ready", b, c + 1)
                tt = B["TT"][:, c * P:(c + 1) * P]
                dve.reciprocal(tt, banks[5][:, 0:P]).then_inc(att["trc"], 1)
                wait("trc", b, c + 1)
                dve.tensor_tensor(tt, banks[4][:, 0:P], tt, ALU.mult).then_inc(att["tt"], 1)

            def t_mask(b, c):
                wait("pt_ready", b, c + 1)
                dve.tensor_tensor(B["TM"][:, c * P:(c + 1) * P].rearrange("p (a d) -> p a d", d=2 * HS),
                                  banks[4 + c][:, 0:P].rearrange("p (a d) -> p a d", d=2 * HS),
                                  const("pair_cols").unsqueeze(1).broadcast_to([P, PC, 2 * HS]), ALU.mult).then_inc(att["tm"], 1)

            def heads_norm(b, c, i, place=None):
                wait("o_ready", b, c + 1)
                num, den = ((banks[4], banks[5]), (banks[6], banks[7]))[c]
                w = GW // 2
                ot = B["OT"][:, c * GW + i * w:c * GW + (i + 1) * w]
                dve.reciprocal(ot, den[:, i * w:(i + 1) * w]).then_inc(att["orc"], 1)
                wait("orc", b, place or 2 * c + i + 1)
                dve.tensor_tensor(ot, num[:, i * w:(i + 1) * w], ot, ALU.mult).then_inc(att["ot"], 1)

            def project(b, jj, last=False):
                if jj == 0:
                    wait("xbo", b, 1)
                wait("pr_ready", b, jj + 1)
                xg = X[:, bass.ds(b * GT * D + jj * 2 * D, 2 * D)]
                dve.tensor_tensor(xg, banks[2 + jj if last else 6][:], xg, ALU.add).then_inc(att["xo"], 1)

            def back(b, slot):
                if 2 <= slot < 10:
                    s1_max(b, slot - 2)
                if slot == 4:
                    t_norm(b, 0)
                if slot == 9:
                    t_norm(b, 1)
                if slot == 10:
                    t_mask(b, 0)
                    t_mask(b, 1)

            def front_alone():
                dve.wait_ge(res["x_in"], 16)
                batch_stats(0)
                batch_normalise(0)
                dve.wait_ge(s_zero, 3)
                dve.tensor_copy(B["ONESR"][:], const("ones")).then_inc(s_picks, 1)
                dve.tensor_copy(B["PICK"][0:H, :].rearrange("p (h m) -> p h m", m=M),
                                const("ident", H)[:, 0:H].unsqueeze(2).broadcast_to([H, H, M])).then_inc(s_picks, 1)
                for slot in range(3 * PINV_ITERS):
                    if slot == 10:
                        dve.wait_ge(res["x_in"], 32)
                        batch_stats(1)
                    front(0, 0, slot, alone=True)
                    if slot == 13:
                        batch_normalise(1)
                start_z(0)
                start_y(0)

            def batch(b, q, first, last):
                def step(slot):
                    if slot in (2, 3) and not first:
                        project(b - 1, slot - 2)
                    back(b, slot)
                    if slot == FFN_STATS_SLOT and not first:
                        wait_alone(att["xo"], (b - 1) * PER["xo"] + 2)
                        stats(s, b - 1, 1)
                    if not last:
                        front(b + 1, 1 - q, slot)
                        if slot == 13:
                            batch_stats(b + 2)
                        if slot == 17:
                            batch_normalise(b + 2)

                if first:
                    dve.wait_ge(res["x_in"], 16 * NG)
                for it in range(PINV_ITERS):
                    wait("m1", b, it + 1)
                    for i, h in enumerate(HALF):
                        dve.scalar_tensor_tensor(pairs(B["B1"][h, :]), eye_half[i], 15.0, pairs(banks[i][h, :]),
                                                 ALU.mult, ALU.subtract).then_inc(att["b2"], 1)
                    if it == 0 and not first:
                        heads_norm(b - 1, 0, 1)
                    step(3 * it)
                    wait("m2", b, it + 1)
                    for i, h in enumerate(HALF):
                        dve.scalar_tensor_tensor(block_half(B["QB"], i), eye_half[i], 13.0, pairs(banks[1 - i][h, :]),
                                                 ALU.mult, ALU.subtract).then_inc(att["qb"], 1)
                    if it == 0 and not first:
                        for i in range(2):
                            heads_norm(b - 1, 1, i)
                    step(3 * it + 1)
                    if it < PINV_ITERS - 1:
                        wait("yz", b, 2 * it + 2)
                        dve.scalar_tensor_tensor(pairs(B["B1"][:]), eye, 7.0, YZ3[:, :, 0:M], ALU.mult, ALU.subtract).then_inc(att["b1"], 1)
                    else:
                        wait("m3", b, it + 1)
                        for c in range(KD):
                            dve.tensor_scalar(pairs(B["ZW"][:])[:, c * PC:(c + 1) * PC, :], pairs(banks[2 + c][:], P)[:, :, M:P], 0.25, None,
                                              ALU.mult).then_inc(att["zw"], 1)
                    step(3 * it + 2)
                if not last:
                    start_z(b + 1)
                wait("w_ready", b, 1)
                for i, h in enumerate(HALF):
                    dve.tensor_copy(B["WS"][h, :], banks[i][h, 0:PAIRS * 2 * HS]).then_inc(att["ws"], 1)
                if not last:
                    start_y(b + 1)
                if last:
                    for i in range(2):
                        for c in range(KD):
                            heads_norm(b, c, i, i * KD + c + 1)
                    for jj in range(2):
                        project(b, jj, True)
                    wait("xo", b, 2)
                else:
                    heads_norm(b, 0, 0)

            over_batches(dve, front_alone, batch)

        ffn_vector(0)
        attention_vector()
        ffn_vector(1)

    @block.scalar
    def _(act):
        def deviation(q, g, n=0):
            act.wait_ge(q["mv"], n * NG + g + 1)
            act.activation(RSTD[:, bass.ds(g * GT, GT)], mvv[:, bass.ds(g * GT, GT), 1], ACT.Sqrt, bias=const("eps")).then_inc(q["sd"], 1)

        def ffn_scalar(n):
            B = fbs[n]

            def need(eng, k, v):
                eng.wait_ge(s[k], n * FFN_PER[k] + (k in GIVEN) + v)

            if n == 0:
                act.wait_ge(s_const, 16)

            def turned(g):
                need(act, "xt_ready", g + 1)
                for k in range(KD):
                    act.copy(XNT[:, k * T + g * GW:k * T + (g + 1) * GW], banks[(0, 5)[g % 2] + k][:]).then_inc(s["xt_sb"], 1)

            def turned_logits(half):
                need(act, "lg_ready", half * QG + QG)
                act.copy(B[f"LGT{half}"], banks[3 + half][:]).then_inc(s["lgt_sb"], 1)

            deviation(s, 0, n)
            deviation(s, 1, n)
            for g in range(NG):
                if g + 2 < NG:
                    deviation(s, g + 2, n)
                turned(g)
                if g == QG + 1:
                    turned_logits(0)
                    if n == 0:
                        act.wait_ge(s_shared, 16 * 3)
                        for high, w in ((SGH, SG), (SUH, SU)):
                            act.copy(high[:], w).then_inc(s_split_hi, 1)

            def high_tokens(g, u):
                act.copy(B["XHL"][2 * u][:].rearrange("p (k t) -> p k t", k=KD),
                         XNT[:].rearrange("p (k t) -> p k t", k=KD)[:, :, bass.ds(g * GW, GW)]).then_inc(s["xh"], 1)

            need(act, "xt_sb", KD * NG)
            high_tokens(0, 0)
            turned_logits(1)
            need(act, "mx", 1)
            act.activation(B["SCORE"][:], B["MX"][:], ACT.Sigmoid).then_inc(s["score"], 1)

            def shared_group(g, u, last=False):
                for f in range(KF):
                    need(act, "gu", g * KF + f + 1)
                    act.activation(B["HSB"][:, (f % 2) * F:(f % 2 + 1) * F], banks[f % 2][:], ACT.Silu).then_inc(s["silu"], 1)
                    if f == 0 and not last:
                        high_tokens(g + 1, 1 - u)

            with act.Fori(0, NG // 2 - 1) as i:
                for u in range(2):
                    shared_group(i * 2 + u, u)
            shared_group(NG - 2, 0)

            def expert(t):
                return act.value_load(B["EXPERT"][0:1, bass.ds(t, 1)], min_val=0, max_val=E - 1)

            def high_weights(w, ex, slot):
                act.copy(WHL[2 * slot][:], B[w][:, bass.ds(ex * (KD * F), KD * F)]).then_inc(s["whi"], 1)

            need(act, "wg", 16)
            need(act, "wu", 16)
            need(act, "expert_of", 1)
            need(act, "x_out", 16 * PARTS_G)
            ex = [expert(u) for u in range(2)]
            high_weights("WG", ex[0], 0)
            high_weights("WU", ex[0], 1)
            high_weights("WG", ex[1], 2)
            shared_group(NG - 1, 1, True)

            def xgt(t, u):
                need(act, "xg_t", t + 1)
                act.copy(XGH[:, u * D:(u + 1) * D], banks[0][:, 0:D]).then_inc(s["xgt"], 1)

            def silu(t, u):
                need(act, "rg", t + 1)
                act.activation(B["RS"][:, u * F:(u + 1) * F], banks[1 + u % 2][:], ACT.Silu).then_inc(s["rsilu"], 1)

            def ht(t, u):
                need(act, "ht_ready", t + 1)
                act.copy(B["HT"][:, u * F:(u + 1) * F], banks[6][:]).then_inc(s["ht_sb"], 1)

            def tile_scalar(it, u, ex, first=False, ahead=2):
                t = it * UNR + u
                silu(t, u)
                if not first:
                    ht(t - 1, (u - 1) % UNR)
                if ahead >= 1:
                    high_weights("WU", ex[u + 1], (2 * u) % 3)
                    xgt(t + 1, (u + 1) % UNR)
                if ahead >= 2:
                    need(act, "ru", t + 1)
                    high_weights("WG", ex[u + 2], (2 * u + 1) % 3)

            xgt(0, 0)
            ex = ex + [expert(u) for u in range(2, UNR + 2)]
            tile_scalar(0, 0, ex, first=True)
            for u in range(1, UNR):
                tile_scalar(0, u, ex)
            with act.Fori(1, TILES3 - 1) as it:
                ex = [None] + [expert(it * UNR + u) for u in range(1, UNR + 2)]
                for u in range(UNR):
                    tile_scalar(it, u, ex)
            ex = [None] + [expert(SLOT_TILES - UNR + u) for u in range(1, UNR)]
            for u in range(UNR):
                tile_scalar(TILES3 - 1, u, ex, ahead=UNR - 1 - u)
            ht(SLOT_TILES - 1, UNR - 1)

        def attention_scalar():
            B = ab
            def wait(k, b, n):
                act.wait_ge(att[k], b * PER[k] + n)

            def batch_deviation(g):
                act.wait_ge(res["agg"], g * GT + GT)
                act.activation(B["LNR"][:], AGG[:].rearrange("p (t c) -> p t c", c=2)[:, :, 1], ACT.Sqrt, bias=const("eps")).then_inc(res["sd"], 1)

            def turned(b):
                wait("xt_ready", b, 1)
                for k in range(KD):
                    act.copy(B["XTS"][:, k * GW:(k + 1) * GW], banks[2 + k][:]).then_inc(att["xts"], 1)

            def rounded(b, dst, src, k):
                act.copy(dst, src).then_inc(att[k], 1)

            def front(b, q, slot, alone=False):
                if 4 <= slot < 8:
                    i, c = divmod(slot - 4, KD)
                    (dst, scale), dst_r = (("QT", HS ** -0.5), ("KT", 1.0))[i], (B["QTR"][q], B["KTR"])[i]
                    part = slice(c * GW, (c + 1) * GW)
                    wait("qk_ready", b, slot - 3)
                    act.mul(B[dst][q][:, part], banks[front_bank(slot, alone)][:], scale).then_inc(att["qk"], 1)
                    wait("qk", b, slot - 3)
                    rounded(b, dst_r[:, part], B[dst][q][:, part], "qkr")
                if slot in (8, 12):
                    i = (slot - 8) // 4
                    wait("v_ready", b, i + 1)
                    act.copy(B["V"][q][:, i * 512:(i + 1) * 512], banks[front_bank(slot, alone)][:]).then_inc(att["v_sb"], 1)
                if slot == 9:
                    wait("bd", b, 2)
                    rounded(b, B["QBDR"][:], B["QBD"][q][:], "bdr")
                if slot == 11:
                    wait("s2s", b, 1)
                    act.activation(B["S2"][:], B["S2"][:], ACT.Exp).then_inc(att["s2e"], 1)
                if slot == 12:
                    wait("bd", b, 4)
                    if not alone:
                        wait("s1max_ready", b - 1, 8)
                    rounded(b, B["KBDR"][:], B["KBD"][q][:], "bdr")
                if slot == 14:
                    wait("s2t_ready", b, 1)
                    for i, h in enumerate(HALF):
                        act.copy(B["S2T"][h, :], banks[turned_banks(alone)[i]][h, :]).then_inc(att["s2t"], 1)

            def exp3(b, n):
                wait("s3t_ready", b, n + 1)
                act.activation(B["E3"][:, n % GT * 512:(n % GT + 1) * 512], banks[4 + n % 2][:], ACT.Exp).then_inc(att["e3"], 1)

            def exp1(b, p):
                wait("s1t_ready", b, p + 1)
                act.activation(B["E1"][:, p * GW:(p + 1) * GW], banks[4 + p % 2][:], ACT.Exp).then_inc(att["e1"], 1)

            def back(b, slot):
                if slot < 4:
                    exp3(b, slot)
                elif 5 <= slot < 9:
                    exp3(b, slot - 1)
                elif slot == 10:
                    wait("nm1_ready", b, 1)
                    act.copy(B["NM1T"][0:H, :], banks[7][0:H, :]).then_inc(att["nm1"], 1)
                elif slot >= 11:
                    exp1(b, slot - 11)

            def front_alone():
                batch_deviation(0)
                turned(0)
                for slot in range(3 * PINV_ITERS):
                    front(0, 0, slot, alone=True)
                    if slot == 11:
                        batch_deviation(1)
                turned(1)

            def batch(b, q, first, last):
                def step(slot):
                    if slot == 0 and not (first or last):
                        turned(b + 1)
                    if not last:
                        front(b + 1, 1 - q, slot)
                        if slot == 14:
                            batch_deviation(b + 2)
                    back(b, slot)

                for it in range(PINV_ITERS):
                    step(3 * it)
                    step(3 * it + 1)
                    if it < PINV_ITERS - 1:
                        wait("m3", b, it + 1)
                        for c in range(KD):
                            act.mul(B["YZ"][:, c * 512:(c + 1) * 512], banks[2 + c][:], 0.25).then_inc(att["yz"], 1)
                    step(3 * it + 2)
                exp1(b, PAIRS - 1)

            over_batches(act, front_alone, batch)

        ffn_scalar(0)
        attention_scalar()
        ffn_scalar(1)

    @block.gpsimd
    def _(pool):
        def wait_alone(semaphore, v):
            pool.wait_ge(semaphore, v)
            pool.sem_inc(s_pool_past, 1)

        def ffn_pool(n):
            B = fbs[n]

            def need(k, v):
                wait_alone(s[k], n * FFN_PER[k] + (k in GIVEN) + v)

            if n == 0:
                for i, (low, w, high) in enumerate(((SGL, SG, SGH), (SUL, SU, SUH))):
                    pool.wait_ge(s_split_hi, i + 1)
                    pool.tensor_tensor(low[:], w, high[:].bitcast(F32), ALU.subtract).then_inc(s_split_lo, 1)
            need("rs", 1)
            def scored(g):
                need("xs_out", g * 16)
                pool.tensor_copy(B["XS"], X[:, bass.ds(g * GT * D, GT * D)]).then_inc(s["xs_raw"], 1)
                pool.tensor_copy(B["RS4"][:], B["RSC"][:, bass.ds(g * GT, GT)]).then_inc(s["xs_raw"], 1)
                pool.tensor_copy(B["NM4"][:], B["NMR"][:, bass.ds(g * GT, GT)]).then_inc(s["xs_raw"], 1)
                need("xs_raw", g * 3 + 3)
                for j in range(GT):
                    row = B["XS"][:, j * D:(j + 1) * D]
                    pool.tensor_scalar(row, row, B["RS4"][:, j:j + 1], B["NM4"][:, j:j + 1], ALU.mult, ALU.add).then_inc(s["xs"], 1)

            def seated(g):
                pool.tensor_copy(B["SIDX"][:], B["SLOT"][:, bass.ds(g * GT, GT)]).then_inc(s["sidx"], 1)
                pool.tensor_copy(B["STOK"][:], B["TOK"][:, bass.ds(g * GT, GT)]).then_inc(s["sidx"], 1)
                need("sidx", g * 2 + 2)
                for j in range(GT):
                    pool.indirect_dma_start(out=who_dram[n], out_offset=bass.IndirectOffsetOnAxis(ap=B["SIDX"][:, j:j + 1], axis=0),
                                            in_=B["STOK"][:, j:j + 1], in_offset=None).then_inc(s["who"], 16)

            scored(0)
            need("slots", 2)
            need("who_init", 16)
            seated(0)
            with pool.Fori(1, NG) as g:
                scored(g)
                need("who", g * (16 * GT))
                seated(g)
            def gather(t, u):
                pool.tensor_copy(B["GIDX"][:, u:u + 1], B["WHO"][:, bass.ds(t, 1)]).then_inc(s["gidx"], 1)
                need("gidx", t + 1)
                pool.indirect_dma_start(out=B["XS"][:, u * D:(u + 1) * D], out_offset=None, in_=xs_dram,
                                        in_offset=bass.IndirectOffsetOnAxis(ap=B["GIDX"][:, u:u + 1], axis=0),
                                        bounds_check=T - 1, oob_is_err=False).then_inc(s[f"gath{u}"], 16)

            def gather_residual(t, u):
                pool.tensor_copy(B["YIDX"][:, u:u + 1], B["WHO"][:, bass.ds(t, 1)]).then_inc(s["yidx"], 1)
                need("yidx", t + 1)
                pool.indirect_dma_start(out=B["RY"][:, u * D:(u + 1) * D], out_offset=None, in_=shared_dram,
                                        in_offset=bass.IndirectOffsetOnAxis(ap=B["YIDX"][:, u:u + 1], axis=0),
                                        bounds_check=T - 1, oob_is_err=False).then_inc(s[f"res_in{u}"], 16)

            def scatter(t, u):
                need("ry", t + 1)
                pool.indirect_dma_start(out=mid_dram if n == 0 else out_flat, out_offset=bass.IndirectOffsetOnAxis(ap=B["YIDX"][:, u:u + 1], axis=0),
                                        in_=B["RY"][:, u * D:(u + 1) * D], in_offset=None,
                                        bounds_check=T - 1, oob_is_err=False).then_inc(s[f"ry_out{u}"], 16)

            def tile_dma(it, u, first=False, last=False):
                t = it * UNR + u
                if not last:
                    need("xg_t", t + 1)
                    gather(t + UNR, u)
                scatter(t, u)
                if not (last and u > 0):
                    if not first:
                        need(f"ry_out{(u - 1) % UNR}", (it if u else it - 1) * 16 + 16)
                    gather_residual(t + UNR - 1, (u - 1) % UNR)

            need("who_sb", 16)
            need("xs_out", 16 * NG)
            for u in range(UNR):
                gather(u, u)
            need("x_out", 16 * PARTS_G)
            need("x_out_last", 16 * (NG - PARTS_G))
            need("ry_clear", 1)
            for u in range(UNR - 1):
                gather_residual(u, u)
            tile_dma(0, 0, first=True)
            for u in range(1, UNR):
                tile_dma(0, u)
            with pool.Fori(1, TILES3 - 1) as it:
                for u in range(UNR):
                    tile_dma(it, u)
            for u in range(UNR):
                tile_dma(TILES3 - 1, u, last=True)
            for u in range(UNR):
                pool.wait_ge(s[f"ry_out{u}"], (n + 1) * FFN_PER[f"ry_out{u}"])

        def attention_pool():
            B = ab
            for name in ("QB",):
                pool.memset(B[name][:], 0.0).then_inc(s_zero, 1)
            for name in ("NM1T", "PICK"):
                pool.memset(B[name][:].bitcast(F32), 0.0).then_inc(s_zero, 1)
            with pool.Fori(0, NG) as b:
                def wait(k, n):
                    wait_alone(att[k], b * PER[k] + n)

                wait("xn", GT)
                xg = X[:, bass.ds(b * GT * D, GT * D)].rearrange("p (t d) -> p t d", d=D)
                pool.tensor_tensor(xg, xg, BO[:].unsqueeze(1).broadcast_to([P, GT, D]), ALU.add).then_inc(att["xbo"], 1)
                for p in range(PAIRS):
                    wait("s3m", p + 1)
                    pool.tensor_scalar(B["NM3BD"][:, p * P:(p + 1) * P], const("ident"), B["NM3"][:, p:p + 1], None, ALU.mult).then_inc(att["nm3"], 1)

        for k in sorted(GIVEN):
            pool.sem_inc(s[k], 1)
        ffn_pool(0)
        pool.wait_ge(s_attn_w, 16 * 5)
        attention_pool()
        ffn_pool(1)

    @block.tensor
    def _(pe):
        ident = const("ident")

        def transposes(src, bank0, inc):
            for k in range(KD):
                for j in range(GT):
                    ins = pe.transpose(banks[bank0 + k][:, j * P:(j + 1) * P], src[:, j * D + k * P:j * D + (k + 1) * P], ident)
            ins.then_inc(inc, 1)

        def ffn_tensor(n):
            B = fbs[n]

            def need(eng, k, v):
                eng.wait_ge(s[k], n * FFN_PER[k] + (k in GIVEN) + v)

            if n == 0:
                pe.wait_ge(s_const, 16)
                pe.wait_ge(s_gate, 16)
                pe.wait_ge(s_gate_pad, 1)

            def turn(g):
                need(pe, "xn", g * GT + GT)
                if g >= 2:
                    need(pe, "xt_sb", (g - 1) * KD)
                transposes(B["XN"][g % 2], (0, 5)[g % 2], s["xt_ready"])

            def logits(g):
                need(pe, "xt_sb", g * KD + KD)
                rows = slice(g % QG * QUAD, (g % QG + 1) * QUAD)
                for k in range(KD):
                    ins = pe.matmul(banks[3 + g // QG][rows, :], GWT[:, k * QUAD:(k + 1) * QUAD], XNT[:, k * T + g * GW:k * T + (g + 1) * GW],
                                    start=(k == 0), stop=(k == KD - 1))
                ins.then_inc(s["lg_ready"], 1)

            def turn_logits(half):
                need(pe, "lgt_sb", half + 1)
                to = banks[2][:, half * QG * GT * E:(half + 1) * QG * GT * E].rearrange("p (q j e) -> p q j e", q=QG, j=GT)
                for j in range(GT):
                    ins = pe.matmul(to[:, :, j, :], B[f"LGT{half}"][:, j * P:(j + 1) * P], ident.rearrange("p (q e) -> p q e", q=QG)[:, :, 0:E],
                                    start=True, stop=True)
                ins.then_inc(s["logits"], 1)

            turn(0)
            for g in range(1, NG):
                turn(g)
                logits(g - 1)
            turn_logits(0)
            logits(NG - 1)
            turn_logits(1)

            def count():
                need(pe, "oh", 1)
                pe.matmul(banks[3][:, 0:NT * E], const("before"), B["OH"][:], start=True, stop=True).then_inc(s["cnt_ready"], 1)
                pe.matmul(banks[4][:, 0:NT * E], const("ones"), B["OH"][:], start=True, stop=True).then_inc(s["cnt_ready"], 1)

            if n == 0:
                pe.wait_ge(s_shared, 16 * 3)
                pe.wait_ge(s_split_lo, 2)
            def shared_group(g, u, first=False):
                def gate_up(f):
                    if f == 0:
                        need(pe, "xl", g + 1)
                    if f < 2:
                        need(pe, "h", g * KF)
                    else:
                        need(pe, "h", g * KF + f - 1)
                    xh, xl = B["XHL"][2 * u:2 * u + 2]
                    for bank, high, low in ((f % 2, SGH, SGL), (5 + f % 2, SUH, SUL)):
                        for k in range(KD):
                            part = slice(k * F + f * P, k * F + (f + 1) * P)
                            for i, (w, tok) in enumerate(((high, xh), (high, xl), (low, xh))):
                                ins = pe.matmul(banks[bank][:], w[:, part], tok[:, k * GW:(k + 1) * GW],
                                                start=(k == 0 and i == 0), stop=(k == KD - 1 and i == 2))
                    ins.then_inc(s["gu"], 1)

                def down(f):
                    need(pe, "h", g * KF + f + 1)
                    if f == 0:
                        need(pe, "x_new", g * 2)
                    for j in range(GT):
                        ins = pe.matmul(banks[7 if j < 2 else 2][:, (j % 2) * D:(j % 2 + 1) * D], B["HB"][:, f * GW + j * P:f * GW + (j + 1) * P],
                                        SDN[:, f * D:(f + 1) * D], start=(f == 0 and j % 2 == 0), stop=(f == KF - 1), skip_group_check=True)
                    if f == KF - 1:
                        ins.then_inc(s["y_ready"], 1)

                gate_up(0)
                if first:
                    count()
                gate_up(1)
                down(0)
                gate_up(2)
                down(1)
                gate_up(3)
                down(2)
                down(3)

            shared_group(0, 0, first=True)
            shared_group(1, 1)
            with pe.Fori(1, NG // 2) as i:
                for u in range(2):
                    shared_group(i * 2 + u, u)

            need(pe, "expert_of", 1)
            def expert(t):
                return pe.value_load(B["EXPERT"][0:1, bass.ds(t, 1)], min_val=0, max_val=E - 1)

            def xt(it, u):
                need(pe, f"gath{u}", it * 16 + 16)
                for k in range(KD):
                    ins = pe.transpose(banks[0][:, k * P:(k + 1) * P], B["XS"][:, u * D + k * P:u * D + (k + 1) * P], ident)
                ins.then_inc(s["xg_t"], 1)

            def through(bank, t, u, m, inc):
                need(pe, "wlo", 2 * t + m + 1)
                slot = (2 * u + m) % 3
                high, low = WHL[2 * slot], WHL[2 * slot + 1]
                for k in range(KD):
                    xh, xl = (part[:, u * D + k * P:u * D + (k + 1) * P] for part in (XGH, XGL))
                    for i, (tok, w) in enumerate(((xh, high), (xh, low), (xl, high))):
                        ins = pe.matmul(banks[bank][:], tok, w[:, k * F:(k + 1) * F],
                                        start=(k == 0 and i == 0), stop=(k == KD - 1 and i == 2))
                ins.then_inc(inc, 1)

            def ht(t, u):
                need(pe, "rh", t + 1)
                for f in range(KF):
                    ins = pe.transpose(banks[6][:, f * P:(f + 1) * P], B["RH"][:, u * F + f * P:u * F + (f + 1) * P], ident)
                ins.then_inc(s["ht_ready"], 1)

            def down(t, u, ex):
                need(pe, "ht_sb", t + 1)
                need(pe, "ry", t)
                for f in range(KF):
                    ins = pe.matmul(banks[7][:, 0:D], B["HT"][:, u * F + f * P:u * F + (f + 1) * P],
                                    B["WD"][:, bass.ds(ex * (KF * D) + f * D, D)], start=(f == 0), stop=(f == KF - 1))
                ins.then_inc(s["ry_ready"], 1)

            def tile_tensor(it, u, before=None, first=False, last=False, loading=False):
                t = it * UNR + u
                need(pe, "xgl", t + 1)
                if not first:
                    need(pe, "rsilu", t)
                through(1 + u % 2, t, u, 0, s["rg"])
                if not first:
                    ht(t - 1, (u - 1) % UNR)
                if before is None and not first:
                    before = expert(t - 1)
                through(3 + u, t, u, 1, s["ru"])
                if not last:
                    xt(it if u < UNR - 1 else it + 1, (u + 1) % UNR)
                if not first:
                    if loading:
                        need(pe, "wd", 32)
                    down(t - 1, (u - 1) % UNR, before)

            xt(0, 0)
            ex = [expert(u) for u in range(UNR - 1)]
            tile_tensor(0, 0, None, first=True)
            need(pe, "x_new", 2 * NG)
            for u in range(1, UNR):
                tile_tensor(0, u, ex[u - 1], loading=(u == 1))
            with pe.Fori(0, (TILES3 - 2) // 2) as i:
                for half in range(2):
                    it = i * 2 + 1 + half
                    for u in range(UNR):
                        tile_tensor(it, u)
            for it in range(1 + (TILES3 - 2) // 2 * 2, TILES3 - 1):
                for u in range(UNR):
                    tile_tensor(it, u)
            ex = [expert(SLOT_TILES - UNR + u - 1) for u in range(UNR + 1)]
            for u in range(UNR):
                tile_tensor(TILES3 - 1, u, ex[u], last=(u == UNR - 1))
            ht(SLOT_TILES - 1, UNR - 1)
            down(SLOT_TILES - 1, UNR - 1, ex[UNR])

        def attention_tensor():
            B = ab
            pe.wait_ge(s_attn_w, 16 * 5)

            def wait(k, b, n):
                pe.wait_ge(att[k], b * PER[k] + n)

            def past_waits():
                pe.sem_inc(s_pe_past, 1)

            def bd(buf, p):
                return buf[:, p * P:(p + 1) * P]

            def turn(b):
                wait("xn", b, GT)
                transposes(B["XN"], 2, att["xt_ready"])

            def front_wide(b, q, slot, alone=False, second=False):
                bank = front_bank(slot, alone) if slot in (4, 5, 6, 7, 8, 10, 12, 16) else None
                if 4 <= slot < 8:
                    i, c = divmod(slot - 4, KD)
                    if slot == 4:
                        wait("xts", b, KD)
                        if not (alone or second):
                            wait("xo", b - 2, 2)
                    elif not alone:
                        wait("qk", b, slot - 4)
                    for k in range(KD):
                        ins = pe.matmul(banks[bank][:], (WQ, WK)[i][:, k * D + c * P:k * D + (c + 1) * P], B["XTS"][:, k * GW:(k + 1) * GW],
                                        start=(k == 0), stop=(k == KD - 1))
                    ins.then_inc(att["qk_ready"], 1)
                if slot in (8, 12):
                    if not alone:
                        if slot == 8:
                            wait("qk", b, 4)
                        else:
                            wait("s3m", b, 2)
                    for jj in range(2):
                        j = (slot - 8) // 2 + jj
                        for k in range(KD):
                            ins = pe.matmul(banks[bank][:, jj * D:(jj + 1) * D], B["XTS"][:, k * GW + j * P:k * GW + (j + 1) * P],
                                            WV[:, k * D:(k + 1) * D], start=(k == 0), stop=(k == KD - 1))
                    ins.then_inc(att["v_ready"], 1)
                if slot == 10:
                    wait("bd", b, 2)
                    wait("kls", b, 1)
                    wait("v_sb", b, 1)
                    for p in range(PAIRS):
                        c = p // PC
                        ins = pe.matmul(banks[bank][:, p * M:(p + 1) * M], bd(B["QBD"][q], p), B["KLS"][:, c * M:(c + 1) * M], start=True, stop=True)
                    ins.then_inc(att["s2_ready"], 1)
                if slot == 14:
                    wait("s2n", b, 1)
                    wait("v_sb", b, 2)
                    if not alone:
                        wait("s3m", b, 5)
                    past_waits()
                    for p in range(PAIRS):
                        for i, h in enumerate(HALF):
                            ins = pe.matmul(banks[turned_banks(alone)[i]][h, p * M:(p + 1) * M], B["S2"][h, p * M:(p + 1) * M], const("eye2")[h],
                                            start=True, stop=True)
                    ins.then_inc(att["s2t_ready"], 1)
                if slot == 16:
                    wait("s2t", b, 2)
                    wait("s3m", b, 7)
                    pe.matmul(banks[bank][:], const("halves"), B["S2T"][:], start=True, stop=True).then_inc(att["row_ready"], 1)

            def column_sums(b, alone=False):
                wait("s3m", b, 8)
                pe.matmul(banks[front_bank(COLUMNS, alone)][:], const("halves"), B["S2"][:], start=True, stop=True).then_inc(att["col_ready"], 1)

            def s3_max(b, p, alone=False):
                c = p // PC
                if p == 0:
                    if not alone:
                        wait("nm1", b - 1, 1)
                    wait("bdr", b, 1)
                    wait("qkr", b, 4)
                elif alone:
                    if p >= 4:
                        wait("s3m", b, p - 3)
                elif p == 1:
                    wait("s2s", b, 1)
                elif p in (2, 3, 7):
                    wait("s3m", b, {2: 1, 3: 3, 7: 6}[p])
                elif p == 4:
                    wait("v_sb", b, 2)
                else:
                    wait("s2t", b, 2)
                pe.matmul(banks[max_bank(p, alone)][:], bd(B["QBDR"], p), B["KTR"][:, c * GW:(c + 1) * GW], start=True, stop=True).then_inc(att["s3max_ready"], 1)

            def s1_max(b, q, n, first):
                c, j = divmod(n, GT)
                if n == 0:
                    wait("bdr", b, 2)
                    if not first:
                        wait("ot", b - 1, 4)
                else:
                    wait("s1m", b, n)
                pe.matmul(banks[7][:], B["QTR"][q][:, c * GW + j * P:c * GW + (j + 1) * P], B["KBDR"][:, c * 512:(c + 1) * 512],
                          start=True, stop=True).then_inc(att["s1max_ready"], 1)

            def start_y(b):
                wait("s2t", b, 2)
                past_waits()
                for p in range(PAIRS):
                    for i, h in enumerate(HALF):
                        s2t = B["S2T"][h, p * M:(p + 1) * M]
                        ins = pe.matmul(banks[1 - i][h, p * M:(p + 1) * M], s2t, s2t, start=True, stop=True)
                ins.then_inc(att["y0_ready"], 1)

            def s3t(b, q, n, first):
                c, j = divmod(n, GT)
                if n == 0:
                    wait("nm3", b, PAIRS)
                    if not first:
                        wait("ot", b - 1, 2)
                elif n in (4, 5):
                    wait("tt", b, 1)
                elif n != 1:
                    wait("e3", b, n - 1)
                bank = banks[4 + n % 2]
                pe.matmul(bank[:], B["KT"][q][:, c * GW + j * P:c * GW + (j + 1) * P], B["QBD"][q][:, c * 512:(c + 1) * 512], start=True, stop=False)
                pe.matmul(bank[:], B["ONESR"][:], B["NM3BD"][:, c * 512:(c + 1) * 512], start=False, stop=True).then_inc(att["s3t_ready"], 1)

            def pv(b, q, c):
                wait("e3", b, 4 * c + 4)
                for j in range(GT):
                    for a in range(PC):
                        rows = slice(32 * a, 32 * a + 32)
                        e3 = B["E3"][:, j * 512 + a * P:j * 512 + (a + 1) * P]
                        pe.matmul(banks[4][rows, 0:P], B["V"][q][:, j * D + c * P + a * 32:j * D + c * P + (a + 1) * 32], e3,
                                  start=(j == 0), stop=(j == GT - 1))
                    for a in range(PC):
                        rows = slice(32 * a, 32 * a + 32)
                        e3 = B["E3"][:, j * 512 + a * P:j * 512 + (a + 1) * P]
                        ins = pe.matmul(banks[5][rows, 0:P], const("ones")[:, 0:32], e3, start=(j == 0), stop=(j == GT - 1))
                ins.then_inc(att["pv_ready"], 1)

            def pt(b):
                wait("tt", b, 2)
                for c in range(KD):
                    pe.transpose(banks[4 + c][:, 0:P], B["TT"][:, c * P:(c + 1) * P], ident).then_inc(att["pt_ready"], 1)

            def s1t(b, q, p):
                c = p // PC
                if p == 0:
                    wait("nm1", b, 1)
                if p < 2:
                    wait("tm", b, p + 1)
                else:
                    wait("e1", b, p - 1)
                bank = banks[4 + p % 2]
                pe.matmul(bank[:], bd(B["KBD"][q], p), B["QT"][q][:, c * GW:(c + 1) * GW], start=True, stop=False)
                pe.matmul(bank[:], bd(B["PICK"], p), B["NM1T"][:], start=False, stop=True).then_inc(att["s1t_ready"], 1)

            def heads(b, c):
                num, den = ((banks[4], banks[5]), (banks[6], banks[7]))[c]
                for a in range(PC):
                    p = c * PC + a
                    pe.matmul(num[32 * a:32 * a + 32, :], B["WS"][:, p * 32:(p + 1) * 32], B["E1"][:, p * GW:(p + 1) * GW], start=True, stop=True)
                for a in range(PC):
                    p = c * PC + a
                    ins = pe.matmul(den[32 * a:32 * a + 32, :], const("pair_cols"), B["E1"][:, p * GW:(p + 1) * GW], start=True, stop=True)
                ins.then_inc(att["o_ready"], 1)

            def project(b, jj, last=False):
                if last:
                    wait("ot", b, 2 * jj + 2)
                elif jj == 0:
                    wait("ot", b, 4)
                else:
                    wait("xo", b, 1)
                for i in range(2):
                    j = jj * 2 + i
                    for c in range(KD):
                        ins = pe.matmul(banks[2 + jj if last else 6][:, i * D:(i + 1) * D], B["OT"][:, c * GW + j * P:c * GW + (j + 1) * P],
                                        WO[:, c * D:(c + 1) * D], start=(c == 0), stop=(c == KD - 1))
                ins.then_inc(att["pr_ready"], 1)

            def back(b, q, slot, first):
                if slot == 1:
                    s3t(b, q, 0, first)
                    s3t(b, q, 1, first)
                elif 2 <= slot < 4:
                    s3t(b, q, slot, first)
                elif slot == 4:
                    pv(b, q, 0)
                elif 5 <= slot < 9:
                    s3t(b, q, slot - 1, first)
                elif slot == 9:
                    pv(b, q, 1)
                elif slot == 10:
                    pt(b)
                elif slot >= 11:
                    s1t(b, q, slot - 11)

            def front_alone():
                turn(0)
                pe.wait_ge(s_picks, 2)
                pe.wait_ge(s_zero, 3)
                for slot in range(3 * PINV_ITERS):
                    front_wide(0, 0, slot, alone=True)
                    for p in S3_MAX.get(slot, ()):
                        s3_max(0, p, alone=True)
                    if slot == 17:
                        column_sums(0, alone=True)
                wait("rs", 0, 1)
                wait("cs", 0, 1)
                turn(1)
                start_y(0)

            def batch(b, q, first, last):
                def step(slot):
                    if slot == 0 and not first:
                        wait("rs", b, 1)
                        wait("cs", b, 1)
                        heads(b - 1, 1)
                        if not last:
                            turn(b + 1)
                    if slot in (2, 3):
                        back(b, q, slot, first)
                        if not first:
                            project(b - 1, slot - 2)
                    if not last:
                        front_wide(b + 1, 1 - q, slot, second=first)
                        for p in S3_MAX.get(slot, ()):
                            s3_max(b + 1, p)
                        if slot == 17:
                            column_sums(b + 1)
                    if 2 <= slot < 10:
                        s1_max(b, q, slot - 2, first)
                    if slot == 10:
                        wait("s1m", b, 8)
                        for j in range(GT):
                            ins = pe.transpose(banks[7][0:H, j * P:(j + 1) * P], B["NM1"][:, j * H:(j + 1) * H], ident)
                        ins.then_inc(att["nm1_ready"], 1)
                    if slot not in (2, 3):
                        back(b, q, slot, first)

                def y_times_b(m):
                    past_waits()
                    for p in range(PAIRS):
                        for i, h in enumerate(HALF):
                            ins = pe.matmul(banks[(i + m) % 2][h, p * M:(p + 1) * M], B["YZ"][h, p * P:p * P + M], B["B1"][h, p * M:(p + 1) * M],
                                            start=True, stop=True)
                    return ins

                for it in range(PINV_ITERS):
                    wait("b1", b, it + 1)
                    y_times_b(0).then_inc(att["m1"], 1)
                    step(3 * it)
                    wait("b2", b, 2 * it + 2)
                    y_times_b(1).then_inc(att["m2"], 1)
                    step(3 * it + 1)
                    wait("qb", b, 2 * it + 2)
                    if it == 0:
                        wait("zt", b, 1)
                        if not last:
                            wait("xts", b + 1, KD)
                    for p in range(PAIRS):
                        ins = pe.matmul(banks[2 + p // PC][:, (p % PC) * P:(p % PC + 1) * P], bd(B["QB"], p), bd(B["YZ"], p), start=True, stop=True)
                    ins.then_inc(att["m3"], 1)
                    step(3 * it + 2)
                s1t(b, q, PAIRS - 1)
                wait("zw", b, 2)
                wait("tm", b, 2)
                past_waits()
                for p in range(PAIRS):
                    for i, h in enumerate(HALF):
                        ins = pe.matmul(banks[i][h, p * 32:(p + 1) * 32], B["ZW"][h, p * M:(p + 1) * M], B["TM"][h, p * 32:(p + 1) * 32],
                                        start=True, stop=True)
                ins.then_inc(att["w_ready"], 1)
                if not last:
                    start_y(b + 1)
                wait("ws", b, 2)
                wait("e1", b, 8)
                heads(b, 0)
                if last:
                    heads(b, 1)
                    project(b, 0, True)
                    project(b, 1, True)

            over_batches(pe, front_alone, batch)

        ffn_tensor(0)
        attention_tensor()
        ffn_tensor(1)


def kernel(L0_attn_x, L0_attn_Wk, L0_attn_Wq, L0_attn_Wv, L0_attn_Wo, L0_attn_bo, L0_ffn_gate_w, L0_ffn_shared_gate, L0_ffn_shared_up,
           L0_ffn_shared_down, L0_ffn_r_gate, L0_ffn_r_up, L0_ffn_r_down):
    import numpy as _np
    import concourse.bacc as _bacc
    from concourse import mybir as _mybir
    from concourse.bass_utils import run_bass_kernel_spmd as _run

    def rows(w):
        w = _np.asarray(w)
        *lead, k, n = w.shape
        w = w.reshape(*lead, k // P, P, n)
        return _np.ascontiguousarray(_np.moveaxis(w, -2, 0).reshape(P, -1))

    def turned(w):
        return rows(_np.swapaxes(_np.asarray(w), -1, -2))

    arrays = {
        "x": _np.ascontiguousarray(L0_attn_x), "wq": rows(L0_attn_Wq), "wk": rows(L0_attn_Wk), "wv": rows(L0_attn_Wv), "wo": rows(L0_attn_Wo),
        "bo": _np.ascontiguousarray(_np.broadcast_to(_np.asarray(L0_attn_bo), (P, D))), "gate_w": turned(L0_ffn_gate_w),
        "sh_gate": turned(L0_ffn_shared_gate), "sh_up": turned(L0_ffn_shared_up), "sh_down": turned(L0_ffn_shared_down),
        "r_gate": turned(L0_ffn_r_gate), "r_up": turned(L0_ffn_r_up), "r_down": turned(L0_ffn_r_down), "consts": constants(),
    }
    nc = _bacc.Bacc("TRN2", target_bir_lowering=False, num_devices=1)
    args = [nc.dram_tensor(f"in_{n}", a.shape, _mybir.dt.from_np(a.dtype), kind="ExternalInput").ap() for n, a in arrays.items()]
    args.append(nc.dram_tensor("out_0", tuple(L0_attn_x.shape), _mybir.dt.float32, kind="ExternalOutput").ap())
    macaron_kernel(nc, *args)
    r = _run(nc, [{f"in_{n}": a for n, a in arrays.items()}], core_ids=[0])
    return r.results[0]["out_0"]
```
